# Optimizing a Trainium2 kernel written in Bass

```python
import numpy as np
import jax
import jax.numpy as jnp

def _softmax(x, axis=-1):
    return jax.nn.softmax(x, axis=axis)

def _gelu(x):
    return jax.nn.gelu(x, approximate=True)

def _silu(x):
    return jax.nn.silu(x)

def _sigmoid(x):
    return jax.nn.sigmoid(x)

def _layernorm(x, axis=-1, eps=1e-05):
    m = jnp.mean(x, axis=axis, keepdims=True)
    v = jnp.var(x, axis=axis, keepdims=True)
    return (x - m) / jnp.sqrt(v + eps)

def _scatter_add(tgt, idx, src, axis=0):
    return tgt.at[idx].add(src)

def _segment_sum(src, seg, n):
    return jax.ops.segment_sum(src, seg, n)
kernel_name = 'mk_decoder_preln_d2_seqx_r4_c01aa3'

def setup_inputs(seed: int=0):
    np.random.seed(seed)
    _w = jnp.asarray

    def _rec_inputs():
        import jax
        import jax.numpy as jnp
        _rk = jax.random.key(seed)
        x = -0.0002928 + 1 * jax.random.normal(jax.random.fold_in(_rk, 1), (4, 1024, 256), jnp.float32)
        _lenS = 1024 - jax.random.randint(jax.random.fold_in(_rk, 7), (4,), 0, max(1, 1024 // 4) + 1, jnp.int32)
        _lenS2 = 77 - jax.random.randint(jax.random.fold_in(_rk, 8), (4,), 0, max(1, 77 // 4) + 1, jnp.int32)
        _ctx_1024P = jax.random.normal(jax.random.fold_in(_rk, 11), (4, 16, 256), jnp.float32)
        _ctx_1024c = jax.random.dirichlet(jax.random.fold_in(_rk, 511), 0.3 * jnp.ones((16,), jnp.float32), (4, 77))
        _ctx_1024t = jnp.einsum('bsk,bkd->bsd', _ctx_1024c, _ctx_1024P)
        _ctx_1024t = _ctx_1024t * jax.lax.rsqrt(jnp.mean(jnp.square(_ctx_1024t)) + 1e-12) * 0.953939
        ctx_1024 = -1.78809e-06 + 0.0312453 * (_ctx_1024t + 0.3 * jax.random.normal(jax.random.fold_in(_rk, 611), (4, 77, 256), jnp.float32))
        return (x, ctx_1024)
    x, ctx_1024 = _rec_inputs()

    def _L0_attn_setup():
        import jax, jax.numpy as jnp
        import numpy as np
        BATCH, SEQ, D_MODEL = (2, 256, 256)
        D_INNER = 2 * D_MODEL
        D_STATE = 16
        D_CONV = 4
        DT_RANK = D_MODEL // 16

        def _mamba_forward(x, W_in, conv_w, conv_b, W_xproj, W_dt, b_dt, A_log, D, W_out):
            xz = x @ W_in
            xc, z = jnp.split(xz, 2, axis=-1)
            xt = jnp.transpose(xc, (0, 2, 1))
            kern = conv_w[:, None, :]
            xt = jax.lax.conv_general_dilated(xt, kern, window_strides=(1,), padding=[(D_CONV - 1, 0)], dimension_numbers=('NCH', 'OIH', 'NCH'), feature_group_count=D_INNER)
            xc = jax.nn.silu(jnp.transpose(xt, (0, 2, 1)) + conv_b)
            proj = xc @ W_xproj
            dt_r = proj[..., :DT_RANK]
            Bm = proj[..., DT_RANK:DT_RANK + D_STATE]
            Cm = proj[..., DT_RANK + D_STATE:]
            dt = jax.nn.softplus(dt_r @ W_dt + b_dt)
            A = -jnp.exp(A_log)
            dA = jnp.exp(dt[..., None] * A)
            dBx = (dt * xc)[..., None] * Bm[:, :, None, :]

            def step(h, inp):
                dA_t, dBx_t, C_t = inp
                h = h * dA_t + dBx_t
                y = jnp.einsum('ben,bn->be', h, C_t)
                return (h, y)
            h0 = jnp.zeros((x.shape[0], D_INNER, D_STATE), dtype=xc.dtype)
            _, ys = jax.lax.scan(step, h0, (jnp.moveaxis(dA, 1, 0), jnp.moveaxis(dBx, 1, 0), jnp.moveaxis(Cm, 1, 0)))
            y = jnp.moveaxis(ys, 0, 1) + xc * D
            y = y * jax.nn.silu(z)
            return y @ W_out
        key = jax.random.key(seed)
        ks = jax.random.split(key, 8)
        g = lambda k, sh, sc: jax.random.normal(k, sh, dtype=jnp.float32) * sc
        x = g(ks[0], (BATCH, SEQ, D_MODEL), 1.0)
        W_in = g(ks[1], (D_MODEL, 2 * D_INNER), D_MODEL ** (-0.5))
        conv_w = g(ks[2], (D_INNER, D_CONV), 0.5)
        conv_b = g(ks[3], (D_INNER,), 0.1)
        W_xproj = g(ks[4], (D_INNER, DT_RANK + 2 * D_STATE), D_INNER ** (-0.5))
        W_dt = g(ks[5], (DT_RANK, D_INNER), DT_RANK ** (-0.5))
        b_dt = jnp.full((D_INNER,), float(np.log(np.expm1(0.01))), dtype=jnp.float32)
        A_log = jnp.log(jnp.broadcast_to(jnp.arange(1, D_STATE + 1, dtype=jnp.float32), (D_INNER, D_STATE)))
        D = jnp.ones((D_INNER,), dtype=jnp.float32)
        W_out = g(ks[6], (D_INNER, D_MODEL), D_INNER ** (-0.5))
        return dict(x=x, W_in=W_in, conv_w=conv_w, conv_b=conv_b, W_xproj=W_xproj, W_dt=W_dt, b_dt=b_dt, A_log=A_log, D=D, W_out=W_out)
    _L0_attn_all = _L0_attn_setup()
    _L0_attn_in = {k: v for k, v in _L0_attn_all.items() if k in ('W_in', 'conv_w', 'conv_b', 'W_xproj', 'W_dt', 'b_dt', 'A_log', 'D', 'W_out')}
    del _L0_attn_all

    def _L0_xattn_setup():
        import jax, jax.numpy as jnp
        import numpy as np
        E, TPE, H, F = (64, 64, 256, 256)
        key = jax.random.key(seed)
        k1, k2, k3, k4 = jax.random.split(key, 4)
        scale = 1.0 / np.sqrt(H)
        return {'x': jax.random.normal(k1, (E, TPE, H), dtype=jnp.float32), 'w1': jax.random.normal(k2, (E, F, H), dtype=jnp.float32) * scale, 'v1': jax.random.normal(k3, (E, F, H), dtype=jnp.float32) * scale, 'w2': jax.random.normal(k4, (E, F, H), dtype=jnp.float32) * scale}
    _L0_xattn_all = _L0_xattn_setup()
    _L0_xattn_in = {k: v for k, v in _L0_xattn_all.items() if k in ()}
    del _L0_xattn_all

    def _L0_ffn_setup():
        import jax, jax.numpy as jnp
        import numpy as np
        B, S, H, E = (4, 512, 256, 8)
        key = jax.random.key(seed)
        k1, k2, k3 = jax.random.split(key, 3)
        scale = 1.0 / np.sqrt(H)
        return {'x': jax.random.normal(k1, (B, S, H), dtype=jnp.float32), 'router_w': jax.random.normal(k2, (H, E), dtype=jnp.float32) * scale, 'router_b': jnp.zeros((E,), dtype=jnp.float32), 'expert_w': jax.random.normal(k3, (E, H, H), dtype=jnp.float32) * scale, 'expert_b': jnp.zeros((E, H), dtype=jnp.float32)}
    _L0_ffn_all = _L0_ffn_setup()
    _L0_ffn_in = {k: v for k, v in _L0_ffn_all.items() if k in ('router_w', 'router_b', 'expert_w', 'expert_b')}
    del _L0_ffn_all

    def _L1_attn_setup():
        import jax, jax.numpy as jnp
        import numpy as np
        NUM_HEADS = 16
        key = jax.random.key(seed)
        ks = jax.random.split(key, 5)
        N, L, E = (4, 256, 256)
        x = jax.random.normal(ks[0], (N, L, E), dtype=jnp.float32)
        sc = 1.0 / np.sqrt(E)
        wq = jax.random.normal(ks[1], (E, E), dtype=jnp.float32) * sc
        wk = jax.random.normal(ks[2], (E, E), dtype=jnp.float32) * sc
        wv = jax.random.normal(ks[3], (E, E), dtype=jnp.float32) * sc
        wo = jax.random.normal(ks[4], (E, E), dtype=jnp.float32) * sc
        return {'x': x, 'wq': wq, 'wk': wk, 'wv': wv, 'wo': wo}
    _L1_attn_all = _L1_attn_setup()
    _L1_attn_in = {k: v for k, v in _L1_attn_all.items() if k in ('wq', 'wk', 'wv', 'wo')}
    del _L1_attn_all

    def _L1_xattn_setup():
        import jax, jax.numpy as jnp
        import numpy as np
        DIM = 256
        NUM_HEADS = 16
        HEAD_DIM = DIM // NUM_HEADS
        key = jax.random.key(seed)
        ks = jax.random.split(key, 11)
        B, N, C = (2, 512, DIM)
        s = 1.0 / np.sqrt(C)
        inp = {'q': jax.random.normal(ks[0], (B, N, C), jnp.float32), 'k': jax.random.normal(ks[1], (B, N, C), jnp.float32), 'v': jax.random.normal(ks[2], (B, N, C), jnp.float32), 'Wq': jax.random.normal(ks[3], (C, C), jnp.float32) * s, 'bq': jnp.zeros((C,), jnp.float32), 'Wk': jax.random.normal(ks[4], (C, C), jnp.float32) * s, 'bk': jnp.zeros((C,), jnp.float32), 'Wv': jax.random.normal(ks[5], (C, C), jnp.float32) * s, 'bv': jnp.zeros((C,), jnp.float32), 'Wo': jax.random.normal(ks[6], (C, C), jnp.float32) * s, 'bo': jnp.zeros((C,), jnp.float32)}
        return inp
    _L1_xattn_all = _L1_xattn_setup()
    _L1_xattn_in = {k: v for k, v in _L1_xattn_all.items() if k in ('Wq', 'bq', 'Wk', 'bk', 'Wv', 'bv', 'Wo', 'bo')}
    del _L1_xattn_all

    def _L1_ffn_setup():
        import jax, jax.numpy as jnp
        import numpy as np
        NUM_EXPERTS = 8
        TOP_K = 2
        DIM = 256
        HIDDEN = 1024
        B, S = (4, 512)
        key = jax.random.key(seed)
        ks = jax.random.split(key, 6)
        scale = 0.02
        x = jax.random.normal(ks[0], (B, S, DIM), dtype=jnp.float32)
        wg = jax.random.normal(ks[1], (NUM_EXPERTS, DIM), dtype=jnp.float32) * scale
        bg = jnp.zeros((NUM_EXPERTS,), dtype=jnp.float32)
        Wgate = jax.random.normal(ks[2], (NUM_EXPERTS, HIDDEN, DIM), dtype=jnp.float32) * scale
        Wup = jax.random.normal(ks[3], (NUM_EXPERTS, HIDDEN, DIM), dtype=jnp.float32) * scale
        Wdown = jax.random.normal(ks[4], (NUM_EXPERTS, DIM, HIDDEN), dtype=jnp.float32) * scale
        return {'x': x, 'wg': wg, 'bg': bg, 'Wgate': Wgate, 'Wup': Wup, 'Wdown': Wdown}
    _L1_ffn_all = _L1_ffn_setup()
    _L1_ffn_in = {k: v for k, v in _L1_ffn_all.items() if k in ('wg', 'bg', 'Wgate', 'Wup', 'Wdown')}
    del _L1_ffn_all
    return {'x': x, 'ctx_1024': ctx_1024, 'L0_attn_W_in': _L0_attn_in['W_in'], 'L0_attn_conv_w': _L0_attn_in['conv_w'], 'L0_attn_conv_b': _L0_attn_in['conv_b'], 'L0_attn_W_xproj': _L0_attn_in['W_xproj'], 'L0_attn_W_dt': _L0_attn_in['W_dt'], 'L0_attn_b_dt': _L0_attn_in['b_dt'], 'L0_attn_A_log': _L0_attn_in['A_log'], 'L0_attn_D': _L0_attn_in['D'], 'L0_attn_W_out': _L0_attn_in['W_out'], 'L0_ffn_router_w': _L0_ffn_in['router_w'], 'L0_ffn_router_b': _L0_ffn_in['router_b'], 'L0_ffn_expert_w': _L0_ffn_in['expert_w'], 'L0_ffn_expert_b': _L0_ffn_in['expert_b'], 'L1_attn_wq': _L1_attn_in['wq'], 'L1_attn_wk': _L1_attn_in['wk'], 'L1_attn_wv': _L1_attn_in['wv'], 'L1_attn_wo': _L1_attn_in['wo'], 'L1_xattn_Wq': _L1_xattn_in['Wq'], 'L1_xattn_bq': _L1_xattn_in['bq'], 'L1_xattn_Wk': _L1_xattn_in['Wk'], 'L1_xattn_bk': _L1_xattn_in['bk'], 'L1_xattn_Wv': _L1_xattn_in['Wv'], 'L1_xattn_bv': _L1_xattn_in['bv'], 'L1_xattn_Wo': _L1_xattn_in['Wo'], 'L1_xattn_bo': _L1_xattn_in['bo'], 'L1_ffn_wg': _L1_ffn_in['wg'], 'L1_ffn_bg': _L1_ffn_in['bg'], 'L1_ffn_Wgate': _L1_ffn_in['Wgate'], 'L1_ffn_Wup': _L1_ffn_in['Wup'], 'L1_ffn_Wdown': _L1_ffn_in['Wdown']}

def reference(x, ctx_1024, L0_attn_W_in, L0_attn_conv_w, L0_attn_conv_b, L0_attn_W_xproj, L0_attn_W_dt, L0_attn_b_dt, L0_attn_A_log, L0_attn_D, L0_attn_W_out, L0_ffn_router_w, L0_ffn_router_b, L0_ffn_expert_w, L0_ffn_expert_b, L1_attn_wq, L1_attn_wk, L1_attn_wv, L1_attn_wo, L1_xattn_Wq, L1_xattn_bq, L1_xattn_Wk, L1_xattn_bk, L1_xattn_Wv, L1_xattn_bv, L1_xattn_Wo, L1_xattn_bo, L1_ffn_wg, L1_ffn_bg, L1_ffn_Wgate, L1_ffn_Wup, L1_ffn_Wdown):
    import jax
    import jax.numpy as jnp

    def _L0_attn_ref(x, W_in, conv_w, conv_b, W_xproj, W_dt, b_dt, A_log, D, W_out):
        import jax, jax.numpy as jnp
        import numpy as np
        BATCH, SEQ, D_MODEL = (2, 256, 256)
        D_INNER = 2 * D_MODEL
        D_STATE = 16
        D_CONV = 4
        DT_RANK = D_MODEL // 16

        def _mamba_forward(x, W_in, conv_w, conv_b, W_xproj, W_dt, b_dt, A_log, D, W_out):
            xz = x @ W_in
            xc, z = jnp.split(xz, 2, axis=-1)
            xt = jnp.transpose(xc, (0, 2, 1))
            kern = conv_w[:, None, :]
            xt = jax.lax.conv_general_dilated(xt, kern, window_strides=(1,), padding=[(D_CONV - 1, 0)], dimension_numbers=('NCH', 'OIH', 'NCH'), feature_group_count=D_INNER)
            xc = jax.nn.silu(jnp.transpose(xt, (0, 2, 1)) + conv_b)
            proj = xc @ W_xproj
            dt_r = proj[..., :DT_RANK]
            Bm = proj[..., DT_RANK:DT_RANK + D_STATE]
            Cm = proj[..., DT_RANK + D_STATE:]
            dt = jax.nn.softplus(dt_r @ W_dt + b_dt)
            A = -jnp.exp(A_log)
            dA = jnp.exp(dt[..., None] * A)
            dBx = (dt * xc)[..., None] * Bm[:, :, None, :]

            def step(h, inp):
                dA_t, dBx_t, C_t = inp
                h = h * dA_t + dBx_t
                y = jnp.einsum('ben,bn->be', h, C_t)
                return (h, y)
            h0 = jnp.zeros((x.shape[0], D_INNER, D_STATE), dtype=xc.dtype)
            _, ys = jax.lax.scan(step, h0, (jnp.moveaxis(dA, 1, 0), jnp.moveaxis(dBx, 1, 0), jnp.moveaxis(Cm, 1, 0)))
            y = jnp.moveaxis(ys, 0, 1) + xc * D
            y = y * jax.nn.silu(z)
            return y @ W_out
        return _mamba_forward(x, W_in, conv_w, conv_b, W_xproj, W_dt, b_dt, A_log, D, W_out)

    def _L0_xattn_ref(x, w1, v1, w2):
        import jax, jax.numpy as jnp
        import numpy as np
        E, TPE, H, F = (64, 64, 256, 256)
        h1 = jnp.einsum('eth,efh->etf', x, w1)
        h2 = jnp.einsum('eth,efh->etf', x, v1)
        g = jax.nn.gelu(h1, approximate=False) * h2
        return jnp.einsum('etf,efh->eth', g, w2)

    def _L0_ffn_ref(x, router_w, router_b, expert_w, expert_b):
        import jax, jax.numpy as jnp
        import numpy as np
        B, S, H, E = (4, 512, 256, 8)
        b, s, h = x.shape
        hs = x.reshape(-1, h)
        logits = hs @ router_w + router_b
        probs = jax.nn.softmax(logits, axis=-1)
        idx = jnp.argmax(probs, axis=-1)
        gate = jnp.take_along_axis(probs, idx[:, None], axis=-1)
        expert_out = jnp.einsum('th,ehd->ted', hs, expert_w) + expert_b
        dispatch = jax.nn.one_hot(idx, expert_w.shape[0], dtype=hs.dtype) * gate
        out = jnp.einsum('te,ted->td', dispatch, expert_out)
        return out.reshape(b, s, h)

    def _L1_attn_ref(x, wq, wk, wv, wo):
        import jax, jax.numpy as jnp
        import numpy as np
        NUM_HEADS = 16
        N, L, E = x.shape
        H = NUM_HEADS
        d = E // H
        q = (x @ wq.T).reshape(N, H, L, d)
        k = (x @ wk.T).reshape(N, H, L, d)
        v = (x @ wv.T).reshape(N, H, L, d)
        scores = jnp.einsum('nhld,nhmd->nhlm', q, k) / jnp.sqrt(jnp.float32(d))
        causal = jnp.tril(jnp.ones((L, L), dtype=bool))
        scores = jnp.where(causal, scores, jnp.float32(-jnp.inf))
        attn = jax.nn.softmax(scores, axis=-1)
        wei = jnp.einsum('nhlm,nhmd->nhld', attn, v).reshape(N, L, H * d)
        return wei @ wo.T

    def _L1_xattn_ref(q, k, v, Wq, bq, Wk, bk, Wv, bv, Wo, bo):
        import jax, jax.numpy as jnp
        import numpy as np
        DIM = 256
        NUM_HEADS = 16
        HEAD_DIM = DIM // NUM_HEADS
        B, Nq, C = q.shape
        Nkv = k.shape[1]
        H, D = (NUM_HEADS, HEAD_DIM)
        qh = (q @ Wq.T + bq).reshape(B, Nq, H, D).transpose(0, 2, 1, 3)
        kh = (k @ Wk.T + bk).reshape(B, Nkv, H, D).transpose(0, 2, 1, 3)
        vh = (v @ Wv.T + bv).reshape(B, Nkv, H, D).transpose(0, 2, 1, 3)
        scale = D ** (-0.5)
        attn = jax.nn.softmax(jnp.einsum('bhqd,bhkd->bhqk', qh, kh) * scale, axis=-1)
        out = jnp.einsum('bhqk,bhkd->bhqd', attn, vh)
        out = out.transpose(0, 2, 1, 3).reshape(B, Nq, C)
        return out @ Wo.T + bo

    def _L1_ffn_ref(x, wg, bg, Wgate, Wup, Wdown):
        import jax, jax.numpy as jnp
        import numpy as np
        NUM_EXPERTS = 8
        TOP_K = 2
        DIM = 256
        HIDDEN = 1024
        B, S = (4, 512)
        b, s, d = x.shape
        xf = x.reshape(-1, d)
        T = xf.shape[0]
        logits = xf @ wg.T + bg
        vals, idx = jax.lax.top_k(logits, TOP_K)
        masked = jnp.full_like(logits, -jnp.inf)
        rows = jnp.arange(T)[:, None]
        masked = masked.at[rows, idx].set(vals)
        weights = jax.nn.softmax(masked, axis=-1)
        out = jnp.zeros_like(xf)
        for e in range(NUM_EXPERTS):
            g = xf @ Wgate[e].T
            u = xf @ Wup[e].T
            h = g * jax.nn.sigmoid(g) * u
            out = out + h @ Wdown[e].T * weights[:, e:e + 1]
        return out.reshape(b, s, d)
    x = x + _L0_attn_ref(_layernorm(x, axis=-1), L0_attn_W_in, L0_attn_conv_w, L0_attn_conv_b, L0_attn_W_xproj, L0_attn_W_dt, L0_attn_b_dt, L0_attn_A_log, L0_attn_D, L0_attn_W_out)
    x = x + _L0_xattn_ref(_layernorm(x, axis=-1), ctx_1024, ctx_1024, ctx_1024)
    x = x + _L0_ffn_ref(_layernorm(x, axis=-1), L0_ffn_router_w, L0_ffn_router_b, L0_ffn_expert_w, L0_ffn_expert_b)
    x = x + _L1_attn_ref(_layernorm(x, axis=-1), L1_attn_wq, L1_attn_wk, L1_attn_wv, L1_attn_wo)
    x = x + _L1_xattn_ref(_layernorm(x, axis=-1), ctx_1024, ctx_1024, L1_xattn_Wq, L1_xattn_bq, L1_xattn_Wk, L1_xattn_bk, L1_xattn_Wv, L1_xattn_bv, L1_xattn_Wo, L1_xattn_bo)
    x = x + _L1_ffn_ref(_layernorm(x, axis=-1), L1_ffn_wg, L1_ffn_bg, L1_ffn_Wgate, L1_ffn_Wup, L1_ffn_Wdown)
    return x

_drawn_inputs = setup_inputs


def setup_inputs(seed=0):
    import zlib

    import numpy as np

    out = dict(_drawn_inputs(seed))
    spreads = {'L0_attn_b_dt': (-4.600165843963623, 0.2),
     'L0_attn_D': (1.0, 0.2),
     'L0_ffn_router_b': (0.0, 0.1),
     'L0_ffn_expert_b': (0.0, 0.1),
     'L1_xattn_bq': (0.0, 2.0),
     'L1_xattn_bk': (0.0, 2.0),
     'L1_xattn_bv': (0.0, 0.1),
     'L1_xattn_bo': (0.0, 0.1),
     'L1_ffn_bg': (0.0, 0.714)}
    factors = {'L1_xattn_Wq': 8.0,
     'L1_xattn_Wk': 8.0,
     'L1_xattn_Wv': 4.013,
     'L1_ffn_wg': 3.274,
     'L1_ffn_Wgate': 2.822,
     'L1_ffn_Wup': 2.794,
     'L1_ffn_Wdown': 2.793}
    for name, (base, spread) in spreads.items():
        noise = np.random.default_rng([zlib.crc32(name.encode()), seed]).standard_normal(out[name].shape)
        drawn = base * np.exp(spread * noise) if base else spread * noise
        out[name] = jnp.asarray(drawn.astype(out[name].dtype))
    for name, factor in factors.items():
        out[name] = (out[name] * factor).astype(out[name].dtype)
    return out
```

```python
from contextlib import ExitStack

import concourse.bass as bass
from concourse import mybir
import numpy as np

F32 = mybir.dt.float32
F32R = mybir.dt.float32r
BF16 = mybir.dt.bfloat16
I32 = mybir.dt.int32
U32 = mybir.dt.uint32
ALU = mybir.AluOpType
ACT = mybir.ActivationFunctionType
AX = mybir.AxisListType

P = 128
NB, SEQ, D = 4, 1024, 256
TOK = NB * SEQ
NT = TOK // P
KD = D // P
CH = 512
TC = CH // P
NCH = TOK // CH
CPB = SEQ // CH
CTX = 77
EPS = 1e-5


def after(eng, sem, i, per, k=None):
    eng.wait_ge(sem, i * per + (per if k is None else k))


def free(eng, sem, i, per, back=2):
    if not isinstance(i, int) or i >= back:
        eng.wait_ge(sem, (i - back + 1) * per)


def n_positive(n):
    return not isinstance(n, int) or n > 0


def chunks(eng, n, mid, front, tail):
    front(0, 0)
    mid(0, 0)
    front(1, 1)
    tail(0, 0)
    with eng.Fori(1, n // 2) as j:
        mid(2 * j - 1, 1)
        front(2 * j, 0)
        tail(2 * j - 1, 1)
        mid(2 * j, 0)
        front(2 * j + 1, 1)
        tail(2 * j, 0)
    mid(n - 1, 1)
    tail(n - 1, 1)


def nothing(i, p):
    pass


class Kernel:

    def __init__(self, nc, ctx, io):
        self.nc, self.io, self.in_use = nc, io, []
        self.resid = self.sb(ctx, "resid", [P, NT, D])
        self.ident = self.sb(ctx, "ident", [P, P])
        self.iota8 = self.sb(ctx, "iota8", [P, 8])
        self.held_vector = ctx.enter_context(nc.semaphore("held_vector"))
        self.held_pool = ctx.enter_context(nc.semaphore("held_pool"))
        self.held_tensor = ctx.enter_context(nc.semaphore("held_tensor"))
        self.minus_half = self.sb(ctx, "minus_half", [P, TC])

    def sb(self, ctx, name, shape, dt=F32):
        return ctx.enter_context(self.nc.sbuf_tensor(name, shape, dt))

    def ps(self, ctx, name, shape, dt=F32):
        return ctx.enter_context(self.nc.psum_tensor(name, shape, dt))

    def sem(self, ctx, name):
        self.in_use.append(self.nc.alloc_semaphore(name=name))
        return self.in_use[-1]

    def clear(self):
        self.nc.clear_and_free_semaphores(self.in_use)
        self.nc.all_engine_barrier()
        self.in_use = []


class LayerNormFront:

    def __init__(self, K, ctx, tag, keep_rows=False):
        nc = K.nc
        self.K, self.nc = K, nc
        sb = lambda n, s, d=F32: K.sb(ctx, f"{tag}_{n}", s, d)
        self.stats = [sb(f"stats{p}", [P, TC, 6]) for p in range(2)]
        self.mv = [sb(f"mv{p}", [P, TC, 2]) for p in range(2)]
        self.veps = [sb(f"veps{p}", [P, TC]) for p in range(2)]
        self.rstd = [sb(f"rstd{p}", [P, TC]) for p in range(2)]
        self.xn = [sb(f"xn{p}", [P, TC, D]) for p in range(2)]
        self.xnT = [sb(f"xnT{p}", [P, KD, CH]) for p in range(2)]
        self.pT = [K.ps(ctx, f"{tag}_pT{k}", [P, CH]) for k in range(KD)]
        sem = lambda n: K.sem(ctx, f"{tag}_{n}")
        self.s_stats, self.s_mv, self.s_veps = sem("stats"), sem("mv"), sem("veps")
        self.s_rstd, self.s_xn, self.s_pT, self.s_xnT = sem("rstd"), sem("xn"), sem("pT"), sem("xnT")

    def vector(self, eng, i, p):
        nc, R = self.nc, self.K.resid
        for t in range(TC):
            nc.vector.bn_stats(self.stats[p][:, t, :], R[:, bass.ds(i * TC + t, 1), :].rearrange("p a d -> p (a d)")).then_inc(self.s_stats, 1)
        after(eng, self.s_stats, i, TC)
        eng.sem_inc(self.K.held_vector)
        for t in range(TC):
            nc.vector.bn_aggr(self.mv[p][:, t, :], self.stats[p][:, t, :]).then_inc(self.s_mv, 1)
        after(eng, self.s_mv, i, TC)
        nc.vector.tensor_scalar(self.veps[p][:, :], self.mv[p][:, :, 1], EPS, None, ALU.add).then_inc(self.s_veps, 1)
        after(eng, self.s_rstd, i, 1)
        free(eng, self.s_pT, i, KD)
        for t in range(TC):
            nc.vector.tensor_scalar(self.xn[p][:, t, :], R[:, bass.ds(i * TC + t, 1), :].rearrange("p a d -> p (a d)"),
                                    self.mv[p][:, t, 0:1], self.rstd[p][:, t:t + 1],
                                    ALU.subtract, ALU.mult).then_inc(self.s_xn, 1)

    def gpsimd(self, eng, i, p):
        after(eng, self.s_veps, i, 1)
        self.nc.gpsimd.tensor_tensor(self.rstd[p][:, :], self.veps[p][:, :], self.K.minus_half[:, :],
                                     ALU.pow).then_inc(self.s_rstd, 1)

    def tensor(self, eng, i, p):
        after(eng, self.s_xn, i, TC)
        for k in range(KD):
            free(eng, self.s_xnT, i, KD, back=1)
            for t in range(TC):
                last = self.nc.tensor.transpose(self.pT[k][:, t * P:(t + 1) * P],
                                                self.xn[p][:, t, k * P:(k + 1) * P], self.K.ident[:, :])
            last.then_inc(self.s_pT, 1)

    def scalar(self, eng, i, p, s_used, per_used):
        free(eng, s_used, i, per_used)
        for k in range(KD):
            after(eng, self.s_pT, i, KD, k + 1)
            self.nc.scalar.copy(self.xnT[p][:, k, :], self.pT[k][:, :]).then_inc(self.s_xnT, 1)


def rows(R, i):
    return R[:, bass.ds(i * TC, TC), :]


def load_and_constants(K):
    nc, io = K.nc, K.io
    with ExitStack() as c:
        s_x, s_c = K.sem(c, "ld_x"), K.sem(c, "ld_c")
        block = c.enter_context(nc.Block())

        @block.sync
        def _(eng):
            eng.dma_start(K.resid[:, :, :], io["x"].rearrange("b (t p) d -> p (b t) d", p=P)).then_inc(s_x, 16)
            eng.wait_ge(s_x, 16)

        @block.vector
        def _(eng):
            nc.vector.memset(K.minus_half[:, :], -0.5)
            nc.vector.memset(K.ident[:, :], 0.0).then_inc(s_c, 1)

        @block.gpsimd
        def _(eng):
            eng.wait_ge(s_c, 1)
            nc.gpsimd.affine_select(out=K.ident[:, :], in_=K.ident[:, :], compare_op=ALU.not_equal, fill=1.0,
                                    base=0, pattern=[[-1, P]], channel_multiplier=1)
            nc.gpsimd.iota(K.iota8[:, :], pattern=[[1, 8]], base=0, channel_multiplier=0,
                           allow_small_or_imprecise_dtypes=True)


def store(K):
    nc, io = K.nc, K.io
    with ExitStack() as c:
        s_out = K.sem(c, "st_out")
        block = c.enter_context(nc.Block())

        @block.sync
        def _(eng):
            eng.dma_start(io["out"].rearrange("b (t p) d -> p (b t) d", p=P), K.resid[:, :, :]).then_inc(s_out, 16)
            eng.wait_ge(s_out, 16)


def run_for(name, eng, ops):
    for op in ops:
        for who, fn in op:
            if who == name:
                fn(eng)


def interleave(main, other):
    out, done = [], 0
    for n, op in enumerate(main):
        out.append(op)
        upto = (n + 1) * len(other) // len(main)
        out += other[done:upto]
        done = upto
    return out


def mamba(K):
    nc, io, R = K.nc, K.io, K.resid
    DI = io["mb_D"].shape[0]
    ME = DI // P
    NST = io["mb_A_log"].shape[1]
    RANK = io["mb_wdt"].shape[0]
    NPROJ = RANK + 2 * NST
    TAPS = io["mb_conv_w"].shape[1]
    GN = 4
    NGR = NST // GN
    ITEMS = NGR * ME
    LO = 64
    with ExitStack() as c:
        ln = LayerNormFront(K, c, "ml")
        sb = lambda n, s, d=F32: K.sb(c, f"mb_{n}", s, d)
        sem = lambda n: K.sem(c, f"mb_s_{n}")
        w_in = sb("w_in_sb", [P, KD, 2 * DI])
        w_x = sb("w_x_sb", [P, ME, NPROJ])
        w_dt = sb("w_dt_sb", [RANK, DI])
        w_out = sb("w_out_sb", [P, ME, D])
        conv_w, conv_b = sb("conv_w_sb", [P, ME, TAPS]), sb("conv_b_sb", [P, ME])
        b_dt, skip = sb("b_dt_sb", [P, ME]), sb("skip", [P, ME])
        a_neg = sb("a_neg", [P, ME, NST])
        u = sb("u", [P, ME, TAPS - 1 + CH])
        acc = [sb(f"acc{q}", [P, CH]) for q in range(2)]
        xc = sb("xc", [P, ME, CH])
        proj = sb("proj", [NPROJ, CH])
        proj_hl = sb("proj_hl", [LO + NPROJ, CH], F32R)
        pick = sb("pick", [LO + NPROJ, 2 * NST])
        spread = sb("spread", [LO + NPROJ, 2 * NST], F32R)
        e1 = acc
        l1 = [sb(f"l1{q}", [P, CH]) for q in range(2)]
        rest = sb("rest", [P, CH])
        dt = sb("dt", [P, ME, CH])
        dtx = sb("dtx", [P, ME, CH])
        b_rep = [sb(f"b_rep{q}", [P, GN, CH]) for q in range(2)]
        c_rep = [sb(f"c_rep{q}", [P, GN, CH]) for q in range(2)]
        decay = [sb(f"decay{q}", [P, GN, 1 + CH]) for q in range(2)]
        drive = [sb(f"drive{q}", [P, GN, 1 + CH]) for q in range(2)]
        hc = [sb(f"hc{q}", [P, GN, CH]) for q in range(2)]
        carried = sb("carried", [P, ME, NST])
        sz = [sb(f"sz{q}", [P, CH]) for q in range(2)]
        yz = sb("yz", [P, ME, CH])
        pA = [K.ps(c, f"mb_pA{q}", [P, CH]) for q in range(2)]
        pY = [K.ps(c, f"mb_pY{m}", [P, CH]) for m in range(ME)]
        (s_in, s_c, s_a, s_sel, s_A, s_Ac, s_car, s_cv, s_xc, s_phl, s_sp, s_dv, s_dt, s_dtx, s_dA, s_dB, s_scan, s_keep, s_hc, s_y,
         s_yd, s_yz, s_o, s_res) = (sem(n) for n in (
             "in", "c", "a", "sel", "A", "Ac", "car", "cv", "xc", "phl", "sp", "dv", "dt", "dtx", "dA", "dB", "scan", "keep",
             "hc", "y", "yd", "yz", "o", "res"))
        U_XC, U_PROJ, U_DT, U_BC = 0, ME, ME + 1, 2 * ME + 1
        U_Z = U_BC + 2 * NST
        USES = U_Z + ME
        later = lambda i: not isinstance(i, int) or i > 0

        def use(i, p, n, matmuls, read):
            out = pA[(p * USES + n) % 2]

            def pe(eng):
                if n >= 2 or later(i):
                    eng.wait_ge(s_Ac, i * USES + n - 1)
                matmuls(eng, out).then_inc(s_A, 1)

            def act(eng):
                after(eng, s_A, i, USES, n + 1)
                read(eng, out).then_inc(s_Ac, 1)
            return [("tensor", pe), ("scalar", act)]

        def front(i, p):
            return [[("vector", lambda eng: ln.vector(eng, i, p)), ("gpsimd", lambda eng: ln.gpsimd(eng, i, p)),
                     ("tensor", lambda eng: ln.tensor(eng, i, p)), ("scalar", lambda eng: ln.scalar(eng, i, p, s_yz, ME))]]

        def in_projection(i, p, n, col, read):
            def matmuls(eng, out):
                if n == U_XC:
                    after(eng, ln.s_xnT, i, KD)
                for k in range(KD):
                    last = nc.tensor.matmul(out[:, :], w_in[:, k, col:col + P], ln.xnT[p][:, k, :],
                                            start=(k == 0), stop=(k == KD - 1))
                return last
            return use(i, p, n, matmuls, read)

        def prepare(i, p):
            ops = []

            def carry(eng):
                if later(i):
                    eng.wait_ge(s_cv, i * ME * TAPS)
                    eng.sem_inc(K.held_pool)
                if p == 0:
                    ins = nc.gpsimd.memset(u[:, :, 0:TAPS - 1], 0.0)
                else:
                    ins = nc.gpsimd.tensor_copy(u[:, :, 0:TAPS - 1], u[:, :, CH:CH + TAPS - 1])
                ins.then_inc(s_car, 1)
            ops.append([("gpsimd", carry)])
            for m in range(ME):
                def read(eng, out, m=m):
                    if m == 0:
                        after(eng, s_car, i, 1)
                    return nc.scalar.copy(u[:, m, TAPS - 1:], out[:, :])
                ops.append(in_projection(i, p, U_XC + m, m * P, read))
            for m in range(ME):
                def conv(eng, m=m):
                    after(eng, s_car, i, 1)
                    after(eng, s_Ac, i, USES, U_XC + m + 1)
                    if m >= 2 or later(i):
                        eng.wait_ge(s_xc, i * ME + m - 1)
                    a = acc[m % 2]
                    nc.vector.tensor_scalar(a[:, :], u[:, m, 0:CH], conv_w[:, m, 0:1], None, ALU.mult).then_inc(s_cv, 1)
                    for j in range(1, TAPS):
                        after(eng, s_cv, i, ME * TAPS, m * TAPS + j)
                        nc.vector.scalar_tensor_tensor(a[:, :], u[:, m, j:j + CH], conv_w[:, m, j:j + 1], a[:, :],
                                                       ALU.mult, ALU.add).then_inc(s_cv, 1)

                def silu(eng, m=m):
                    after(eng, s_cv, i, ME * TAPS, (m + 1) * TAPS)
                    if m == 0 and later(i):
                        eng.wait_ge(s_yz, i * ME)
                    nc.scalar.activation(xc[:, m, :], acc[m % 2][:, :], ACT.Silu, bias=conv_b[:, m:m + 1]).then_inc(s_xc, 1)
                ops.append([("vector", conv), ("scalar", silu)])

            def project(eng, out):
                after(eng, s_xc, i, ME)
                for m in range(ME):
                    last = nc.tensor.matmul(out[0:NPROJ, :], w_x[:, m, :], xc[:, m, :], start=(m == 0), stop=(m == ME - 1))
                return last
            ops.append(use(i, p, U_PROJ, project, lambda eng, out: nc.scalar.copy(proj[:, :], out[0:NPROJ, :])))

            def parts(eng):
                after(eng, s_Ac, i, USES, U_PROJ + 1)
                nc.vector.tensor_copy(proj_hl[0:NPROJ, :], proj[:, :]).then_inc(s_phl, 1)
                after(eng, s_phl, i, 2, 1)
                nc.vector.tensor_tensor(proj_hl[LO:LO + NPROJ, :], proj[:, :], proj_hl[0:NPROJ, :].bitcast(F32),
                                        ALU.subtract).then_inc(s_phl, 1)
            ops.append([("vector", parts)])

            for m in range(ME):
                def matmuls(eng, out, m=m):
                    if m == 0:
                        after(eng, s_Ac, i, USES, U_PROJ + 1)
                    return nc.tensor.matmul(out[:, :], w_dt[:, m * P:(m + 1) * P], proj[0:RANK, :], start=True, stop=True)

                def read(eng, out, m=m):
                    if m >= 2 or later(i):
                        eng.wait_ge(s_dt, i * ME + m - 1)
                    nc.scalar.activation(e1[m % 2][:, :], out[:, :], ACT.Abs, bias=b_dt[:, m:m + 1]).then_inc(s_sp, 1)
                    if m == 0 and later(i):
                        eng.wait_ge(s_scan, i * ITEMS)
                        eng.wait_ge(s_dtx, i * ME)
                    return nc.scalar.activation(dt[:, m, :], out[:, :], ACT.Relu, bias=b_dt[:, m:m + 1])
                op = use(i, p, U_DT + m, matmuls, read)

                def act(eng, m=m):
                    after(eng, s_sp, i, 3 * ME, 3 * m + 1)
                    nc.scalar.activation(e1[m % 2][:, :], e1[m % 2][:, :], ACT.Exp, scale=-1.0).then_inc(s_sp, 1)
                    after(eng, s_sp, i, 3 * ME, 3 * m + 2)
                    nc.scalar.activation(l1[m % 2][:, :], e1[m % 2][:, :], ACT.Ln, bias=1.0).then_inc(s_sp, 1)

                def dve(eng, m=m):
                    ch = Chain(eng, s_dv, i, 3 * ME)
                    ch.n = 3 * m
                    after(eng, s_sp, i, 3 * ME, 3 * m + 2)
                    ch.do(nc.vector.tensor_scalar(rest[:, :], e1[m % 2][:, :], 1.0, 1.0, ALU.add, ALU.subtract))
                    ch.do(nc.vector.tensor_tensor(rest[:, :], e1[m % 2][:, :], rest[:, :], ALU.subtract))
                    after(eng, s_sp, i, 3 * ME, 3 * m + 3)
                    ch.do(nc.vector.tensor_tensor(rest[:, :], l1[m % 2][:, :], rest[:, :], ALU.add))
                    nc.vector.tensor_tensor(dt[:, m, :], dt[:, m, :], rest[:, :], ALU.add).then_inc(s_dt, 1)
                    after(eng, s_dt, i, ME, m + 1)
                    if m == 0 and later(i):
                        eng.wait_ge(s_dB, i * 2 * ITEMS)
                    nc.vector.tensor_tensor(dtx[:, m, :], dt[:, m, :], xc[:, m, :], ALU.mult).then_inc(s_dtx, 1)
                ops.append(op + [("scalar", act), ("vector", dve)])
            return ops

        def broadcast(i, p, g):
            ops = []
            for half, rep in ((0, b_rep), (1, c_rep)):
                for n in range(GN):
                    row = half * NST + g * GN + n

                    def matmuls(eng, out, row=row):
                        if g == 0 and row == 0:
                            after(eng, s_phl, i, 2)
                        return nc.tensor.matmul(out[:, :], spread[:, row:row + 1].to_broadcast([LO + NPROJ, P]), proj_hl[:, :], start=True, stop=True)

                    def read(eng, out, rep=rep, n=n, half=half):
                        if n == 0 and half == 0 and (g >= 2 or later(i)):
                            eng.wait_ge(s_hc, i * ITEMS + ME * (g - 1))
                        return nc.scalar.copy(rep[g % 2][:, n, :], out[:, :])
                    ops.append(use(i, p, U_BC + g * 2 * GN + half * GN + n, matmuls, read))
            return ops

        def item(i, p, g, m):
            s = g * ME + m
            q = s % 2

            def act(eng):
                if s >= 2 or later(i):
                    eng.wait_ge(s_scan, i * ITEMS + s - 1)
                after(eng, s_dt, i, ME, m + 1)
                for n in range(GN):
                    last = nc.scalar.activation(decay[q][:, n, 1:], dt[:, m, :], ACT.Exp,
                                                scale=a_neg[:, m, g * GN + n:g * GN + n + 1])
                last.then_inc(s_dA, 1)

            def pool(eng):
                if s >= 2 or later(i):
                    eng.wait_ge(s_hc, i * ITEMS + s - 1)
                after(eng, s_dtx, i, ME, m + 1)
                after(eng, s_Ac, i, USES, U_BC + g * 2 * GN + GN)
                nc.gpsimd.tensor_tensor(drive[q][:, :, 1:], dtx[:, m, :].unsqueeze(1).to_broadcast([P, GN, CH]),
                                        b_rep[g % 2][:, :, :], ALU.mult).then_inc(s_dB, 1)
                if p == 0:
                    ins = nc.gpsimd.memset(drive[q][:, :, 0], 0.0)
                else:
                    ins = nc.gpsimd.tensor_copy(drive[q][:, :, 0], carried[:, m, g * GN:(g + 1) * GN])
                ins.then_inc(s_dB, 1)

            def dve(eng):
                after(eng, s_dA, i, ITEMS, s + 1)
                after(eng, s_dB, i, 2 * ITEMS, 2 * s + 2)
                long = lambda T: T[q][:, :, :].rearrange("p n t -> p (n t)")
                nc.vector.tensor_tensor_scan(long(drive), long(decay), long(drive), 0.0, ALU.mult, ALU.add).then_inc(s_scan, 1)
                after(eng, s_scan, i, ITEMS, s + 1)
                if p == 0:
                    nc.vector.tensor_copy(carried[:, m, g * GN:(g + 1) * GN], drive[q][:, :, CH]).then_inc(s_keep, 1)
                after(eng, s_Ac, i, USES, U_BC + (g + 1) * 2 * GN)
                if s >= 2 or later(i):
                    eng.wait_ge(s_y, i * ITEMS + s - 1)
                nc.vector.tensor_tensor(hc[q][:, :, :], drive[q][:, :, 1:], c_rep[g % 2][:, :, :], ALU.mult).then_inc(s_hc, 1)

            def pe(eng):
                if g == 0 and m == 0 and later(i):
                    eng.wait_ge(s_res, i * TC)
                after(eng, s_hc, i, ITEMS, s + 1)
                for n in range(GN):
                    last = nc.tensor.matmul(pY[m][:, :], K.ident[:, :], hc[q][:, n, :], start=(g == 0 and n == 0),
                                            stop=(g == NGR - 1 and n == GN - 1))
                last.then_inc(s_y, 1)
            return [("scalar", act), ("gpsimd", pool), ("vector", dve), ("tensor", pe)]

        def finish(i, p):
            ops = []
            for m in range(ME):
                def read(eng, out, m=m):
                    if m >= 2 or later(i):
                        eng.wait_ge(s_yz, i * ME + m - 1)
                    return nc.scalar.activation(sz[m % 2][:, :], out[:, :], ACT.Silu)

                def dve(eng, m=m):
                    after(eng, s_y, i, ITEMS, ITEMS - ME + m + 1)
                    if m == 0 and later(i):
                        eng.wait_ge(s_o, i * TC)
                    nc.vector.scalar_tensor_tensor(yz[:, m, :], xc[:, m, :], skip[:, m:m + 1], pY[m][:, :],
                                                   ALU.mult, ALU.add).then_inc(s_yd, 1)
                    after(eng, s_yd, i, ME, m + 1)
                    after(eng, s_Ac, i, USES, U_Z + m + 1)
                    nc.vector.tensor_tensor(yz[:, m, :], yz[:, m, :], sz[m % 2][:, :], ALU.mult).then_inc(s_yz, 1)
                ops.append(in_projection(i, p, U_Z + m, DI + m * P, read) + [("vector", dve)])
            for t in range(TC):
                def pe(eng, t=t):
                    after(eng, s_yz, i, ME)
                    for m in range(ME):
                        last = nc.tensor.matmul(pY[t][:, 0:D], yz[:, m, t * P:(t + 1) * P], w_out[:, m, :],
                                                start=(m == 0), stop=(m == ME - 1))
                    last.then_inc(s_o, 1)

                def dve(eng, t=t):
                    after(eng, s_o, i, TC, t + 1)
                    row = R[:, bass.ds(i * TC + t, 1), :].rearrange("p a d -> p (a d)")
                    nc.vector.tensor_tensor(row, row, pY[t][:, 0:D], ALU.add).then_inc(s_res, 1)
                ops.append([("tensor", pe), ("vector", dve)])
            return ops

        def step(i, p, front_ops):
            ops = prepare(i, p)
            ops += broadcast(i, p, 0)
            for g in range(NGR):
                scans = [item(i, p, g, m) for m in range(ME)]
                ops += interleave(scans, broadcast(i, p, g + 1) if g + 1 < NGR else front_ops)
            return ops + finish(i, p)

        def emit(name, eng):
            run_for(name, eng, front(0, 0) + step(0, 0, front(1, 1)) + step(1, 1, front(2, 0)))
            with eng.Fori(1, NB - 1) as b:
                run_for(name, eng, step(2 * b, 0, front(2 * b + 1, 1)) + step(2 * b + 1, 1, front(2 * b + 2, 0)))
            run_for(name, eng, step(NCH - 2, 0, front(NCH - 1, 1)) + step(NCH - 1, 1, []))

        block = c.enter_context(nc.Block())
        assert ME == TC and TAPS <= CH

        @block.sync
        def _(eng):
            loads = [(w_in[:, :, :], io["mb_w_in"].rearrange("(k p) n -> p k n", p=P)),
                     (w_x[:, :, :], io["mb_w_x"].rearrange("(m p) n -> p m n", p=P)),
                     (w_dt[:, :], io["mb_wdt"]),
                     (w_out[:, :, :], io["mb_w_out"].rearrange("(m p) n -> p m n", p=P)),
                     (a_neg[:, :, :], io["mb_A_log"].rearrange("(m p) n -> p m n", p=P)),
                     (conv_w[:, :, :], io["mb_conv_w"].rearrange("(m p) j -> p m j", p=P))]
            for dst, name in ((conv_b, "mb_conv_b"), (b_dt, "mb_b_dt"), (skip, "mb_D")):
                loads.append((dst[:, :], io[name].rearrange("(m p) -> p m", p=P)))
            with nc.allow_non_contiguous_dma(reason="a few numbers to a partition"):
                for dst, src in loads:
                    eng.dma_start(dst, src).then_inc(s_in, 16)
        ALL_IN = 16 * 9

        @block.gpsimd
        def _(eng):
            eng.wait_ge(s_c, 1)
            for n, lo in enumerate((0, LO)):
                nc.gpsimd.affine_select(out=pick[:, :], in_=pick[:, :], compare_op=ALU.not_equal, fill=1.0,
                                        base=-(lo + RANK), pattern=[[-1, 2 * NST]], channel_multiplier=1).then_inc(s_sel, 1)
                eng.wait_ge(s_sel, n + 1)
            emit("gpsimd", eng)

        @block.vector
        def _(eng):
            nc.vector.memset(pick[:, :], 0.0)
            for q in range(2):
                nc.vector.memset(decay[q][:, :, 0], 0.0)
            nc.vector.memset(e1[0][:, :], 0.0)
            eng.drain().then_inc(s_c, 1)
            eng.wait_ge(s_c, 1)
            nc.vector.tensor_copy(proj_hl[:, :], e1[0][0:LO + NPROJ, :]).then_inc(s_a, 1)
            eng.wait_ge(s_in, ALL_IN)
            eng.wait_ge(s_sel, 2)
            nc.vector.tensor_copy(spread[:, :], pick[:, :]).then_inc(s_a, 1)
            eng.wait_ge(s_c, 2)
            nc.vector.tensor_scalar(a_neg[:, :, :], a_neg[:, :, :], -1.0, None, ALU.mult).then_inc(s_a, 1)
            eng.wait_ge(s_a, 3)
            emit("vector", eng)

        @block.scalar
        def _(eng):
            eng.wait_ge(s_in, ALL_IN)
            eng.wait_ge(s_c, 1)
            nc.scalar.activation(a_neg[:, :, :], a_neg[:, :, :], ACT.Exp).then_inc(s_c, 1)
            eng.wait_ge(s_a, 3)
            emit("scalar", eng)

        @block.tensor
        def _(eng):
            eng.wait_ge(s_in, ALL_IN)
            eng.wait_ge(s_a, 3)
            emit("tensor", eng)


def context_glu(K):
    nc, io, R = K.nc, K.io, K.resid
    with ExitStack() as c:
        ln = LayerNormFront(K, c, "cg")
        sb = lambda n, s, d=F32: K.sb(c, f"cg_{n}", s, d)
        sem = lambda n: K.sem(c, f"cg_{n}")
        ctxT = sb("ctxT", [P, NB, KD, CTX])
        ctx_rows = sb("ctx_rows", [CTX, NB, D])
        ctxT_now = [sb(f"ctxT_now{p}", [P, KD, CTX]) for p in range(2)]
        gelu_h = [sb(f"gelu_h{p}", [CTX, CH]) for p in range(2)]
        gT = [sb(f"gT{p}", [CTX, CH]) for p in range(2)]
        pH = [K.ps(c, f"cg_pH{p}", [CTX, CH]) for p in range(2)]
        pO = K.ps(c, "cg_pO", [P, TC, D])
        s_in, s_now, s_h, s_gelu, s_g, s_o, s_res = (
            sem(n) for n in ("in", "now", "h", "gelu", "g", "o", "res"))
        block = c.enter_context(nc.Block())

        @block.sync
        def _(eng):
            eng.dma_start(ctxT[:, :, :, :], io["ctxT"].rearrange("b (k p) s -> p b k s", p=P)).then_inc(s_in, 16)
            eng.dma_start(ctx_rows[:, :, :], io["ctx"].rearrange("b s d -> s b d")).then_inc(s_in, 16)

        @block.gpsimd
        def _(eng):
            def front(i, p):
                ln.gpsimd(eng, i, p)
                free(eng, s_h, i, 1)
                b = i // CPB
                nc.gpsimd.tensor_copy(ctxT_now[p][:, :, :], ctxT[:, bass.ds(b, 1), :, :].rearrange("p a k s -> p (a k) s")
                                      ).then_inc(s_now, 1)
            eng.wait_ge(s_in, 32)
            chunks(eng, NCH, nothing, front, nothing)

        @block.vector
        def _(eng):
            def tail(i, p):
                after(eng, s_gelu, i, 1)
                free(eng, s_o, i, 1)
                nc.vector.tensor_tensor(gT[p][:, :], gelu_h[p][:, :], pH[p][:, :], ALU.mult).then_inc(s_g, 1)
                after(eng, s_o, i, 1)
                nc.vector.tensor_tensor(rows(R, i), rows(R, i), pO[:, :, :], ALU.add).then_inc(s_res, 1)
            chunks(eng, NCH, nothing, lambda i, p: ln.vector(eng, i, p), tail)

        @block.scalar
        def _(eng):
            def mid(i, p):
                after(eng, s_h, i, 1)
                free(eng, s_g, i, 1)
                nc.scalar.activation(gelu_h[p][:, :], pH[p][:, :], ACT.Gelu).then_inc(s_gelu, 1)
            chunks(eng, NCH, mid, lambda i, p: ln.scalar(eng, i, p, s_h, 1), nothing)

        @block.tensor
        def _(eng):
            def mid(i, p):
                after(eng, ln.s_xnT, i, KD)
                after(eng, s_now, i, 1)
                free(eng, s_g, i, 1)
                for k in range(KD):
                    last = nc.tensor.matmul(pH[p][:, :], ctxT_now[p][:, k, :], ln.xnT[p][:, k, :],
                                            start=(k == 0), stop=(k == KD - 1))
                last.then_inc(s_h, 1)

            def tail(i, p):
                after(eng, s_g, i, 1)
                free(eng, s_res, i, 1, back=1)
                for t in range(TC):
                    last = nc.tensor.matmul(pO[:, t, :], gT[p][:, t * P:(t + 1) * P],
                                            ctx_rows[:, bass.ds(i // CPB, 1), :].rearrange("s a d -> s (a d)"),
                                            start=True, stop=True)
                last.then_inc(s_o, 1)
            eng.wait_ge(s_in, 32)
            chunks(eng, NCH, mid, lambda i, p: ln.tensor(eng, i, p), tail)


class Chain:

    def __init__(self, eng, sem, i, size):
        self.eng, self.sem, self.i, self.size, self.n = eng, sem, i, size, 0

    def do(self, ins):
        self.n += 1
        ins.then_inc(self.sem, 1)
        after(self.eng, self.sem, self.i, self.size, self.n)

    def done(self):
        assert self.n == self.size, (self.n, self.size)


def top1_experts(K):
    nc, io, R = K.nc, K.io, K.resid
    NE = io["t1_w"].shape[0]
    HALF = NE // 2
    with ExitStack() as c:
        ln = LayerNormFront(K, c, "t1")
        sb = lambda n, s, d=F32: K.sb(c, f"t1_{n}", s, d)
        sem = lambda n: K.sem(c, f"t1_{n}")
        router = sb("router", [P, KD, NE])
        router_b = sb("router_b", [P, NE])
        w = sb("w", [P, KD, NE, D])
        b = sb("b", [NE, D])
        logit = sb("logit", [P, TC, NE])
        top = sb("top", [P, TC])
        shifted = sb("shifted", [P, TC, NE])
        e = sb("e", [P, TC, NE])
        total = sb("total", [P, TC])
        gate = sb("gate", [P, TC])
        best = sb("best", [P, TC, 8])
        index = sb("index", [P, TC, 8], U32)
        index_f = sb("index_f", [P, TC])
        send = [sb(f"send{p}", [P, TC, NE]) for p in range(2)]
        sendT = [sb(f"sendT{p}", [NE, CH]) for p in range(2)]
        pY = [K.ps(c, f"t1_pY{h}", [P, HALF, D]) for h in range(2)]
        pB = K.ps(c, "t1_pB", [P, D])
        pS = K.ps(c, "t1_pS", [P, CH])
        logits_ps = pS[:, 0:TC * NE].rearrange("p (t e) -> p t e", e=NE)
        bias_ps = pB[:, :]
        s_in, s_lg, s_v, s_e, s_send, s_sT, s_sTc, s_b, s_badd, s_y, s_comb, s_acc = (
            sem(n) for n in ("in", "lg", "v", "e", "send", "sT", "sTc", "b", "badd", "y", "comb", "acc"))
        block = c.enter_context(nc.Block())
        G = 2 * TC

        @block.sync
        def _(eng):
            eng.dma_start(router[:, :, :], io["t1_router"].rearrange("(k p) e -> p k e", p=P)).then_inc(s_in, 16)
            eng.dma_start(router_b[:, :], io["t1_router_b"].partition_broadcast(P)).then_inc(s_in, 16)
            eng.dma_start(b[:, :], io["t1_b"]).then_inc(s_in, 16)
            for k in range(KD):
                eng.dma_start(w[:, k, :, :], io["t1_w"][:, k * P:(k + 1) * P, :].rearrange("e p d -> p e d")).then_inc(s_in, 16)

        @block.gpsimd
        def _(eng):
            chunks(eng, NCH, nothing, lambda i, p: ln.gpsimd(eng, i, p), nothing)

        @block.vector
        def _(eng):
            def mid(i, p):
                after(eng, s_lg, i, 1)
                ch = Chain(eng, s_v, i, 8)
                ch.do(nc.vector.tensor_tensor(logit[:, :, :], logits_ps,
                                              router_b[:, :].unsqueeze(1).to_broadcast([P, TC, NE]), ALU.add))
                ch.do(nc.vector.tensor_reduce(top[:, :], logit[:, :, :], axis=AX.X, op=ALU.max))
                ch.do(nc.vector.tensor_tensor(shifted[:, :, :], logit[:, :, :],
                                              top[:, :].unsqueeze(2).to_broadcast([P, TC, NE]), ALU.subtract))
                after(eng, s_e, i, 1)
                ch.do(nc.vector.tensor_reduce(total[:, :], e[:, :, :], axis=AX.X, op=ALU.add))
                ch.do(nc.vector.reciprocal(gate[:, :], total[:, :]))
                eng.sem_inc(K.held_vector)
                for t in range(TC):
                    last = nc.vector.max(best[:, t, :], e[:, t, :])
                ch.do(last)
                eng.sem_inc(K.held_vector)
                for t in range(TC):
                    last = nc.vector.max_index(index[:, t, :], best[:, t, :], e[:, t, :])
                ch.do(last)
                ch.do(nc.vector.tensor_copy(index_f[:, :], index[:, :, 0]))
                free(eng, s_sT, i, 1)
                for t in range(TC):
                    nc.vector.tensor_scalar(send[p][:, t, :], K.iota8[:, :], index_f[:, t:t + 1], gate[:, t:t + 1],
                                            ALU.is_equal, ALU.mult).then_inc(s_send, 1)
                ch.done()

            def tail(i, p):
                after(eng, s_send, i, TC)
                for t in range(TC):
                    row = R[:, bass.ds(i * TC + t, 1), :].rearrange("p a d -> p (a d)")
                    after(eng, s_b, i, TC, t + 1)
                    nc.vector.tensor_tensor(row, row, bias_ps, ALU.add).then_inc(s_badd, 1)
                    after(eng, s_badd, i, TC, t + 1)
                    for h in range(2):
                        after(eng, s_y, i, G, 2 * t + h + 1)
                        for j in range(HALF):
                            ins = nc.vector.scalar_tensor_tensor(row, pY[h][:, j, :], send[p][:, t, h * HALF + j:h * HALF + j + 1],
                                                                 row, ALU.mult, ALU.add)
                            if j < HALF - 1:
                                ins.then_inc(s_acc, 1)
                                after(eng, s_acc, i, G * (HALF - 1), (2 * t + h) * (HALF - 1) + j + 1)
                        ins.then_inc(s_comb, 1)
                        after(eng, s_comb, i, G, 2 * t + h + 1)
            chunks(eng, NCH, mid, lambda i, p: ln.vector(eng, i, p), tail)

        @block.scalar
        def _(eng):
            def mid(i, p):
                after(eng, s_v, i, 8, 3)
                nc.scalar.activation(e[:, :, :], shifted[:, :, :], ACT.Exp).then_inc(s_e, 1)

            def tail(i, p):
                after(eng, s_sT, i, 1)
                free(eng, s_b, i, TC)
                nc.scalar.copy(sendT[p][:, :], pS[0:NE, :]).then_inc(s_sTc, 1)
            chunks(eng, NCH, mid, lambda i, p: ln.scalar(eng, i, p, s_y, G), tail)

        @block.tensor
        def _(eng):
            def mid(i, p):
                after(eng, ln.s_xnT, i, KD)
                free(eng, s_sTc, i, 1, back=1)
                for t in range(TC):
                    for k in range(KD):
                        last = nc.tensor.matmul(logits_ps[:, t, :], ln.xnT[p][:, k, t * P:(t + 1) * P], router[:, k, :],
                                                start=(k == 0), stop=(k == KD - 1))
                last.then_inc(s_lg, 1)

            def tail(i, p):
                def group(t, h):
                    n = 2 * t + h
                    if n >= 2 or not isinstance(i, int) or i > 0:
                        eng.wait_ge(s_comb, i * G + n - 1)
                    for k in range(KD):
                        for q in range(HALF // 2):
                            last = nc.tensor.matmul(pY[h][:, 2 * q:2 * q + 2, :], ln.xnT[p][:, k, t * P:(t + 1) * P],
                                                    w[:, k, h * HALF + 2 * q:h * HALF + 2 * q + 2, :],
                                                    start=(k == 0), stop=(k == KD - 1))
                    last.then_inc(s_y, 1)
                group(0, 0)
                group(0, 1)
                after(eng, s_send, i, TC)
                for t in range(TC):
                    last = nc.tensor.transpose(pS[0:NE, t * P:(t + 1) * P], send[p][:, t, :], K.ident[:, :])
                last.then_inc(s_sT, 1)
                after(eng, s_sTc, i, 1)
                for t in range(TC):
                    if t > 0:
                        group(t, 0)
                    if t > 0 or not isinstance(i, int) or i > 0:
                        eng.wait_ge(s_badd, i * TC + t)
                    nc.tensor.matmul(bias_ps, sendT[p][:, t * P:(t + 1) * P], b[:, :], start=True, stop=True).then_inc(s_b, 1)
                    if t > 0:
                        group(t, 1)
            eng.wait_ge(s_in, 16 * (3 + KD))
            chunks(eng, NCH, mid, lambda i, p: ln.tensor(eng, i, p), tail)



def self_attention(K):
    with ExitStack() as c:
        q_rows, k_rows = (K.sb(c, f"sa_{n}_rows", [P, NT, D]) for n in ("q", "k"))
        v_dram = K.nc.dram_tensor("sa_v_dram", [TOK, D], F32).ap()
        _project_qkv(K, q_rows, k_rows, v_dram)
        _attend(K, q_rows, k_rows, v_dram)


def _project_qkv(K, q_rows, k_rows, v_dram):
    nc, io = K.nc, K.io
    with ExitStack() as c:
        ln = LayerNormFront(K, c, "qk")
        sb = lambda n, s, d=F32: K.sb(c, f"qk_{n}", s, d)
        sem = lambda n: K.sem(c, f"qk_{n}")
        w = sb("w", [P, KD, 3, D])
        v_rows = [sb(f"v_rows{p}", [P, TC, D]) for p in range(2)]
        pQK = [K.ps(c, f"qk_pQK{q}", [P, 2, D]) for q in range(2)]
        pV = [K.ps(c, f"qk_pV{q}", [P, D]) for q in range(2)]
        s_in, s_mm, s_q, s_v = (sem(n) for n in ("in", "mm", "q", "v"))
        s_out = [sem(f"out{p}") for p in range(2)]
        block = c.enter_context(nc.Block())

        @block.sync
        def _(eng):
            for n, name in enumerate(("sa_wqT", "sa_wkT", "sa_wvT")):
                eng.dma_start(w[:, :, n, :], io[name].rearrange("(k p) n -> p k n", p=P)).then_inc(s_in, 16)

            def tail(i, p):
                after(eng, s_v, i, TC)
                eng.dma_start(v_dram[bass.ds(i * CH, CH), :].rearrange("(t p) d -> p t d", p=P), v_rows[p][:, :, :]
                              ).then_inc(s_out[p], 16)
            chunks(eng, NCH, nothing, nothing, tail)
            for p in range(2):
                eng.wait_ge(s_out[p], 16 * (NCH // 2))

        @block.gpsimd
        def _(eng):
            chunks(eng, NCH, nothing, lambda i, p: ln.gpsimd(eng, i, p), nothing)

        @block.vector
        def _(eng):
            def tail(i, p):
                for t in range(TC):
                    after(eng, s_mm, i, TC, t + 1)
                    nc.vector.tensor_scalar(q_rows[:, bass.ds(i * TC + t, 1), :].rearrange("p a d -> p (a d)"),
                                            pQK[t % 2][:, 0, :], 0.25, None, ALU.mult).then_inc(s_q, 1)
                    nc.vector.tensor_copy(k_rows[:, bass.ds(i * TC + t, 1), :].rearrange("p a d -> p (a d)"),
                                          pQK[t % 2][:, 1, :]).then_inc(s_q, 1)
            chunks(eng, NCH, nothing, lambda i, p: ln.vector(eng, i, p), tail)

        @block.scalar
        def _(eng):
            def tail(i, p):
                if not isinstance(i, int) or i >= 2:
                    eng.wait_ge(s_out[p], (i // 2) * 16)
                for t in range(TC):
                    after(eng, s_mm, i, TC, t + 1)
                    nc.scalar.copy(v_rows[p][:, t, :], pV[t % 2][:, :]).then_inc(s_v, 1)
            chunks(eng, NCH, nothing, lambda i, p: ln.scalar(eng, i, p, s_mm, TC), tail)

        @block.tensor
        def _(eng):
            def tail(i, p):
                after(eng, ln.s_xnT, i, KD)
                for t in range(TC):
                    n = i * TC + t
                    if t >= 2 or n_positive(i):
                        eng.wait_ge(s_q, 2 * n - 2)
                        eng.wait_ge(s_v, n - 1)
                    for k in range(KD):
                        nc.tensor.matmul(pQK[t % 2][:, :, :], ln.xnT[p][:, k, t * P:(t + 1) * P], w[:, k, 0:2, :],
                                         start=(k == 0), stop=(k == KD - 1))
                    for k in range(KD):
                        last = nc.tensor.matmul(pV[t % 2][:, :], ln.xnT[p][:, k, t * P:(t + 1) * P], w[:, k, 2, :],
                                                start=(k == 0), stop=(k == KD - 1))
                    last.then_inc(s_mm, 1)
            eng.wait_ge(s_in, 48)
            chunks(eng, NCH, nothing, lambda i, p: ln.tensor(eng, i, p), tail)


def _attend(K, q_rows, k_rows, v_dram):
    nc, io, R = K.nc, K.io, K.resid
    HD = 16
    C16 = D // HD
    NPOS = P // 2 * C16
    QB = NPOS // P
    PARTS = 4 * HD
    NEG = -3e38
    HALF = NPOS // 2
    with ExitStack() as c:
        sb = lambda n, s, d=F32: K.sb(c, f"at_{n}", s, d)
        sem = lambda n: K.sem(c, f"at_{n}")
        wo = sb("wo", [P, KD, D])
        ident_bf = sb("ident_bf", [P, P], BF16)
        mask_q = sb("mask_q", [P, P], BF16)
        mask_k = sb("mask_k", [P, P], BF16)
        zero_bf = sb("zero_bf", [P, 32], BF16)
        pick = sb("pick", [P, 2, HD + 1])
        q_hl = [sb(f"q_hl{p}", [P, C16, 2, 2, HD], F32R) for p in range(2)]
        k_hl = [sb(f"k_hl{p}", [P, C16, 2, 2, HD], F32R) for p in range(2)]
        qT = [sb(f"qT{p}", [PARTS + 2, 2, NPOS], F32R) for p in range(2)]
        kT = [sb(f"kT{p}", [PARTS + 2, 2, NPOS], F32R) for p in range(2)]
        ones = sb("ones", [P, 2 * NPOS])
        nm = sb("nm", [P, 2, QB])
        nm_hl = sb("nm_hl", [P, 2, 2, QB], F32R)
        nmT = [sb(f"nmT{p}", [4 * QB, P], F32R) for p in range(2)]
        v = [sb(f"v{p}", [P, 2, QB, 32]) for p in range(2)]
        e = [sb(f"e{g}", [P, 2, 512]) for g in range(3)]
        o_sb = sb("o_sb", [P, 2, HALF])
        inv = sb("inv", [P, C16])
        wei = sb("wei", [P, D])
        weiT = sb("weiT", [P, KD, P])
        pF = [K.ps(c, f"at_pF{q}", [P, 512]) for q in range(2)]
        pS = K.ps(c, "at_pS", [P, 2, 512])
        pE = K.ps(c, "at_pE", [P, 2, 512])
        pO = [K.ps(c, f"at_pO{q}", [P, 512]) for q in range(2)]
        (s_in, s_c, s_c2, s_hl, s_tq, s_tk, s_qT, s_kT, s_sc, s_max, s_nm, s_nmT, s_nmc, s_st, s_ex, s_pv, s_ob0, s_ob1,
         s_bk, s_inv, s_wei, s_wT, s_wTc, s_f, s_res) = (sem(n) for n in (
             "in", "c", "c2", "hl", "tq", "tk", "qTs", "kTs", "sc", "max", "nms", "nmTs", "nmc", "st", "ex", "pv", "ob0", "ob1",
             "bk", "invs", "weis", "wT", "wTc", "f", "res"))
        s_row = [sem(f"row{p}") for p in range(2)]
        s_v = [sem(f"v{p}s") for p in range(2)]
        flat = lambda a: a.rearrange("p a d -> p (a d)")

        S_ITEMS = [((0, 1), qb) for qb in range(QB // 2)] + [((a,), qb) for qb in range(QB // 2, QB) for a in range(2)]
        NS = len(S_ITEMS)
        width = lambda hf, kb: min(HALF, HALF * (hf + 1) - kb * P)
        SLOTS = [[(1, 0)], [(1, 1)], [(1, 2)], [(1, 3)], [(0, 0)], [(0, 1), (0, 3)], [(1, 4)], [(1, 5), (1, 7)], [(0, 2), (1, 6)]]
        NG = len(SLOTS)
        assert all(sum(width(*x) for x in s) == 512 for s in SLOTS)
        LAST = {(hf, kb % 2): (hf, kb) for s in SLOTS for hf, kb in s}
        FIRST = {}
        for s in SLOTS:
            for hf, kb in s:
                FIRST.setdefault((hf, kb % 2), (hf, kb))

        def front(i, p):
            ops = []

            def split(eng):
                if not isinstance(i, int) or i >= 2:
                    eng.wait_ge(s_tq, 4 * i - 4)
                    eng.wait_ge(s_tk, 4 * i - 4)
                both_of = lambda rows_: flat(rows_[:, bass.ds(i, 1), :]).rearrange("p (c d) -> p c d", d=HD
                                                                                    ).unsqueeze(2).to_broadcast([P, C16, 2, HD])
                q_part = lambda x: q_hl[p][:, :, :, x, :]
                k_part = lambda x: k_hl[p][:, :, x, :, :]
                nc.gpsimd.tensor_copy(q_part(0), both_of(q_rows)).then_inc(s_hl, 1)
                nc.gpsimd.tensor_copy(k_part(0), both_of(k_rows)).then_inc(s_hl, 1)
                after(eng, s_hl, i, 4, 1)
                eng.sem_inc(K.held_pool)
                nc.gpsimd.tensor_tensor(q_part(1), both_of(q_rows), q_part(0).bitcast(F32), ALU.subtract).then_inc(s_hl, 1)
                after(eng, s_hl, i, 4, 2)
                eng.sem_inc(K.held_pool)
                nc.gpsimd.tensor_tensor(k_part(1), both_of(k_rows), k_part(0).bitcast(F32), ALU.subtract).then_inc(s_hl, 1)
            ops.append([("gpsimd", split)])

            def load_v(eng):
                if not isinstance(i, int) or i >= 2:
                    eng.wait_ge(s_pv, NG * (i - 1))
                for a in range(2):
                    src = v_dram[bass.ds(i * P + a * (P // 2), P // 2), :].rearrange("(kb r) (c d) -> (r c) kb d", r=P // C16, d=HD)
                    eng.dma_start(v[p][:, a, :, 0:HD], src).then_inc(s_v[p], 16)
            ops.append([("sync", load_v)])

            def group(g):
                def pe(eng):
                    if g == 0:
                        after(eng, s_hl, i, 4)
                        if n_positive(i):
                            eng.wait_ge(s_nmc, i)
                    if g or n_positive(i):
                        eng.wait_ge(s_qT, i * 4 + g)
                        eng.wait_ge(s_kT, i * 4 + g)
                        eng.sem_inc(K.held_tensor)
                    for cc in range(4):
                        col = q_hl[p][:, 4 * g + cc, :, :, :].rearrange("p x y d -> p (x y d)").bitcast(F32)
                        last = nc.tensor.transpose(pF[0][0:PARTS, cc * P:(cc + 1) * P], col, K.ident[:, :])
                    last.then_inc(s_tq, 1)
                    for cc in range(4):
                        col = k_hl[p][:, 4 * g + cc, :, :, :].rearrange("p x y d -> p (x y d)").bitcast(F32)
                        last = nc.tensor.transpose(pF[1][0:PARTS, cc * P:(cc + 1) * P], col, K.ident[:, :])
                    last.then_inc(s_tk, 1)

                def out(T):
                    return T[0:PARTS, :, :].rearrange("x a (r c) -> x c a r", c=C16)[:, 4 * g:4 * g + 4, :, :]

                def act(eng):
                    if g == 0 and (not isinstance(i, int) or i >= 2):
                        eng.wait_ge(s_pv, NG * (i - 1))
                    after(eng, s_tq, i, 4, g + 1)
                    nc.scalar.copy(out(qT[p]), pF[0][0:PARTS, :].rearrange("x (c a r) -> x c a r", c=4, a=2)).then_inc(s_qT, 1)

                def dve(eng):
                    if g == 0 and (not isinstance(i, int) or i >= 2):
                        eng.wait_ge(s_pv, NG * (i - 1))
                    after(eng, s_tk, i, 4, g + 1)
                    nc.vector.tensor_copy(out(kT[p]), pF[1][0:PARTS, :].rearrange("x (c a r) -> x c a r", c=4, a=2)).then_inc(s_kT, 1)
                ops.append([("tensor", pe), ("scalar", act), ("vector", dve)])
            for g in range(4):
                group(g)

            def item(s):
                heads, qb = S_ITEMS[s]
                w = (qb + 1) * P

                def pe(eng):
                    if s == 0:
                        after(eng, s_qT, i, 4)
                        after(eng, s_kT, i, 4)
                    if s or n_positive(i):
                        eng.wait_ge(s_max, i * NS + s)
                    for a in heads:
                        for w0 in range(0, w, 512):
                            w1 = min(w, w0 + 512)
                            bank = a if len(heads) == 2 else w0 // 512
                            nc.tensor.matmul(pS[:, bank, 0:w1 - w0], qT[p][0:PARTS, a, qb * P:(qb + 1) * P],
                                             kT[p][0:PARTS, a, w0:w1], start=True, stop=(w1 < w))
                        last = nc.tensor.matmul(pS[:, bank, w1 - w0 - P:w1 - w0], ident_bf[:, :], mask_q[:, :],
                                                start=False, stop=True)
                    last.then_inc(s_sc, 1)

                def dve(eng):
                    after(eng, s_sc, i, NS, s + 1)
                    if len(heads) == 2:
                        src, dst = pS[:, :, 0:w], nm[:, :, qb]
                    else:
                        src, dst = pS[:, :, :].rearrange("p b n -> p (b n)")[:, 0:w], nm[:, heads[0], qb:qb + 1]
                    nc.vector.tensor_reduce(dst, src, axis=AX.X, op=ALU.max, negate=True).then_inc(s_max, 1)
                ops.append([("tensor", pe), ("vector", dve)])
            for s in range(NS):
                item(s)

            def parts_of_max(eng):
                after(eng, s_max, i, NS)
                if n_positive(i):
                    eng.wait_ge(s_nmT, i)
                nc.vector.tensor_copy(nm_hl[:, 0, :, :], nm[:, :, :]).then_inc(s_nm, 1)
                after(eng, s_nm, i, 2, 1)
                nc.vector.tensor_tensor(nm_hl[:, 1, :, :], nm[:, :, :], nm_hl[:, 0, :, :].bitcast(F32), ALU.subtract).then_inc(s_nm, 1)

            def pe_max(eng):
                after(eng, s_nm, i, 2)
                nc.tensor.transpose(pF[0][0:4 * QB, 0:P], nm_hl[:, :, :, :].rearrange("p x a b -> p (x a b)").bitcast(F32), K.ident[:, :]).then_inc(s_nmT, 1)

            def act_max(eng):
                if not isinstance(i, int) or i >= 2:
                    eng.wait_ge(s_row[p], (i // 2) * 32)
                after(eng, s_nmT, i, 1)
                nc.scalar.copy(nmT[p][:, :], pF[0][0:4 * QB, 0:P]).then_inc(s_nmc, 1)

            def move_max(eng):
                after(eng, s_nmc, i, 1)
                for part in range(2):
                    eng.dma_start(qT[p][PARTS + part:PARTS + part + 1, :, :].bitcast(F32).rearrange("o a (b q) -> o (a b) q", q=P),
                                  nmT[p][part * 2 * QB:(part + 1) * 2 * QB, :].bitcast(F32)).then_inc(s_row[p], 16)
            ops.append([("vector", parts_of_max), ("tensor", pe_max), ("scalar", act_max), ("sync", move_max)])
            return ops

        def tail(i, p):
            ops = []

            def scores(g):
                def pe(eng):
                    if g == 0:
                        eng.wait_ge(s_row[p], (i // 2) * 32 + 32)
                    if g or n_positive(i):
                        eng.wait_ge(s_ex, i * NG + g)
                    for a in range(2):
                        at = 0
                        for n, (hf, kb) in enumerate(SLOTS[g]):
                            w = width(hf, kb)
                            diag = kb * P >= hf * HALF
                            q0 = HALF * (hf + 1) - w
                            last = nc.tensor.matmul(pE[:, a, at:at + w], kT[p][:, a, kb * P:(kb + 1) * P],
                                                    qT[p][:, a, q0:q0 + w], start=(n == 0), stop=not diag, skip_group_check=True)
                            if diag:
                                last = nc.tensor.matmul(pE[:, a, at:at + P], ident_bf[:, :], mask_k[:, :],
                                                        start=False, stop=True, skip_group_check=True)
                            at += w
                    last.then_inc(s_st, 1)

                def act(eng):
                    after(eng, s_st, i, NG, g + 1)
                    if g >= 3 or n_positive(i):
                        eng.wait_ge(s_pv, i * NG + g - 2)
                    nc.scalar.activation(e[g % 3][:, :, :], pE[:, :, :], ACT.Exp).then_inc(s_ex, 1)
                return [("tensor", pe), ("scalar", act)]

            def product(g):
                def pe(eng):
                    if g == 0:
                        eng.wait_ge(s_v[p], (i // 2) * 32 + 32)
                        if n_positive(i):
                            eng.wait_ge(s_res, i)
                    after(eng, s_ex, i, NG, g + 1)
                    at = 0
                    for hf, kb in SLOTS[g]:
                        w = width(hf, kb)
                        for a in range(2):
                            j = 2 * a + kb % 2
                            first, final = FIRST[hf, kb % 2] == (hf, kb), LAST[hf, kb % 2] == (hf, kb)
                            last = nc.tensor.matmul(pO[hf][32 * j:32 * j + 32, HALF - w:HALF], v[p][:, a, kb, :],
                                                    e[g % 3][:, a, at:at + w], start=first, stop=final, skip_group_check=True)
                            if first and w < HALF:
                                last = nc.tensor.matmul(pO[hf][32 * j:32 * j + 32, 0:HALF - w], zero_bf[:, :],
                                                        ident_bf[:, 0:HALF - w], start=False, stop=True, skip_group_check=True)
                        at += w
                    last.then_inc(s_pv, 1)
                return [("tensor", pe)]
            ops.append(scores(0))
            for g in range(1, NG):
                ops.append(scores(g))
                ops.append(product(g - 1))
            ops.append(product(NG - 1))

            def act_o(eng):
                after(eng, s_pv, i, NG)
                if n_positive(i):
                    eng.wait_ge(s_bk, i)
                nc.scalar.copy(o_sb[:, 0, :], pO[0][:, :]).then_inc(s_ob0, 1)

            def dve_o(eng):
                after(eng, s_pv, i, NG)
                if n_positive(i):
                    eng.wait_ge(s_bk, i)
                nc.vector.tensor_copy(o_sb[:, 1, :], pO[1][:, :]).then_inc(s_ob1, 1)

            def pe_back(eng):
                after(eng, s_ob0, i, 1)
                after(eng, s_ob1, i, 1)
                for cc in range(C16):
                    col = o_sb[:, :, :].rearrange("x f (r c) -> x c (f r)", c=C16)[:, cc, :]
                    for a in range(2):
                        last = nc.tensor.matmul(pO[0][64 * a:64 * a + 64, cc * (HD + 1):(cc + 1) * (HD + 1)], col, pick[:, a, :],
                                                start=True, stop=True)
                last.then_inc(s_bk, 1)

            def dve_wei(eng):
                back = pO[0][:, 0:C16 * (HD + 1)].rearrange("p (c d) -> p c d", d=HD + 1)
                after(eng, s_bk, i, 1)
                nc.vector.reciprocal(inv[:, :], back[:, :, HD]).then_inc(s_inv, 1)
                after(eng, s_inv, i, 1)
                if n_positive(i):
                    eng.wait_ge(s_wT, i)
                nc.vector.tensor_tensor(wei[:, :].rearrange("p (c d) -> p c d", d=HD), back[:, :, 0:HD],
                                        inv[:, :].unsqueeze(2).to_broadcast([P, C16, HD]), ALU.mult).then_inc(s_wei, 1)

            def pe_wT(eng):
                after(eng, s_wei, i, 1)
                for k in range(KD):
                    last = nc.tensor.transpose(pO[1][:, k * P:(k + 1) * P], wei[:, k * P:(k + 1) * P], K.ident[:, :])
                last.then_inc(s_wT, 1)

            def act_wT(eng):
                after(eng, s_wT, i, 1)
                if n_positive(i):
                    eng.wait_ge(s_f, i)
                nc.scalar.copy(weiT[:, :, :], pO[1][:, 0:D].rearrange("p (k q) -> p k q", k=KD)).then_inc(s_wTc, 1)

            def pe_f(eng):
                after(eng, s_wTc, i, 1)
                for k in range(KD):
                    last = nc.tensor.matmul(pO[0][:, 0:D], weiT[:, k, :], wo[:, k, :], start=(k == 0), stop=(k == KD - 1))
                last.then_inc(s_f, 1)

            def dve_res(eng):
                after(eng, s_f, i, 1)
                row = flat(R[:, bass.ds(i, 1), :])
                nc.vector.tensor_tensor(row, row, pO[0][:, 0:D], ALU.add).then_inc(s_res, 1)
            ops.append([("scalar", act_o), ("vector", dve_o), ("tensor", pe_back)])
            ops.append([("vector", dve_wei), ("tensor", pe_wT)])
            ops.append([("scalar", act_wT), ("tensor", pe_f)])
            ops.append([("vector", dve_res)])
            return ops

        def both(tail_ops, front_ops):
            out, done = [], 0
            for n, op in enumerate(tail_ops):
                out.append(op)
                upto = (n + 1) * len(front_ops) // len(tail_ops)
                out += front_ops[done:upto]
                done = upto
            return out + front_ops[done:]

        def emit(name, eng):
            def run(ops):
                for op in ops:
                    for who, fn in op:
                        if who == name:
                            fn(eng)
            run(front(0, 0))
            run(both(tail(0, 0), front(1, 1)))
            with eng.Fori(1, NT // 2) as j:
                run(both(tail(2 * j - 1, 1), front(2 * j, 0)))
                run(both(tail(2 * j, 0), front(2 * j + 1, 1)))
            run(tail(NT - 1, 1))

        block = c.enter_context(nc.Block())

        @block.sync
        def _(eng):
            eng.dma_start(wo[:, :, :], io["sa_woT"].rearrange("(k p) n -> p k n", p=P)).then_inc(s_in, 16)
            eng.wait_ge(s_c2, 1)
            emit("sync", eng)

        @block.gpsimd
        def _(eng):
            eng.wait_ge(s_c, 1)
            for mask, step, mult in ((mask_q, -1, 1), (mask_k, 1, -1)):
                nc.gpsimd.affine_select(out=mask[:, :], in_=mask[:, :], compare_op=ALU.is_ge, fill=NEG,
                                        base=0, pattern=[[step, P]], channel_multiplier=mult)
            nc.gpsimd.tensor_copy(ident_bf[:, :], K.ident[:, :])
            for par in range(2):
                nc.gpsimd.affine_select(out=pick[:, :, :], in_=pick[:, :, :], compare_op=ALU.not_equal, fill=1.0,
                                        base=-32 * par, pattern=[[-64, 2], [-1, HD + 1]], channel_multiplier=1).then_inc(s_c2, 1)
                eng.wait_ge(s_c2, 1 + par)
            emit("gpsimd", eng)

        @block.vector
        def _(eng):
            nc.vector.memset(mask_q[:, :], 0.0)
            nc.vector.memset(mask_k[:, :], 0.0)
            nc.vector.memset(zero_bf[:, :], 0.0)
            nc.vector.memset(pick[:, :, :], 0.0)
            nc.vector.memset(ones[:, :], 1.0)
            for p in range(2):
                nc.vector.memset(v[p][:, :, :, HD:HD + 1], 1.0)
                nc.vector.memset(v[p][:, :, :, HD + 1:32], 0.0)
            eng.drain().then_inc(s_c, 1)
            eng.wait_ge(s_c, 1)
            for p in range(2):
                last = nc.vector.tensor_copy(kT[p][PARTS:PARTS + 2, :, :],
                                             ones[PARTS:PARTS + 2, :].rearrange("x (a l) -> x a l", a=2)).then_inc(s_c, 1)
            emit("vector", eng)

        @block.scalar
        def _(eng):
            emit("scalar", eng)

        @block.tensor
        def _(eng):
            eng.wait_ge(s_in, 16)
            eng.wait_ge(s_c, 3)
            eng.wait_ge(s_c2, 2)
            emit("tensor", eng)


def cross_attention(K):
    nc, io, R = K.nc, K.io, K.resid
    HD = 16
    NH = D // HD
    HM = P // HD
    HG = HM // 2
    SCALE = float(HD) ** -0.5
    with ExitStack() as c:
        ln = LayerNormFront(K, c, "xa")
        sb = lambda n, s, d=F32: K.sb(c, f"xa_{n}", s, d)
        sem = lambda n: K.sem(c, f"xa_{n}")
        ctxT = sb("ctxT", [P, KD, NB, CTX])
        wq, wk, wv, wo = (sb(n, [P, KD, D]) for n in ("wq", "wk", "wv", "wo"))
        bq, bk = sb("bq", [P, KD]), sb("bk", [P, KD])
        bv, bo = sb("bv", [P, D]), sb("bo", [P, D])
        own = sb("own", [P, HM])
        kT = sb("kT", [P, KD, NB, CTX])
        kdiag = [sb(f"kdiag{m}", [P, NB, HM, CTX]) for m in range(KD)]
        v = sb("v", [CTX, NB, D])
        qT = [sb(f"qT{p}", [P, KD, CH]) for p in range(2)]
        top = [sb(f"top{m}", [P, HM]) for m in range(KD)]
        e = [sb(f"e{m}", [P, HM, CTX]) for m in range(KD)]
        total = sb("total", [P, NH])
        inv = sb("inv", [P, NH])
        eT = [sb(f"eT{q}", [CTX, 4, P]) for q in range(2)]
        mixed = sb("mixed", [P, D])
        mixedT = sb("mixedT", [P, KD, P])
        pS = [K.ps(c, f"xa_pS{m}", [P, 2, 512]) for m in range(KD)]
        pX = K.ps(c, "xa_pX", [P, 512])
        pV = K.ps(c, "xa_pV", [P, D])
        (s_in, s_own, s_kT, s_kTc, s_kd, s_vp, s_vc, s_q, s_qc, s_S, s_sub, s_v, s_exp, s_eT, s_eTc, s_pv, s_mix, s_mT,
         s_mTc, s_F, s_res, s_bo) = (sem(n) for n in (
             "in", "own", "kTp", "kTc", "kd", "vp", "vc", "q", "qc", "S", "sub", "v", "exp", "eTp", "eTc", "pv", "mix",
             "mT", "mTc", "F", "res", "bosum"))
        LOADS = 9
        block = c.enter_context(nc.Block())

        def tiles(fn):
            def tail(i, p):
                for t in range(TC):
                    fn(i, p, t, i * TC + t)
            return tail

        @block.sync
        def _(eng):
            for k in range(KD):
                eng.dma_start(ctxT[:, k, :, :], io["ctxT"][:, k * P:(k + 1) * P, :].rearrange("b p s -> p b s")).then_inc(s_in, 16)
            for dst, name in ((wq, "xa_wqT"), (wk, "xa_wkT"), (wv, "xa_wvT"), (wo, "xa_woT")):
                eng.dma_start(dst[:, :, :], io[name].rearrange("(k p) n -> p k n", p=P)).then_inc(s_in, 16)
            with nc.allow_non_contiguous_dma(reason="256 biases, one to a partition"):
                eng.dma_start(bq[:, :], io["xa_bq"].rearrange("(k p) -> p k", p=P)).then_inc(s_in, 16)
                eng.dma_start(bk[:, :], io["xa_bk"].rearrange("(k p) -> p k", p=P)).then_inc(s_in, 16)
            eng.dma_start(bv[:, :], io["xa_bv"].partition_broadcast(P)).then_inc(s_in, 16)
            eng.dma_start(bo[:, :], io["xa_bo"].partition_broadcast(P)).then_inc(s_in, 16)
        ALL_IN = 16 * (KD + 8)

        @block.gpsimd
        def _(eng):
            nc.gpsimd.memset(own[:, :], 1.0).then_inc(s_own, 1)
            eng.wait_ge(s_own, 1)
            nc.gpsimd.affine_select(out=own[:, :], in_=own[:, :], compare_op=ALU.is_ge, fill=0.0, base=0,
                                    pattern=[[-HD, HM]], channel_multiplier=1).then_inc(s_own, 1)
            eng.wait_ge(s_own, 2)
            nc.gpsimd.affine_select(out=own[:, :], in_=own[:, :], compare_op=ALU.is_ge, fill=0.0, base=HD - 1,
                                    pattern=[[HD, HM]], channel_multiplier=-1).then_inc(s_own, 1)

            def tail(i, p, t, n):
                after(eng, s_res, n, 1)
                row = R[:, bass.ds(n, 1), :].rearrange("p a d -> p (a d)")
                nc.gpsimd.tensor_tensor(row, row, bo[:, :], ALU.add).then_inc(s_bo, 1)
            eng.wait_ge(s_in, ALL_IN)
            chunks(eng, NCH, nothing, lambda i, p: ln.gpsimd(eng, i, p), tiles(tail))

        @block.vector
        def _(eng):
            eng.wait_ge(s_in, ALL_IN)
            eng.wait_ge(s_own, 3)
            for m in range(KD):
                eng.wait_ge(s_kTc, m + 1)
                for h in range(HM):
                    ins = nc.vector.tensor_scalar(kdiag[m][:, :, h, :], kT[:, m, :, :], own[:, h:h + 1], None, ALU.mult)
                ins.then_inc(s_kd, 1)
            for b in range(NB):
                eng.wait_ge(s_vp, b + 1)
                nc.vector.tensor_tensor(v[:, b, :], pV[0:CTX, :], bv[0:CTX, :], ALU.add).then_inc(s_vc, 1)

            def tail(i, p, t, n):
                for m in range(KD):
                    after(eng, s_S, n, KD, m + 1)
                    scores = pS[m][:, :, 0:HG * CTX].rearrange("p g (h s) -> p g h s", s=CTX)
                    nc.vector.tensor_reduce(top[m][:, :].rearrange("p (g h) -> p g h", g=2), scores, axis=AX.X, op=ALU.max
                                            ).then_inc(s_v, 1)
                    after(eng, s_v, n, KD + 2, m + 1)
                    if n_positive(n):
                        eng.wait_ge(s_eT, n * 4)
                    nc.vector.tensor_tensor(e[m][:, :, :].rearrange("p (g h) s -> p g h s", g=2), scores,
                                            top[m][:, :].rearrange("p (g h) -> p g h", g=2).unsqueeze(3).to_broadcast([P, 2, HG, CTX]),
                                            ALU.subtract).then_inc(s_sub, 1)
                for m in range(KD):
                    after(eng, s_exp, n, KD, m + 1)
                    ins = nc.vector.tensor_reduce(total[:, m * HM:(m + 1) * HM], e[m][:, :, :], axis=AX.X, op=ALU.add)
                ins.then_inc(s_v, 1)
                after(eng, s_v, n, KD + 2, KD + 1)
                nc.vector.reciprocal(inv[:, :], total[:, :]).then_inc(s_v, 1)
                after(eng, s_v, n, KD + 2)
                after(eng, s_pv, n, 4)
                if n_positive(n):
                    eng.wait_ge(s_mT, n)
                nc.vector.tensor_tensor(mixed[:, :].rearrange("p (h d) -> p h d", d=HD),
                                        pV[:, :].rearrange("p (h d) -> p h d", d=HD),
                                        inv[:, :].unsqueeze(2).to_broadcast([P, NH, HD]), ALU.mult).then_inc(s_mix, 1)
                after(eng, s_F, n, 1)
                row = R[:, bass.ds(n, 1), :].rearrange("p a d -> p (a d)")
                nc.vector.tensor_tensor(row, row, pX[:, 0:D], ALU.add).then_inc(s_res, 1)
            chunks(eng, NCH, nothing, lambda i, p: ln.vector(eng, i, p), tiles(tail))

        @block.scalar
        def _(eng):
            eng.wait_ge(s_in, ALL_IN)
            for m in range(KD):
                eng.wait_ge(s_kT, m + 1)
                nc.scalar.activation(kT[:, m, :, :], pX[:, 0:NB * CTX].rearrange("p (b s) -> p b s", s=CTX),
                                     ACT.Identity, bias=bk[:, m:m + 1]).then_inc(s_kTc, 1)

            def mid(i, p):
                for m in range(KD):
                    after(eng, s_q, i, KD, m + 1)
                    if m == 0:
                        free(eng, s_S, i, KD * TC)
                    nc.scalar.activation(qT[p][:, m, :], pS[m][:, 0, :], ACT.Identity, bias=bq[:, m:m + 1]).then_inc(s_qc, 1)

            def tail(i, p, t, n):
                for m in range(KD):
                    after(eng, s_sub, n, KD, m + 1)
                    nc.scalar.activation(e[m][:, :, :], e[m][:, :, :], ACT.Exp, scale=SCALE).then_inc(s_exp, 1)
                for g in range(4):
                    after(eng, s_eT, n, 4, g + 1)
                    if n_positive(n) or g >= 2:
                        eng.wait_ge(s_pv, n * 4 + g - 1)
                    nc.scalar.copy(eT[g % 2][:, :, :], pX[0:CTX, :].rearrange("s (h q) -> s h q", q=P)).then_inc(s_eTc, 1)
                after(eng, s_mT, n, 1)
                if n_positive(n):
                    eng.wait_ge(s_F, n)
                nc.scalar.copy(mixedT[:, :, :], pX[:, 0:D].rearrange("p (k q) -> p k q", k=KD)).then_inc(s_mTc, 1)
            chunks(eng, NCH, mid, lambda i, p: ln.scalar(eng, i, p, s_q, KD), tiles(tail))

        @block.tensor
        def _(eng):
            eng.wait_ge(s_in, ALL_IN)
            for m in range(KD):
                if m:
                    eng.wait_ge(s_kTc, m)
                for k in range(KD):
                    last = nc.tensor.matmul(pX[:, 0:NB * CTX], wk[:, k, m * P:(m + 1) * P],
                                            ctxT[:, k, :, :].rearrange("p b s -> p (b s)"), start=(k == 0), stop=(k == KD - 1))
                last.then_inc(s_kT, 1)
            for b in range(NB):
                if b:
                    eng.wait_ge(s_vc, b)
                for k in range(KD):
                    last = nc.tensor.matmul(pV[0:CTX, :], ctxT[:, k, b, :], wv[:, k, :], start=(k == 0), stop=(k == KD - 1))
                last.then_inc(s_vp, 1)
            eng.wait_ge(s_kd, KD)
            eng.wait_ge(s_vc, NB)

            def mid(i, p):
                after(eng, ln.s_xnT, i, KD)
                if n_positive(i):
                    eng.wait_ge(s_sub, i * TC * KD)
                for m in range(KD):
                    for k in range(KD):
                        last = nc.tensor.matmul(pS[m][:, 0, :], wq[:, k, m * P:(m + 1) * P], ln.xnT[p][:, k, :],
                                                start=(k == 0), stop=(k == KD - 1))
                    last.then_inc(s_q, 1)

            def scores(i, p, t, n):
                for m in range(KD):
                    if t == 0:
                        after(eng, s_qc, i, KD)
                    else:
                        eng.wait_ge(s_sub, n * KD - KD + m + 1)
                    for g in range(2):
                        last = nc.tensor.matmul(pS[m][:, g, 0:HG * CTX], qT[p][:, m, t * P:(t + 1) * P],
                                                kdiag[m][:, bass.ds(i // CPB, 1), g * HG:(g + 1) * HG, :].rearrange("p a h s -> p (a h s)"),
                                                start=True, stop=True)
                    last.then_inc(s_S, 1)

            def tail(i, p):
                scores(i, p, 0, i * TC)
                for t in range(TC):
                    n = i * TC + t
                    if n_positive(n):
                        eng.wait_ge(s_res, n)
                        eng.wait_ge(s_mix, n)
                    for g in range(4):
                        after(eng, s_exp, n, KD, g // 2 + 1)
                        if g:
                            eng.wait_ge(s_eTc, n * 4 + g)
                        for h in range(4):
                            last = nc.tensor.transpose(pX[0:CTX, h * P:(h + 1) * P], e[g // 2][:, (g % 2) * 4 + h, :], K.ident[:, :])
                        last.then_inc(s_eT, 1)
                        if g == 0 and t + 1 < TC:
                            scores(i, p, t + 1, n + 1)
                        after(eng, s_eTc, n, 4, g + 1)
                        for h in range(4):
                            hh = g * 4 + h
                            last = nc.tensor.matmul(pV[:, hh * HD:(hh + 1) * HD], eT[g % 2][:, h, :],
                                                    v[:, bass.ds(i // CPB, 1), hh * HD:(hh + 1) * HD].rearrange("s a d -> s (a d)"),
                                                    start=True, stop=True)
                        last.then_inc(s_pv, 1)
                    after(eng, s_mix, n, 1)
                    for k in range(KD):
                        last = nc.tensor.transpose(pX[:, k * P:(k + 1) * P], mixed[:, k * P:(k + 1) * P], K.ident[:, :])
                    last.then_inc(s_mT, 1)
                    after(eng, s_mTc, n, 1)
                    for k in range(KD):
                        last = nc.tensor.matmul(pX[:, 0:D], mixedT[:, k, :], wo[:, k, :], start=(k == 0), stop=(k == KD - 1))
                    last.then_inc(s_F, 1)
            chunks(eng, NCH, mid, lambda i, p: ln.tensor(eng, i, p), tail)


def top2_experts(K):
    with ExitStack() as c:
        xnT_all = K.sb(c, "t2_xnT_all", [P, KD, TOK])
        weight = K.sb(c, "t2_weight", [P, NT, K.io["t2_router"].shape[1]])
        _route_top2(K, xnT_all, weight)
        _dense_experts(K, xnT_all, weight)


def _route_top2(K, xnT_all, weight):
    nc, io = K.nc, K.io
    NE = weight.shape[2]
    with ExitStack() as c:
        ln = LayerNormFront(K, c, "r2")
        sb = lambda n, s, d=F32: K.sb(c, f"r2_{n}", s, d)
        sem = lambda n: K.sem(c, f"r2_{n}")
        router = sb("router", [P, KD, NE])
        router_b = sb("router_b", [P, NE])
        logit = sb("logit", [P, TC, NE])
        best = sb("best", [P, TC, 8])
        index = sb("index", [P, TC, 8], U32)
        index_f = sb("index_f", [P, TC, 2])
        behind = sb("behind", [P, TC])
        w2 = sb("w2", [P, TC, 2])
        total = sb("total", [P, TC])
        first = sb("first", [P, TC, NE])
        pS = K.ps(c, "r2_pS", [P, TC, NE])
        s_in, s_lg, s_v, s_e, s_copy, s_w = (sem(n) for n in ("in", "lg", "v", "e", "copy", "w"))
        N = 8 + TC
        block = c.enter_context(nc.Block())

        @block.sync
        def _(eng):
            eng.dma_start(router[:, :, :], io["t2_router"].rearrange("(k p) e -> p k e", p=P)).then_inc(s_in, 16)
            eng.dma_start(router_b[:, :], io["t2_router_b"].partition_broadcast(P)).then_inc(s_in, 16)

        @block.gpsimd
        def _(eng):
            def mid(i, p):
                after(eng, ln.s_xnT, i, KD)
                eng.sem_inc(K.held_pool)
                nc.gpsimd.tensor_copy(xnT_all[:, :, bass.ds(i * CH, CH)], ln.xnT[p][:, :, :]).then_inc(s_copy, 1)
            chunks(eng, NCH, nothing, lambda i, p: ln.gpsimd(eng, i, p), mid)

        @block.vector
        def _(eng):
            def mid(i, p):
                after(eng, s_lg, i, 1)
                ch = Chain(eng, s_v, i, N)
                ch.do(nc.vector.tensor_tensor(logit[:, :, :], pS[:, :, :],
                                              router_b[:, :].unsqueeze(1).to_broadcast([P, TC, NE]), ALU.add))
                eng.sem_inc(K.held_vector)
                for t in range(TC):
                    nc.vector.max(best[:, t, :], logit[:, t, :]).then_inc(s_v, 1)
                ch.n += TC
                after(eng, s_v, i, N, ch.n)
                eng.sem_inc(K.held_vector)
                for t in range(TC - 1):
                    nc.vector.max_index(index[:, t, :], best[:, t, :], logit[:, t, :])
                ch.do(nc.vector.max_index(index[:, TC - 1, :], best[:, TC - 1, :], logit[:, TC - 1, :]))
                ch.do(nc.vector.tensor_copy(index_f[:, :, :], index[:, :, 0:2]))
                ch.do(nc.vector.tensor_tensor(behind[:, :], best[:, :, 1], best[:, :, 0], ALU.subtract))
                after(eng, s_e, i, 1)
                ch.do(nc.vector.tensor_scalar(total[:, :], w2[:, :, 1], 1.0, None, ALU.add))
                ch.do(nc.vector.reciprocal(w2[:, :, 0], total[:, :]))
                ch.do(nc.vector.tensor_tensor(w2[:, :, 1], w2[:, :, 1], w2[:, :, 0], ALU.mult))
                for t in range(TC):
                    ins = nc.vector.tensor_scalar(first[:, t, :], K.iota8[:, :], index_f[:, t, 0:1], w2[:, t, 0:1],
                                                  ALU.is_equal, ALU.mult)
                    ins2 = nc.vector.tensor_scalar(weight[:, bass.ds(i * TC + t, 1), :].rearrange("p a e -> p (a e)"),
                                                   K.iota8[:, :], index_f[:, t, 1:2], w2[:, t, 1:2],
                                                   ALU.is_equal, ALU.mult)
                    if t == TC - 1:
                        ch.do(ins2)
                ins = nc.vector.tensor_tensor(weight[:, bass.ds(i * TC, TC), :], weight[:, bass.ds(i * TC, TC), :],
                                              first[:, :, :], ALU.add).then_inc(s_w, 1)
                ch.done()
            chunks(eng, NCH, mid, lambda i, p: ln.vector(eng, i, p), nothing)

        @block.scalar
        def _(eng):
            def mid(i, p):
                after(eng, s_v, i, N, TC + 4)
                nc.scalar.activation(w2[:, :, 1], behind[:, :], ACT.Exp).then_inc(s_e, 1)

            def front(i, p):
                free(eng, s_copy, i, 1)
                ln.scalar(eng, i, p, s_lg, 1)
            chunks(eng, NCH, mid, front, nothing)

        @block.tensor
        def _(eng):
            def mid(i, p):
                after(eng, ln.s_xnT, i, KD)
                if not isinstance(i, int) or i > 0:
                    after(eng, s_v, i - 1, N, 1)
                for t in range(TC):
                    for k in range(KD):
                        last = nc.tensor.matmul(pS[:, t, :], ln.xnT[p][:, k, t * P:(t + 1) * P], router[:, k, :],
                                                start=(k == 0), stop=(k == KD - 1))
                last.then_inc(s_lg, 1)
            eng.wait_ge(s_in, 32)
            chunks(eng, NCH, mid, lambda i, p: ln.tensor(eng, i, p), nothing)


def _dense_experts(K, xnT_all, weight):
    nc, io, R = K.nc, K.io, K.resid
    NE, _, HID = io["t2_wgT"].shape
    HT = HID // P
    GU, HB = 2, 4
    with ExitStack() as c:
        sb = lambda n, s, d=F32: K.sb(c, f"de_{n}", s, d)
        sem = lambda n: K.sem(c, f"de_{n}")
        wg = [sb(f"wg{q}", [P, KD, HID]) for q in range(2)]
        wu = [sb(f"wu{q}", [P, KD, HID]) for q in range(2)]
        wd = [sb(f"wd{q}", [P, HT, D]) for q in range(2)]
        silu = [sb(f"silu{q}", [P, CH]) for q in range(GU)]
        hT = [sb(f"hT{q}", [P, CH]) for q in range(HB)]
        pG = [K.ps(c, f"de_pG{q}", [P, CH]) for q in range(GU)]
        pU = [K.ps(c, f"de_pU{q}", [P, CH]) for q in range(GU)]
        pO = [K.ps(c, f"de_pO{q}", [P, TC, D]) for q in range(2)]
        s_w = [sem(f"w{q}") for q in range(2)]
        s_wfree, s_gu, s_silu, s_h, s_down, s_comb = (
            sem(n) for n in ("wfree", "gu", "silu", "h", "down", "comb"))
        block = c.enter_context(nc.Block())
        LOADS = 3

        def steps(eng, body, around=None):
            with eng.Fori(0, NE // 2) as pair:
                for q in range(2):
                    e = pair * 2 + q
                    if around:
                        around(e, q)
                    if body:
                        with eng.Fori(0, NCH // 2) as cc:
                            for o in range(2):
                                body((e * NCH) + cc * 2 + o, e, cc * 2 + o, q, o)

        @block.sync
        def _(eng):
            eng.sem_inc(s_wfree, 2)
            def load(e, q):
                eng.wait_ge(s_wfree, e + 1)
                for dst, name in ((wg[q], "t2_wgT"), (wu[q], "t2_wuT"), (wd[q], "t2_wdT")):
                    src = io[name][bass.ds(e, 1), :, :].rearrange("a (k p) n -> p (a k) n", p=P)
                    eng.dma_start(dst[:, :, :], src).then_inc(s_w[q], 16)
            steps(eng, None, load)

        @block.scalar
        def _(eng):
            def body(f, e, ch, q, o):
                for j in range(HT):
                    n = f * HT + j
                    eng.wait_ge(s_h, n + 1)
                    eng.wait_ge(s_gu, n + 1)
                    nc.scalar.activation(silu[j % GU][:, :], pG[j % GU][:, :], ACT.Silu).then_inc(s_silu, 1)
            steps(eng, body)

        @block.vector
        def _(eng):
            eng.sem_inc(s_h, GU)
            eng.sem_inc(s_comb, 2 * TC)
            def body(f, e, ch, q, o):
                for j in range(HT):
                    n = f * HT + j
                    eng.wait_ge(s_down, n + 1)
                    eng.wait_ge(s_silu, n + 1)
                    nc.vector.tensor_tensor(hT[j % HB][:, :], silu[j % GU][:, :], pU[j % GU][:, :], ALU.mult).then_inc(s_h, 1)
                eng.wait_ge(s_down, f * HT + HT + HB)
                for t in range(TC):
                    tile = ch * TC + t
                    row = R[:, bass.ds(tile, 1), :].rearrange("p a d -> p (a d)")
                    w = weight[:, bass.ds(tile, 1), bass.ds(e, 1)].rearrange("p a e -> p (a e)")
                    nc.vector.scalar_tensor_tensor(row, pO[o][:, t, :], w, row, ALU.mult, ALU.add).then_inc(s_comb, 1)
            steps(eng, body)

        @block.tensor
        def _(eng):
            eng.sem_inc(s_down, HB)
            def body(f, e, ch, q, o):
                def gate_up(j):
                    eng.wait_ge(s_h, f * HT + j + 1)
                    for w, out in ((wg[q], pG[j % GU]), (wu[q], pU[j % GU])):
                        for k in range(KD):
                            last = nc.tensor.matmul(out[:, :], w[:, k, j * P:(j + 1) * P],
                                                    xnT_all[:, k, bass.ds(ch * CH, CH)], start=(k == 0), stop=(k == KD - 1))
                    last.then_inc(s_gu, 1)

                def down(j):
                    eng.wait_ge(s_h, f * HT + j + 1 + GU)
                    if j == 0:
                        eng.wait_ge(s_comb, (f + 1) * TC)
                    for t in range(TC):
                        last = nc.tensor.matmul(pO[o][:, t, :], hT[j % HB][:, t * P:(t + 1) * P], wd[q][:, j, :],
                                                start=(j == 0 and t % 2 == 0), stop=(j == HT - 1), skip_group_check=True)
                    last.then_inc(s_down, 1)
                gate_up(0)
                for j in range(1, HT):
                    gate_up(j)
                    down(j - 1)
                down(HT - 1)
            with eng.Fori(0, NE // 2) as pair:
                for q in range(2):
                    e = pair * 2 + q
                    eng.wait_ge(s_w[q], (pair + 1) * (16 * LOADS))
                    eng.sem_inc(K.held_tensor)
                    with eng.Fori(0, NCH // 2) as cc:
                        for o in range(2):
                            body((e * NCH) + cc * 2 + o, e, cc * 2 + o, q, o)
                    eng.drain().then_inc(s_wfree, 1)


STAGES = [load_and_constants, mamba, context_glu, top1_experts, self_attention, cross_attention, top2_experts, store]


def decoder(nc, io, stages=None):
    with ExitStack() as ctx:
        K = Kernel(nc, ctx, io)
        for stage in stages or STAGES:
            stage(K)
            K.clear()


def layout(inputs):
    t = lambda n, *axes: np.ascontiguousarray(np.transpose(np.asarray(inputs[n]), axes))
    same = lambda n: np.ascontiguousarray(np.asarray(inputs[n]))
    return {
        "x": same("x"), "ctx": same("ctx_1024"), "ctxT": t("ctx_1024", 0, 2, 1),
        "t1_router": same("L0_ffn_router_w"), "t1_router_b": same("L0_ffn_router_b"),
        "t2_router": t("L1_ffn_wg", 1, 0), "t2_router_b": same("L1_ffn_bg"),
        "t2_wgT": t("L1_ffn_Wgate", 0, 2, 1), "t2_wuT": t("L1_ffn_Wup", 0, 2, 1), "t2_wdT": t("L1_ffn_Wdown", 0, 2, 1),
        "xa_wqT": t("L1_xattn_Wq", 1, 0), "xa_wkT": t("L1_xattn_Wk", 1, 0), "xa_wvT": t("L1_xattn_Wv", 1, 0),
        "xa_woT": t("L1_xattn_Wo", 1, 0), "xa_bq": same("L1_xattn_bq"), "xa_bk": same("L1_xattn_bk"),
        "xa_bv": same("L1_xattn_bv"), "xa_bo": same("L1_xattn_bo"),
        "sa_wqT": t("L1_attn_wq", 1, 0), "sa_wkT": t("L1_attn_wk", 1, 0), "sa_wvT": t("L1_attn_wv", 1, 0),
        "sa_woT": t("L1_attn_wo", 1, 0),
        "mb_w_in": same("L0_attn_W_in"), "mb_conv_w": same("L0_attn_conv_w"), "mb_conv_b": same("L0_attn_conv_b"),
        "mb_w_x": same("L0_attn_W_xproj"), "mb_wdt": same("L0_attn_W_dt"), "mb_b_dt": same("L0_attn_b_dt"),
        "mb_A_log": same("L0_attn_A_log"), "mb_D": same("L0_attn_D"), "mb_w_out": same("L0_attn_W_out"),
        "t1_w": same("L0_ffn_expert_w"), "t1_b": same("L0_ffn_expert_b"),
    }


def kernel(**inputs):
    import concourse.bacc as bacc
    from concourse.bass_utils import run_bass_kernel_spmd

    nc = bacc.Bacc("TRN2", target_bir_lowering=False, num_devices=1)
    arrays, io = {}, {}
    for name, a in layout(inputs).items():
        arrays[f"in_{name}"] = a
        io[name] = nc.dram_tensor(f"in_{name}", a.shape, mybir.dt.from_np(a.dtype), kind="ExternalInput").ap()
    io["out"] = nc.dram_tensor("out", (NB, SEQ, D), F32, kind="ExternalOutput").ap()
    decoder(nc, io)
    r = run_bass_kernel_spmd(nc, [arrays], core_ids=[0])
    return r.results[0]["out"]
```

```python
from contextlib import ExitStack

import concourse.bass as bass
from concourse import mybir
import numpy as np

F32 = mybir.dt.float32
F32R = mybir.dt.float32r
BF16 = mybir.dt.bfloat16
I32 = mybir.dt.int32
U32 = mybir.dt.uint32
ALU = mybir.AluOpType
ACT = mybir.ActivationFunctionType
AX = mybir.AxisListType

P = 128
NB, SEQ, D = 4, 1024, 256
TOK = NB * SEQ
NT = TOK // P
KD = D // P
CH = 512
TC = CH // P
NCH = TOK // CH
CPB = SEQ // CH
CTX = 77
EPS = 1e-5
TOP = 2
ST = 256
NST_TILES = TOP * TOK // ST + 8


def after(eng, sem, i, per, k=None):
    eng.wait_ge(sem, i * per + (per if k is None else k))


def free(eng, sem, i, per, back=2):
    if not isinstance(i, int) or i >= back:
        eng.wait_ge(sem, (i - back + 1) * per)


def n_positive(n):
    return not isinstance(n, int) or n > 0


def chunks(eng, n, mid, front, tail):
    front(0, 0)
    mid(0, 0)
    front(1, 1)
    tail(0, 0)
    with eng.Fori(1, n // 2) as j:
        mid(2 * j - 1, 1)
        front(2 * j, 0)
        tail(2 * j - 1, 1)
        mid(2 * j, 0)
        front(2 * j + 1, 1)
        tail(2 * j, 0)
    mid(n - 1, 1)
    tail(n - 1, 1)


def nothing(i, p):
    pass


class Kernel:

    def __init__(self, nc, ctx, io):
        self.nc, self.io, self.in_use = nc, io, []
        self.resid = self.sb(ctx, "resid", [P, NT, D])
        self.ident = self.sb(ctx, "ident", [P, P])
        self.iota8 = self.sb(ctx, "iota8", [P, 8])
        self.held_vector = ctx.enter_context(nc.semaphore("held_vector"))
        self.held_pool = ctx.enter_context(nc.semaphore("held_pool"))
        self.held_tensor = ctx.enter_context(nc.semaphore("held_tensor"))
        self.minus_half = self.sb(ctx, "minus_half", [P, TC])

    def sb(self, ctx, name, shape, dt=F32):
        return ctx.enter_context(self.nc.sbuf_tensor(name, shape, dt))

    def ps(self, ctx, name, shape, dt=F32):
        return ctx.enter_context(self.nc.psum_tensor(name, shape, dt))

    def sem(self, ctx, name):
        self.in_use.append(self.nc.alloc_semaphore(name=name))
        return self.in_use[-1]

    def clear(self):
        self.nc.clear_and_free_semaphores(self.in_use)
        self.nc.all_engine_barrier()
        self.in_use = []


class LayerNormFront:

    def __init__(self, K, ctx, tag, keep_rows=False):
        nc = K.nc
        self.K, self.nc = K, nc
        sb = lambda n, s, d=F32: K.sb(ctx, f"{tag}_{n}", s, d)
        self.stats = [sb(f"stats{p}", [P, TC, 6]) for p in range(2)]
        self.mv = [sb(f"mv{p}", [P, TC, 2]) for p in range(2)]
        self.veps = [sb(f"veps{p}", [P, TC]) for p in range(2)]
        self.rstd = [sb(f"rstd{p}", [P, TC]) for p in range(2)]
        self.xn = [sb(f"xn{p}", [P, TC, D]) for p in range(2)]
        self.xnT = [sb(f"xnT{p}", [P, KD, CH]) for p in range(2)]
        self.pT = [K.ps(ctx, f"{tag}_pT{k}", [P, CH]) for k in range(KD)]
        sem = lambda n: K.sem(ctx, f"{tag}_{n}")
        self.s_stats, self.s_mv, self.s_veps = sem("stats"), sem("mv"), sem("veps")
        self.s_rstd, self.s_xn, self.s_pT, self.s_xnT = sem("rstd"), sem("xn"), sem("pT"), sem("xnT")

    def vector(self, eng, i, p):
        self.statistics(eng, i, p)
        self.normalise(eng, i, p)

    def statistics(self, eng, i, p):
        nc, R = self.nc, self.K.resid
        for t in range(TC):
            nc.vector.bn_stats(self.stats[p][:, t, :], R[:, bass.ds(i * TC + t, 1), :].rearrange("p a d -> p (a d)")).then_inc(self.s_stats, 1)
        after(eng, self.s_stats, i, TC)
        eng.sem_inc(self.K.held_vector)
        for t in range(TC):
            nc.vector.bn_aggr(self.mv[p][:, t, :], self.stats[p][:, t, :]).then_inc(self.s_mv, 1)
        after(eng, self.s_mv, i, TC)
        nc.vector.tensor_scalar(self.veps[p][:, :], self.mv[p][:, :, 1], EPS, None, ALU.add).then_inc(self.s_veps, 1)

    def normalise(self, eng, i, p):
        nc, R = self.nc, self.K.resid
        after(eng, self.s_rstd, i, 1)
        free(eng, self.s_pT, i, KD)
        for t in range(TC):
            nc.vector.tensor_scalar(self.xn[p][:, t, :], R[:, bass.ds(i * TC + t, 1), :].rearrange("p a d -> p (a d)"),
                                    self.mv[p][:, t, 0:1], self.rstd[p][:, t:t + 1],
                                    ALU.subtract, ALU.mult).then_inc(self.s_xn, 1)

    def gpsimd(self, eng, i, p):
        after(eng, self.s_veps, i, 1)
        self.nc.gpsimd.tensor_tensor(self.rstd[p][:, :], self.veps[p][:, :], self.K.minus_half[:, :],
                                     ALU.pow).then_inc(self.s_rstd, 1)

    def tensor(self, eng, i, p):
        after(eng, self.s_xn, i, TC)
        for k in range(KD):
            free(eng, self.s_xnT, i, KD, back=1)
            for t in range(TC):
                last = self.nc.tensor.transpose(self.pT[k][:, t * P:(t + 1) * P],
                                                self.xn[p][:, t, k * P:(k + 1) * P], self.K.ident[:, :])
            last.then_inc(self.s_pT, 1)

    def scalar(self, eng, i, p, s_used=None, per_used=None):
        if s_used is not None:
            free(eng, s_used, i, per_used)
        for k in range(KD):
            after(eng, self.s_pT, i, KD, k + 1)
            self.nc.scalar.copy(self.xnT[p][:, k, :], self.pT[k][:, :]).then_inc(self.s_xnT, 1)


def rows(R, i):
    return R[:, bass.ds(i * TC, TC), :]


def load_and_constants(K):
    nc, io = K.nc, K.io
    with ExitStack() as c:
        s_x, s_c = K.sem(c, "ld_x"), K.sem(c, "ld_c")
        block = c.enter_context(nc.Block())

        @block.sync
        def _(eng):
            eng.dma_start(K.resid[:, :, :], io["x"].rearrange("b (t p) d -> p (b t) d", p=P)).then_inc(s_x, 16)
            eng.wait_ge(s_x, 16)

        @block.vector
        def _(eng):
            nc.vector.memset(K.minus_half[:, :], -0.5)
            nc.vector.memset(K.ident[:, :], 0.0).then_inc(s_c, 1)

        @block.gpsimd
        def _(eng):
            eng.wait_ge(s_c, 1)
            nc.gpsimd.affine_select(out=K.ident[:, :], in_=K.ident[:, :], compare_op=ALU.not_equal, fill=1.0,
                                    base=0, pattern=[[-1, P]], channel_multiplier=1)
            nc.gpsimd.iota(K.iota8[:, :], pattern=[[1, 8]], base=0, channel_multiplier=0,
                           allow_small_or_imprecise_dtypes=True)


def store(K):
    nc, io = K.nc, K.io
    with ExitStack() as c:
        s_out = K.sem(c, "st_out")
        block = c.enter_context(nc.Block())

        @block.sync
        def _(eng):
            eng.dma_start(io["out"].rearrange("b (t p) d -> p (b t) d", p=P), K.resid[:, :, :]).then_inc(s_out, 16)
            eng.wait_ge(s_out, 16)


def run_for(name, eng, ops):
    for op in ops:
        for who, fn in op:
            if who == name:
                fn(eng)


def interleave(main, other):
    out, done = [], 0
    for n, op in enumerate(main):
        out.append(op)
        upto = (n + 1) * len(other) // len(main)
        out += other[done:upto]
        done = upto
    return out


def mamba(K):
    nc, io, R = K.nc, K.io, K.resid
    DI = io["mb_D"].shape[0]
    ME = DI // P
    NST = io["mb_A_log"].shape[1]
    RANK = io["mb_wdt"].shape[0]
    NPROJ = RANK + 2 * NST
    TAPS = io["mb_conv_w"].shape[1]
    GN = 4
    NGR = NST // GN
    ITEMS = NGR * ME
    LO = 64
    with ExitStack() as c:
        ln = LayerNormFront(K, c, "ml")
        sb = lambda n, s, d=F32: K.sb(c, f"mb_{n}", s, d)
        sem = lambda n: K.sem(c, f"mb_s_{n}")
        w_in = sb("w_in_sb", [P, KD, 2 * DI])
        w_x = sb("w_x_sb", [P, ME, NPROJ])
        w_dt = sb("w_dt_sb", [RANK, DI])
        w_out = sb("w_out_sb", [P, ME, D])
        conv_w, conv_b = sb("conv_w_sb", [P, ME, TAPS]), sb("conv_b_sb", [P, ME])
        b_dt, skip = sb("b_dt_sb", [P, ME]), sb("skip", [P, ME])
        a_neg = sb("a_neg", [P, ME, NST])
        u = sb("u", [P, ME, TAPS - 1 + CH])
        xc = [sb(f"xc{q}", [P, ME, CH]) for q in range(2)]
        proj = sb("proj", [NPROJ, CH])
        proj_hl = sb("proj_hl", [LO + NPROJ, CH], F32R)
        pick = sb("pick", [LO + NPROJ, 2 * NST])
        spread = sb("spread", [LO + NPROJ, 2 * NST], F32R)
        rests = [sb(f"rest{q}", [P, CH]) for q in range(2)]
        dt = sb("dt", [P, ME, CH])
        dtx = sb("dtx", [P, ME, CH])
        b_rep = [sb(f"b_rep{q}", [P, GN, CH]) for q in range(2)]
        c_rep = [sb(f"c_rep{q}", [P, GN, CH]) for q in range(2)]
        decay = [sb(f"decay{q}", [P, GN, 1 + CH]) for q in range(2)]
        drive = [sb(f"drive{q}", [P, GN, 1 + CH]) for q in range(2)]
        hc = [sb(f"hc{q}", [P, GN, CH]) for q in range(2)]
        log1 = [sb(f"log1{q}", [P, CH]) for q in range(2)]
        carried = sb("carried", [P, ME, NST])
        mix = sb("mix", [P, CH])
        yz = sb("yz", [P, ME, CH])
        pA = [K.ps(c, f"mb_pA{q}", [P, CH]) for q in range(2)]
        pY = [K.ps(c, f"mb_pY{m}", [P, CH]) for m in range(ME)]
        (s_in, s_c, s_a, s_sel, s_A, s_Ac, s_car, s_cv, s_xc, s_phl, s_sp, s_dv, s_dt, s_dtx, s_dA, s_dB, s_scan, s_keep, s_hc, s_y,
         s_yd, s_yz, s_o, s_res) = (sem(n) for n in (
             "in", "c", "a", "sel", "A", "Ac", "car", "cv", "xc", "phl", "sp", "dv", "dt", "dtx", "dA", "dB", "scan", "keep",
             "hc", "y", "yd", "yz", "o", "res"))
        BC = 2 * GN
        bc = lambda g, lo, hi: [(f"BC{g}", k) for k in range(lo, hi)]
        ORDER = ([("DT", 2), ("DT", 3)] + bc(1, 0, BC) + bc(2, 0, 4) + [("XC'", 0)] + bc(2, 4, 6) + [("XC'", 1)]
                 + bc(2, 6, BC) + [("XC'", 2)] + bc(3, 0, 2) + [("XC'", 3)] + bc(3, 2, BC) + [("Z", m) for m in range(ME)]
                 + [("PROJ'", 0), ("DT'", 0), ("DT'", 1)] + bc("0'", 0, BC))
        USES = len(ORDER)
        W = {name: w for w, name in enumerate(ORDER)}
        assert NGR == 4
        window_bc = lambda i, g, k: (i, W[f"BC{g}", k]) if g else (i - 1, W["BC0'", k])

        def bc_done(i, g, n):
            return window_bc(i, g, n - 1)

        def used(eng, i, w):
            eng.wait_ge(s_Ac, (i + 1) * USES + w + 1)
        later = lambda i: not isinstance(i, int) or i > 0

        def use(i, p, w, matmuls, read):
            out = pA[((p + 1) * USES + w) % 2]

            def pe(eng):
                if not isinstance(i, int) or i >= 0 or w >= 2:
                    used(eng, i, w - 2)
                matmuls(eng, out).then_inc(s_A, 1)

            def act(eng):
                eng.wait_ge(s_A, (i + 1) * USES + w + 1)
                read(eng, out).then_inc(s_Ac, 1)
            return [("tensor", pe), ("scalar", act)]

        def skip_uses(i, w, n):
            def act(eng):
                if (i, w) != (-1, 0):
                    used(eng, i, w - 1)
                eng.sem_inc(s_Ac, n)

            def pe(eng):
                if (i, w) != (-1, 0):
                    used(eng, i, w - 1)
                eng.sem_inc(s_A, n)
            return [[("tensor", pe), ("scalar", act)]]

        def front(i, p):
            def act(eng):
                if not isinstance(i, int) or i >= 2:
                    used(eng, i - 2, W["Z", ME - 1])
                ln.scalar(eng, i, p)
            def pe(eng):
                if not isinstance(i, int) or i >= 2:
                    eng.wait_ge(s_res, (i - 1) * TC)
                ln.tensor(eng, i, p)
            return ([("vector", lambda eng: ln.statistics(eng, i, p))], [("gpsimd", lambda eng: ln.gpsimd(eng, i, p))],
                    [("vector", lambda eng: ln.normalise(eng, i, p))], [("tensor", pe), ("scalar", act)])

        def in_projection(i, p, window, w, col, read):
            def matmuls(eng, out):
                if w == W["XC'", 0]:
                    after(eng, ln.s_xnT, i, KD)
                for k in range(KD):
                    last = nc.tensor.matmul(out[:, :], w_in[:, k, col:col + P], ln.xnT[p][:, k, :],
                                            start=(k == 0), stop=(k == KD - 1))
                return last
            return use(*window, w, matmuls, read)

        def project_in(i, p):
            ops = []

            def carry(eng):
                if later(i):
                    eng.wait_ge(s_cv, i * ME * TAPS)
                    eng.sem_inc(K.held_pool)
                if p == 0:
                    ins = nc.gpsimd.memset(u[:, :, 0:TAPS - 1], 0.0)
                else:
                    ins = nc.gpsimd.tensor_copy(u[:, :, 0:TAPS - 1], u[:, :, CH:CH + TAPS - 1])
                ins.then_inc(s_car, 1)
            ops.append([("gpsimd", carry)])
            for m in range(ME):
                def read(eng, out, m=m):
                    if m == 0:
                        after(eng, s_car, i, 1)
                    return nc.scalar.copy(u[:, m, TAPS - 1:], out[:, :])
                ops.append(in_projection(i, p, (i - 1, 1 - p), W["XC'", m], m * P, read))
            return ops

        def convolve(i, p):
            ops, silus = [], []
            for m in range(ME):
                def conv(eng, m=m):
                    after(eng, s_car, i, 1)
                    used(eng, i - 1, W["XC'", m])
                    a = xc[p][:, m, :]
                    if m == 0 and (not isinstance(i, int) or i >= 2):
                        eng.wait_ge(s_yd, (i - 1) * ME)
                    nc.vector.tensor_scalar(a, u[:, m, 0:CH], conv_w[:, m, 0:1], None, ALU.mult).then_inc(s_cv, 1)
                    for j in range(1, TAPS):
                        after(eng, s_cv, i, ME * TAPS, m * TAPS + j)
                        nc.vector.scalar_tensor_tensor(a, u[:, m, j:j + CH], conv_w[:, m, j:j + 1], a,
                                                       ALU.mult, ALU.add).then_inc(s_cv, 1)

                def silu(eng, m=m):
                    after(eng, s_cv, i, ME * TAPS, (m + 1) * TAPS)
                    nc.scalar.activation(xc[p][:, m, :], xc[p][:, m, :], ACT.Silu, bias=conv_b[:, m:m + 1]).then_inc(s_xc, 1)
                ops.append([("vector", conv)])
                silus.append([("scalar", silu)])
            return ops, silus

        def project(i, p):
            def matmuls(eng, out):
                for m in range(ME):
                    after(eng, s_xc, i, ME, m + 1)
                    last = nc.tensor.matmul(out[0:NPROJ, :], w_x[:, m, :], xc[p][:, m, :], start=(m == 0), stop=(m == ME - 1))
                return last

            def parts(eng):
                used(eng, i - 1, W["PROJ'", 0])
                nc.vector.tensor_copy(proj_hl[0:NPROJ, :], proj[:, :]).then_inc(s_phl, 1)
                after(eng, s_phl, i, 2, 1)
                nc.vector.tensor_tensor(proj_hl[LO:LO + NPROJ, :], proj[:, :], proj_hl[0:NPROJ, :].bitcast(F32),
                                        ALU.subtract).then_inc(s_phl, 1)
            return [use(i - 1, 1 - p, W["PROJ'", 0], matmuls, lambda eng, out: nc.scalar.copy(proj[:, :], out[0:NPROJ, :])), [("vector", parts)]]

        def step_sizes(i, p):
            sizes, logs, products = [], [], []
            nth = lambda m, k: 3 * (m - m % 2) + 2 * k + m % 2 + 1

            def logarithms(*tiles):
                def act(eng):
                    for m in tiles:
                        after(eng, s_sp, i, 3 * ME, nth(m, 0))
                        nc.scalar.activation(dtx[:, m, :], dtx[:, m, :], ACT.Exp, scale=-1.0).then_inc(s_sp, 1)
                    for m in tiles:
                        after(eng, s_sp, i, 3 * ME, nth(m, 1))
                        if m >= 2 or later(i):
                            eng.wait_ge(s_dt, i * ME + m - 1)
                        nc.scalar.activation(log1[m % 2][:, :], dtx[:, m, :], ACT.Ln, bias=1.0).then_inc(s_sp, 1)
                return act

            for m in range(ME):
                def matmuls(eng, out, m=m):
                    if m == 0:
                        used(eng, i - 1, W["PROJ'", 0])
                    return nc.tensor.matmul(out[:, :], w_dt[:, m * P:(m + 1) * P], proj[0:RANK, :], start=True, stop=True)

                def read(eng, out, m=m):
                    if later(i):
                        last_of_m = i * ITEMS - ME + m + 1
                        eng.wait_ge(s_dB, 2 * last_of_m)
                        eng.wait_ge(s_dA, last_of_m)
                    nc.scalar.activation(dtx[:, m, :], out[:, :], ACT.Abs, bias=b_dt[:, m:m + 1]).then_inc(s_sp, 1)
                    return nc.scalar.activation(dt[:, m, :], out[:, :], ACT.Relu, bias=b_dt[:, m:m + 1])

                def dve(eng, m=m):
                    ch = Chain(eng, s_dv, i, 3 * ME)
                    ch.n = 3 * m
                    rest = rests[m % 2]
                    after(eng, s_sp, i, 3 * ME, nth(m, 1))
                    if m >= 2 or later(i):
                        eng.wait_ge(s_dt, i * ME + m - 1)
                    ch.do(nc.vector.tensor_scalar(rest[:, :], dtx[:, m, :], 1.0, 1.0, ALU.add, ALU.subtract))
                    ch.do(nc.vector.tensor_tensor(rest[:, :], dtx[:, m, :], rest[:, :], ALU.subtract))
                    after(eng, s_sp, i, 3 * ME, nth(m, 2))
                    ch.do(nc.vector.tensor_tensor(rest[:, :], log1[m % 2][:, :], rest[:, :], ALU.add))
                    nc.vector.tensor_tensor(dt[:, m, :], dt[:, m, :], rest[:, :], ALU.add).then_inc(s_dt, 1)

                def pool(eng, m=m):
                    after(eng, s_dt, i, ME, m + 1)
                    nc.gpsimd.tensor_tensor(dtx[:, m, :], dt[:, m, :], xc[p][:, m, :], ALU.mult).then_inc(s_dtx, 1)
                window = (i - 1, 1 - p, W["DT'", m]) if m < 2 else (i, p, W["DT", m])
                sizes.append(use(*window, matmuls, read))
                logs.append([("vector", dve)])
                products.append([("gpsimd", pool)])
            return sizes[:2] + [[("scalar", logarithms(0, 1))]] + logs[:2], sizes[2:] + [[("scalar", logarithms(2, 3))]] + logs[2:], products

        def broadcast(i, p, g):
            ops = []
            for half, rep in ((0, b_rep), (1, c_rep)):
                for n in range(GN):
                    row = half * NST + g * GN + n

                    def matmuls(eng, out, row=row):
                        if g == 0 and row == 0:
                            after(eng, s_phl, i, 2)
                        return nc.tensor.matmul(out[:, :], spread[:, row:row + 1].to_broadcast([LO + NPROJ, P]), proj_hl[:, :], start=True, stop=True)

                    def read(eng, out, rep=rep, n=n, half=half):
                        if n == 0 and half == 0 and (g >= 2 or later(i)):
                            eng.wait_ge(s_hc, i * ITEMS + ME * (g - 1))
                        return nc.scalar.copy(rep[g % 2][:, n, :], out[:, :])
                    w_i, w = window_bc(i, g, half * GN + n)
                    ops.append(use(w_i, p if g else 1 - p, w, matmuls, read))
            return ops

        def item(i, p, g, m):
            s = g * ME + m
            q = s % 2

            def act(eng):
                if s >= 2 or later(i):
                    eng.wait_ge(s_scan, i * ITEMS + s - 1)
                after(eng, s_dt, i, ME, m + 1)
                for n in range(GN):
                    last = nc.scalar.activation(decay[q][:, n, 1:], dt[:, m, :], ACT.Exp,
                                                scale=a_neg[:, m, g * GN + n:g * GN + n + 1])
                last.then_inc(s_dA, 1)

            def pool(eng):
                if s >= 2 or later(i):
                    eng.wait_ge(s_hc, i * ITEMS + s - 1)
                after(eng, s_dtx, i, ME, m + 1)
                used(eng, *bc_done(i, g, GN))
                nc.gpsimd.tensor_tensor(drive[q][:, :, 1:], dtx[:, m, :].unsqueeze(1).to_broadcast([P, GN, CH]),
                                        b_rep[g % 2][:, :, :], ALU.mult).then_inc(s_dB, 1)
                if p == 0:
                    ins = nc.gpsimd.memset(drive[q][:, :, 0], 0.0)
                else:
                    ins = nc.gpsimd.tensor_copy(drive[q][:, :, 0], carried[:, m, g * GN:(g + 1) * GN])
                ins.then_inc(s_dB, 1)

            def dve(eng):
                after(eng, s_dA, i, ITEMS, s + 1)
                after(eng, s_dB, i, 2 * ITEMS, 2 * s + 2)
                long = lambda T: T[q][:, :, :].rearrange("p n t -> p (n t)")
                nc.vector.tensor_tensor_scan(long(drive), long(decay), long(drive), 0.0, ALU.mult, ALU.add).then_inc(s_scan, 1)
                after(eng, s_scan, i, ITEMS, s + 1)
                if p == 0:
                    nc.vector.tensor_copy(carried[:, m, g * GN:(g + 1) * GN], drive[q][:, :, CH]).then_inc(s_keep, 1)
                used(eng, *bc_done(i, g, BC))
                if s >= 2 or later(i):
                    eng.wait_ge(s_y, i * ITEMS + s - 1)
                nc.vector.tensor_tensor(hc[q][:, :, :], drive[q][:, :, 1:], c_rep[g % 2][:, :, :], ALU.mult).then_inc(s_hc, 1)
            return [("scalar", act), ("gpsimd", pool), ("vector", dve)]

        def state_sum(i, p, g, m):
            s = g * ME + m

            def pe(eng):
                if g == 0 and later(i):
                    eng.wait_ge(s_yd, (i - 1) * ME + m + 1)
                after(eng, s_hc, i, ITEMS, s + 1)
                for n in range(GN):
                    last = nc.tensor.matmul(pY[m][:, :], K.ident[:, :], hc[s % 2][:, n, :], start=(g == 0 and n == 0),
                                            stop=(g == NGR - 1 and n == GN - 1))
                last.then_inc(s_y, 1)
            return [[("tensor", pe)]]

        def gates(i, p):
            ops = []
            for m in range(ME):
                def read(eng, out, m=m):
                    if m == 0 and later(i):
                        eng.wait_ge(s_o, i * TC)
                    return nc.scalar.activation(yz[:, m, :], out[:, :], ACT.Silu)
                ops.append(in_projection(i, p, (i, p), W["Z", m], DI + m * P, read))
            return ops

        def finish(i, p):
            ops = []
            for m in range(ME):
                def dve(eng, m=m):
                    after(eng, s_y, i, ITEMS, ITEMS - ME + m + 1)
                    if m > 0 or later(i):
                        eng.wait_ge(s_yz, i * ME + m)
                    nc.vector.scalar_tensor_tensor(mix[:, :], xc[p][:, m, :], skip[:, m:m + 1], pY[m][:, :],
                                                   ALU.mult, ALU.add).then_inc(s_yd, 1)
                    after(eng, s_yd, i, ME, m + 1)
                    used(eng, i, W["Z", m])
                    nc.vector.tensor_tensor(yz[:, m, :], yz[:, m, :], mix[:, :], ALU.mult).then_inc(s_yz, 1)
                ops.append([("vector", dve)])
            return ops

        def project_out(i, p, fronts):
            out = lambda t: ln.pT[t // 2][:, t % 2 * D:(t % 2 + 1) * D]
            matmuls, adds = [], []
            for t in range(TC):
                def pe(eng, t=t):
                    if t == 0:
                        after(eng, s_yz, i, ME)
                        eng.wait_ge(ln.s_xnT, fronts * KD)
                    for m in range(ME):
                        last = nc.tensor.matmul(out(t), yz[:, m, t * P:(t + 1) * P], w_out[:, m, :],
                                                start=(m == 0), stop=(m == ME - 1))
                    if t % 2:
                        last.then_inc(s_o, 2)

                def dve(eng, t=t):
                    after(eng, s_o, i, TC, (t // 2 + 1) * 2)
                    row = R[:, bass.ds(i * TC + t, 1), :].rearrange("p a d -> p (a d)")
                    nc.vector.tensor_tensor(row, row, out(t), ALU.add).then_inc(s_res, 1)
                matmuls.append([("tensor", pe)])
                adds.append([("vector", dve)])
            return matmuls, adds

        def window(i, p, before=True, following=True):
            n, pn = i + 1, 1 - p
            group = [None] + [broadcast(i, p, g) for g in range(1, NGR)]
            z = gates(i, p)
            done = finish(i, p)
            slots = [[] for _ in range(ITEMS)]
            for g in range(1, NGR):
                for k in range(BC):
                    slots[ME * (g - 1) + k // 2].append(group[g][k])
            if before:
                late = finish(i - 1, pn)[2:]
                matmuls, adds = project_out(i - 1, pn, i + 1)
            _, sizes23, products = step_sizes(i, p)
            slots[0] = sizes23 + slots[0] + (late if before else [])
            slots[1] = slots[1] + products[2:]
            if before:
                slots[2] += matmuls[:1]
                slots[3] += matmuls[1:3] + adds[:2]
                slots[4] = matmuls[3:] + slots[4] + adds[2:]
            if following:
                stats, power, normal, transposes = front(n, pn)
                carried_in, *xs = project_in(n, pn)
                convs, silus = convolve(n, pn)
                sizes01, _, products = step_sizes(n, pn)
                slots[0].append(stats)
                slots[1].append(power)
                slots[2].append(normal)
                slots[4].append(carried_in)
                slots[5] = [transposes] + slots[5]
                for m in range(ME):
                    slots[5 + m].append(xs[m])
                    slots[7 + m].append(convs[m])
                slots[12] += z + silus
                slots[13] += project(n, pn)
                slots[14] += sizes01 + broadcast(n, pn, 0)[:GN]
                slots[15] += products[:2] + broadcast(n, pn, 0)[GN:] + done[:2]
            else:
                for m in range(ME):
                    slots[5 + m] += skip_uses(i, W["XC'", m], 1)
                slots[12] += z
                slots[15] += done[:2]
            ops, waiting = [], []
            for s in range(ITEMS):
                g, m = s // ME, s % ME
                ops += [item(i, p, g, m)] + slots[s] + waiting
                waiting = state_sum(i, p, g, m)
            return ops + waiting

        def emit(name, eng):
            stats, power, normal, transposes = front(0, 0)
            carried_in, *xs = project_in(0, 0)
            convs, silus = convolve(0, 0)
            sizes01, _, products = step_sizes(0, 0)
            skip = lambda w, upto: skip_uses(-1, w, W[upto] - w)
            start, at = [stats, power, normal, transposes, carried_in], 0
            for m in range(ME):
                start += skip(at, ("XC'", m)) + [xs[m]]
                at = W["XC'", m] + 1
            start += (convs + silus + skip(at, ("PROJ'", 0)) + project(0, 0) + sizes01 + broadcast(0, 0, 0) + products[:2])
            run_for(name, eng, start + window(0, 0, before=False) + window(1, 1))
            with eng.Fori(1, NB - 1) as b:
                run_for(name, eng, window(2 * b, 0) + window(2 * b + 1, 1))
            run_for(name, eng, window(NCH - 2, 0) + window(NCH - 1, 1, following=False))
            matmuls, adds = project_out(NCH - 1, 1, NCH)
            run_for(name, eng, finish(NCH - 1, 1)[2:] + matmuls + adds)

        block = c.enter_context(nc.Block())
        assert ME == TC and TAPS <= CH

        @block.sync
        def _(eng):
            loads = [(w_in[:, :, :], io["mb_w_in"].rearrange("(k p) n -> p k n", p=P)),
                     (w_x[:, :, :], io["mb_w_x"].rearrange("(m p) n -> p m n", p=P)),
                     (w_dt[:, :], io["mb_wdt"]),
                     (w_out[:, :, :], io["mb_w_out"].rearrange("(m p) n -> p m n", p=P)),
                     (a_neg[:, :, :], io["mb_A_log"].rearrange("(m p) n -> p m n", p=P)),
                     (conv_w[:, :, :], io["mb_conv_w"].rearrange("(m p) j -> p m j", p=P))]
            for dst, name in ((conv_b, "mb_conv_b"), (b_dt, "mb_b_dt"), (skip, "mb_D")):
                loads.append((dst[:, :], io[name].rearrange("(m p) -> p m", p=P)))
            with nc.allow_non_contiguous_dma(reason="a few numbers to a partition"):
                for dst, src in loads:
                    eng.dma_start(dst, src).then_inc(s_in, 16)
        ALL_IN = 16 * 9

        @block.gpsimd
        def _(eng):
            eng.wait_ge(s_c, 1)
            for n, lo in enumerate((0, LO)):
                nc.gpsimd.affine_select(out=pick[:, :], in_=pick[:, :], compare_op=ALU.not_equal, fill=1.0,
                                        base=-(lo + RANK), pattern=[[-1, 2 * NST]], channel_multiplier=1).then_inc(s_sel, 1)
                eng.wait_ge(s_sel, n + 1)
            emit("gpsimd", eng)

        @block.vector
        def _(eng):
            nc.vector.memset(pick[:, :], 0.0)
            for q in range(2):
                nc.vector.memset(decay[q][:, :, 0], 0.0)
            nc.vector.memset(rests[0][:, :], 0.0)
            eng.drain().then_inc(s_c, 1)
            eng.wait_ge(s_c, 1)
            nc.vector.tensor_copy(proj_hl[:, :], rests[0][0:LO + NPROJ, :]).then_inc(s_a, 1)
            eng.wait_ge(s_in, ALL_IN)
            eng.wait_ge(s_sel, 2)
            nc.vector.tensor_copy(spread[:, :], pick[:, :]).then_inc(s_a, 1)
            eng.wait_ge(s_c, 2)
            nc.vector.tensor_scalar(a_neg[:, :, :], a_neg[:, :, :], -1.0, None, ALU.mult).then_inc(s_a, 1)
            eng.wait_ge(s_a, 3)
            emit("vector", eng)

        @block.scalar
        def _(eng):
            eng.wait_ge(s_in, ALL_IN)
            eng.wait_ge(s_c, 1)
            nc.scalar.activation(a_neg[:, :, :], a_neg[:, :, :], ACT.Exp).then_inc(s_c, 1)
            eng.wait_ge(s_a, 3)
            emit("scalar", eng)

        @block.tensor
        def _(eng):
            eng.wait_ge(s_in, ALL_IN)
            eng.wait_ge(s_a, 3)
            emit("tensor", eng)


def context_glu(K):
    nc, io, R = K.nc, K.io, K.resid
    with ExitStack() as c:
        ln = LayerNormFront(K, c, "cg")
        sb = lambda n, s, d=F32: K.sb(c, f"cg_{n}", s, d)
        sem = lambda n: K.sem(c, f"cg_{n}")
        ctxT = sb("ctxT", [P, NB, KD, CTX])
        ctx_rows = sb("ctx_rows", [CTX, NB, D])
        ctxT_now = [sb(f"ctxT_now{p}", [P, KD, CTX]) for p in range(2)]
        gelu_h = [sb(f"gelu_h{p}", [CTX, CH]) for p in range(2)]
        gT = [sb(f"gT{p}", [CTX, CH]) for p in range(2)]
        pH = [K.ps(c, f"cg_pH{p}", [CTX, CH]) for p in range(2)]
        pO = K.ps(c, "cg_pO", [P, TC, D])
        s_in, s_now, s_h, s_gelu, s_g, s_o, s_res = (
            sem(n) for n in ("in", "now", "h", "gelu", "g", "o", "res"))
        block = c.enter_context(nc.Block())

        @block.sync
        def _(eng):
            eng.dma_start(ctxT[:, :, :, :], io["ctxT"].rearrange("b (k p) s -> p b k s", p=P)).then_inc(s_in, 16)
            eng.dma_start(ctx_rows[:, :, :], io["ctx"].rearrange("b s d -> s b d")).then_inc(s_in, 16)

        @block.gpsimd
        def _(eng):
            def front(i, p):
                ln.gpsimd(eng, i, p)
                free(eng, s_h, i, 1)
                b = i // CPB
                nc.gpsimd.tensor_copy(ctxT_now[p][:, :, :], ctxT[:, bass.ds(b, 1), :, :].rearrange("p a k s -> p (a k) s")
                                      ).then_inc(s_now, 1)
            eng.wait_ge(s_in, 32)
            chunks(eng, NCH, nothing, front, nothing)

        @block.vector
        def _(eng):
            def tail(i, p):
                after(eng, s_gelu, i, 1)
                free(eng, s_o, i, 1)
                nc.vector.tensor_tensor(gT[p][:, :], gelu_h[p][:, :], pH[p][:, :], ALU.mult).then_inc(s_g, 1)
                after(eng, s_o, i, 1)
                nc.vector.tensor_tensor(rows(R, i), rows(R, i), pO[:, :, :], ALU.add).then_inc(s_res, 1)
            chunks(eng, NCH, nothing, lambda i, p: ln.vector(eng, i, p), tail)

        @block.scalar
        def _(eng):
            def mid(i, p):
                after(eng, s_h, i, 1)
                free(eng, s_g, i, 1)
                nc.scalar.activation(gelu_h[p][:, :], pH[p][:, :], ACT.Gelu).then_inc(s_gelu, 1)
            chunks(eng, NCH, mid, lambda i, p: ln.scalar(eng, i, p, s_h, 1), nothing)

        @block.tensor
        def _(eng):
            def mid(i, p):
                after(eng, ln.s_xnT, i, KD)
                after(eng, s_now, i, 1)
                free(eng, s_g, i, 1)
                for k in range(KD):
                    last = nc.tensor.matmul(pH[p][:, :], ctxT_now[p][:, k, :], ln.xnT[p][:, k, :],
                                            start=(k == 0), stop=(k == KD - 1))
                last.then_inc(s_h, 1)

            def tail(i, p):
                after(eng, s_g, i, 1)
                free(eng, s_res, i, 1, back=1)
                for t in range(TC):
                    last = nc.tensor.matmul(pO[:, t, :], gT[p][:, t * P:(t + 1) * P],
                                            ctx_rows[:, bass.ds(i // CPB, 1), :].rearrange("s a d -> s (a d)"),
                                            start=True, stop=True)
                last.then_inc(s_o, 1)
            eng.wait_ge(s_in, 32)
            chunks(eng, NCH, mid, lambda i, p: ln.tensor(eng, i, p), tail)


class Chain:

    def __init__(self, eng, sem, i, size):
        self.eng, self.sem, self.i, self.size, self.n = eng, sem, i, size, 0

    def do(self, ins):
        self.n += 1
        ins.then_inc(self.sem, 1)
        after(self.eng, self.sem, self.i, self.size or 0, self.n)

    def done(self):
        assert self.n == self.size


def top1_experts(K):
    nc, io, R = K.nc, K.io, K.resid
    NE = io["t1_w"].shape[0]
    HALF = NE // 2
    with ExitStack() as c:
        ln = LayerNormFront(K, c, "t1")
        sb = lambda n, s, d=F32: K.sb(c, f"t1_{n}", s, d)
        sem = lambda n: K.sem(c, f"t1_{n}")
        router = sb("router", [P, KD, NE])
        router_b = sb("router_b", [P, NE])
        w = sb("w", [P, KD, NE, D])
        b = sb("b", [NE, D])
        logit = sb("logit", [P, TC, NE])
        top = sb("top", [P, TC])
        shifted = sb("shifted", [P, TC, NE])
        e = sb("e", [P, TC, NE])
        total = sb("total", [P, TC])
        gate = sb("gate", [P, TC])
        best = sb("best", [P, TC, 8])
        index = sb("index", [P, TC, 8], U32)
        index_f = sb("index_f", [P, TC])
        send = [sb(f"send{p}", [P, TC, NE]) for p in range(2)]
        sendT = [sb(f"sendT{p}", [NE, CH]) for p in range(2)]
        pY = [K.ps(c, f"t1_pY{h}", [P, HALF, D]) for h in range(2)]
        pB = K.ps(c, "t1_pB", [P, D])
        pS = K.ps(c, "t1_pS", [P, CH])
        logits_ps = pS[:, 0:TC * NE].rearrange("p (t e) -> p t e", e=NE)
        bias_ps = pB[:, :]
        s_in, s_lg, s_v, s_e, s_send, s_sT, s_sTc, s_b, s_badd, s_y, s_comb, s_acc = (
            sem(n) for n in ("in", "lg", "v", "e", "send", "sT", "sTc", "b", "badd", "y", "comb", "acc"))
        block = c.enter_context(nc.Block())
        G = 2 * TC

        @block.sync
        def _(eng):
            eng.dma_start(router[:, :, :], io["t1_router"].rearrange("(k p) e -> p k e", p=P)).then_inc(s_in, 16)
            eng.dma_start(router_b[:, :], io["t1_router_b"].partition_broadcast(P)).then_inc(s_in, 16)
            eng.dma_start(b[:, :], io["t1_b"]).then_inc(s_in, 16)
            for k in range(KD):
                eng.dma_start(w[:, k, :, :], io["t1_w"][:, k * P:(k + 1) * P, :].rearrange("e p d -> p e d")).then_inc(s_in, 16)

        @block.gpsimd
        def _(eng):
            chunks(eng, NCH, nothing, lambda i, p: ln.gpsimd(eng, i, p), nothing)

        @block.vector
        def _(eng):
            def mid(i, p):
                after(eng, s_lg, i, 1)
                ch = Chain(eng, s_v, i, 8)
                ch.do(nc.vector.tensor_tensor(logit[:, :, :], logits_ps,
                                              router_b[:, :].unsqueeze(1).to_broadcast([P, TC, NE]), ALU.add))
                ch.do(nc.vector.tensor_reduce(top[:, :], logit[:, :, :], axis=AX.X, op=ALU.max))
                ch.do(nc.vector.tensor_tensor(shifted[:, :, :], logit[:, :, :],
                                              top[:, :].unsqueeze(2).to_broadcast([P, TC, NE]), ALU.subtract))
                after(eng, s_e, i, 1)
                ch.do(nc.vector.tensor_reduce(total[:, :], e[:, :, :], axis=AX.X, op=ALU.add))
                ch.do(nc.vector.reciprocal(gate[:, :], total[:, :]))
                eng.sem_inc(K.held_vector)
                for t in range(TC):
                    last = nc.vector.max(best[:, t, :], e[:, t, :])
                ch.do(last)
                eng.sem_inc(K.held_vector)
                for t in range(TC):
                    last = nc.vector.max_index(index[:, t, :], best[:, t, :], e[:, t, :])
                ch.do(last)
                ch.do(nc.vector.tensor_copy(index_f[:, :], index[:, :, 0]))
                free(eng, s_sT, i, 1)
                for t in range(TC):
                    nc.vector.tensor_scalar(send[p][:, t, :], K.iota8[:, :], index_f[:, t:t + 1], gate[:, t:t + 1],
                                            ALU.is_equal, ALU.mult).then_inc(s_send, 1)
                ch.done()

            def tail(i, p):
                after(eng, s_send, i, TC)
                for t in range(TC):
                    row = R[:, bass.ds(i * TC + t, 1), :].rearrange("p a d -> p (a d)")
                    after(eng, s_b, i, TC, t + 1)
                    nc.vector.tensor_tensor(row, row, bias_ps, ALU.add).then_inc(s_badd, 1)
                    after(eng, s_badd, i, TC, t + 1)
                    for h in range(2):
                        after(eng, s_y, i, G, 2 * t + h + 1)
                        for j in range(HALF):
                            ins = nc.vector.scalar_tensor_tensor(row, pY[h][:, j, :], send[p][:, t, h * HALF + j:h * HALF + j + 1],
                                                                 row, ALU.mult, ALU.add)
                            if j < HALF - 1:
                                ins.then_inc(s_acc, 1)
                                after(eng, s_acc, i, G * (HALF - 1), (2 * t + h) * (HALF - 1) + j + 1)
                        ins.then_inc(s_comb, 1)
                        after(eng, s_comb, i, G, 2 * t + h + 1)
            chunks(eng, NCH, mid, lambda i, p: ln.vector(eng, i, p), tail)

        @block.scalar
        def _(eng):
            def mid(i, p):
                after(eng, s_v, i, 8, 3)
                nc.scalar.activation(e[:, :, :], shifted[:, :, :], ACT.Exp).then_inc(s_e, 1)

            def tail(i, p):
                after(eng, s_sT, i, 1)
                free(eng, s_b, i, TC)
                nc.scalar.copy(sendT[p][:, :], pS[0:NE, :]).then_inc(s_sTc, 1)
            chunks(eng, NCH, mid, lambda i, p: ln.scalar(eng, i, p, s_y, G), tail)

        @block.tensor
        def _(eng):
            def mid(i, p):
                after(eng, ln.s_xnT, i, KD)
                free(eng, s_sTc, i, 1, back=1)
                for t in range(TC):
                    for k in range(KD):
                        last = nc.tensor.matmul(logits_ps[:, t, :], ln.xnT[p][:, k, t * P:(t + 1) * P], router[:, k, :],
                                                start=(k == 0), stop=(k == KD - 1))
                last.then_inc(s_lg, 1)

            def tail(i, p):
                def group(t, h):
                    n = 2 * t + h
                    if n >= 2 or not isinstance(i, int) or i > 0:
                        eng.wait_ge(s_comb, i * G + n - 1)
                    for k in range(KD):
                        for q in range(HALF // 2):
                            last = nc.tensor.matmul(pY[h][:, 2 * q:2 * q + 2, :], ln.xnT[p][:, k, t * P:(t + 1) * P],
                                                    w[:, k, h * HALF + 2 * q:h * HALF + 2 * q + 2, :],
                                                    start=(k == 0), stop=(k == KD - 1))
                    last.then_inc(s_y, 1)
                group(0, 0)
                group(0, 1)
                after(eng, s_send, i, TC)
                for t in range(TC):
                    last = nc.tensor.transpose(pS[0:NE, t * P:(t + 1) * P], send[p][:, t, :], K.ident[:, :])
                last.then_inc(s_sT, 1)
                after(eng, s_sTc, i, 1)
                for t in range(TC):
                    if t > 0:
                        group(t, 0)
                    if t > 0 or not isinstance(i, int) or i > 0:
                        eng.wait_ge(s_badd, i * TC + t)
                    nc.tensor.matmul(bias_ps, sendT[p][:, t * P:(t + 1) * P], b[:, :], start=True, stop=True).then_inc(s_b, 1)
                    if t > 0:
                        group(t, 1)
            eng.wait_ge(s_in, 16 * (3 + KD))
            chunks(eng, NCH, mid, lambda i, p: ln.tensor(eng, i, p), tail)



def self_attention(K):
    with ExitStack() as c:
        q_rows, k_rows = (K.sb(c, f"sa_{n}_rows", [P, NT, D]) for n in ("q", "k"))
        v_dram = K.nc.dram_tensor("sa_v_dram", [TOK, D], F32).ap()
        _project_qkv(K, q_rows, k_rows, v_dram)
        _attend(K, q_rows, k_rows, v_dram)


def _project_qkv(K, q_rows, k_rows, v_dram):
    nc, io = K.nc, K.io
    with ExitStack() as c:
        ln = LayerNormFront(K, c, "qk")
        sb = lambda n, s, d=F32: K.sb(c, f"qk_{n}", s, d)
        sem = lambda n: K.sem(c, f"qk_{n}")
        w = sb("w", [P, KD, 3, D])
        v_rows = [sb(f"v_rows{p}", [P, TC, D]) for p in range(2)]
        pQK = [K.ps(c, f"qk_pQK{q}", [P, 2, D]) for q in range(2)]
        pV = [K.ps(c, f"qk_pV{q}", [P, D]) for q in range(2)]
        s_in, s_mm, s_q, s_v = (sem(n) for n in ("in", "mm", "q", "v"))
        s_out = [sem(f"out{p}") for p in range(2)]
        block = c.enter_context(nc.Block())

        @block.sync
        def _(eng):
            for n, name in enumerate(("sa_wqT", "sa_wkT", "sa_wvT")):
                eng.dma_start(w[:, :, n, :], io[name].rearrange("(k p) n -> p k n", p=P)).then_inc(s_in, 16)

            def tail(i, p):
                after(eng, s_v, i, TC)
                eng.dma_start(v_dram[bass.ds(i * CH, CH), :].rearrange("(t p) d -> p t d", p=P), v_rows[p][:, :, :]
                              ).then_inc(s_out[p], 16)
            chunks(eng, NCH, nothing, nothing, tail)
            for p in range(2):
                eng.wait_ge(s_out[p], 16 * (NCH // 2))

        @block.gpsimd
        def _(eng):
            chunks(eng, NCH, nothing, lambda i, p: ln.gpsimd(eng, i, p), nothing)

        @block.vector
        def _(eng):
            def tail(i, p):
                for t in range(TC):
                    after(eng, s_mm, i, TC, t + 1)
                    nc.vector.tensor_scalar(q_rows[:, bass.ds(i * TC + t, 1), :].rearrange("p a d -> p (a d)"),
                                            pQK[t % 2][:, 0, :], 0.25, None, ALU.mult).then_inc(s_q, 1)
                    nc.vector.tensor_copy(k_rows[:, bass.ds(i * TC + t, 1), :].rearrange("p a d -> p (a d)"),
                                          pQK[t % 2][:, 1, :]).then_inc(s_q, 1)
            chunks(eng, NCH, nothing, lambda i, p: ln.vector(eng, i, p), tail)

        @block.scalar
        def _(eng):
            def tail(i, p):
                if not isinstance(i, int) or i >= 2:
                    eng.wait_ge(s_out[p], (i // 2) * 16)
                for t in range(TC):
                    after(eng, s_mm, i, TC, t + 1)
                    nc.scalar.copy(v_rows[p][:, t, :], pV[t % 2][:, :]).then_inc(s_v, 1)
            chunks(eng, NCH, nothing, lambda i, p: ln.scalar(eng, i, p, s_mm, TC), tail)

        @block.tensor
        def _(eng):
            def tail(i, p):
                after(eng, ln.s_xnT, i, KD)
                for t in range(TC):
                    n = i * TC + t
                    if t >= 2 or n_positive(i):
                        eng.wait_ge(s_q, 2 * n - 2)
                        eng.wait_ge(s_v, n - 1)
                    for k in range(KD):
                        nc.tensor.matmul(pQK[t % 2][:, :, :], ln.xnT[p][:, k, t * P:(t + 1) * P], w[:, k, 0:2, :],
                                         start=(k == 0), stop=(k == KD - 1))
                    for k in range(KD):
                        last = nc.tensor.matmul(pV[t % 2][:, :], ln.xnT[p][:, k, t * P:(t + 1) * P], w[:, k, 2, :],
                                                start=(k == 0), stop=(k == KD - 1))
                    last.then_inc(s_mm, 1)
            eng.wait_ge(s_in, 48)
            chunks(eng, NCH, nothing, lambda i, p: ln.tensor(eng, i, p), tail)


def _attend(K, q_rows, k_rows, v_dram):
    nc, io, R = K.nc, K.io, K.resid
    HD = 16
    C16 = D // HD
    NPOS = P // 2 * C16
    QB = NPOS // P
    PARTS = 4 * HD
    NEG = -3e38
    HALF = NPOS // 2
    with ExitStack() as c:
        sb = lambda n, s, d=F32: K.sb(c, f"at_{n}", s, d)
        sem = lambda n: K.sem(c, f"at_{n}")
        wo = sb("wo", [P, KD, D])
        ident_bf = sb("ident_bf", [P, P], BF16)
        mask_q = sb("mask_q", [P, P], BF16)
        mask_k = sb("mask_k", [P, P], BF16)
        zero_bf = sb("zero_bf", [P, 32], BF16)
        pick = sb("pick", [P, 2, HD + 1])
        q_hl = [sb(f"q_hl{p}", [P, C16, 2, 2, HD], F32R) for p in range(2)]
        k_hl = [sb(f"k_hl{p}", [P, C16, 2, 2, HD], F32R) for p in range(2)]
        qT = [sb(f"qT{p}", [PARTS + 2, 2, NPOS], F32R) for p in range(2)]
        kT = [sb(f"kT{p}", [PARTS + 2, 2, NPOS], F32R) for p in range(2)]
        ones = sb("ones", [P, 2 * NPOS])
        nm = sb("nm", [P, 2, QB])
        nm_hl = sb("nm_hl", [P, 2, 2, QB], F32R)
        nmT = [sb(f"nmT{p}", [4 * QB, P], F32R) for p in range(2)]
        v = [sb(f"v{p}", [P, 2, QB, 32]) for p in range(2)]
        e = [sb(f"e{g}", [P, 2, 512]) for g in range(3)]
        o_sb = sb("o_sb", [P, 2, HALF])
        inv = sb("inv", [P, C16])
        wei = sb("wei", [P, D])
        weiT = sb("weiT", [P, KD, P])
        pF = [K.ps(c, f"at_pF{q}", [P, 512]) for q in range(2)]
        pS = K.ps(c, "at_pS", [P, 2, 512])
        pE = K.ps(c, "at_pE", [P, 2, 512])
        pO = [K.ps(c, f"at_pO{q}", [P, 512]) for q in range(2)]
        (s_in, s_c, s_c2, s_hl, s_tq, s_tk, s_qT, s_kT, s_sc, s_max, s_nm, s_nmT, s_nmc, s_st, s_ex, s_pv, s_ob0, s_ob1,
         s_bk, s_inv, s_wei, s_wT, s_wTc, s_f, s_res) = (sem(n) for n in (
             "in", "c", "c2", "hl", "tq", "tk", "qTs", "kTs", "sc", "max", "nms", "nmTs", "nmc", "st", "ex", "pv", "ob0", "ob1",
             "bk", "invs", "weis", "wT", "wTc", "f", "res"))
        s_row = [sem(f"row{p}") for p in range(2)]
        s_v = [sem(f"v{p}s") for p in range(2)]
        flat = lambda a: a.rearrange("p a d -> p (a d)")

        S_ITEMS = [((0, 1), qb) for qb in range(QB // 2)] + [((a,), qb) for qb in range(QB // 2, QB) for a in range(2)]
        NS = len(S_ITEMS)
        width = lambda hf, kb: min(HALF, HALF * (hf + 1) - kb * P)
        SLOTS = [[(1, 0)], [(1, 1)], [(1, 2)], [(1, 3)], [(0, 0)], [(0, 1), (0, 3)], [(1, 4)], [(1, 5), (1, 7)], [(0, 2), (1, 6)]]
        NG = len(SLOTS)
        assert all(sum(width(*x) for x in s) == 512 for s in SLOTS)
        LAST = {(hf, kb % 2): (hf, kb) for s in SLOTS for hf, kb in s}
        FIRST = {}
        for s in SLOTS:
            for hf, kb in s:
                FIRST.setdefault((hf, kb % 2), (hf, kb))

        def front(i, p):
            ops = []

            def split(eng):
                if not isinstance(i, int) or i >= 2:
                    eng.wait_ge(s_tq, 4 * i - 4)
                    eng.wait_ge(s_tk, 4 * i - 4)
                both_of = lambda rows_: flat(rows_[:, bass.ds(i, 1), :]).rearrange("p (c d) -> p c d", d=HD
                                                                                    ).unsqueeze(2).to_broadcast([P, C16, 2, HD])
                q_part = lambda x: q_hl[p][:, :, :, x, :]
                k_part = lambda x: k_hl[p][:, :, x, :, :]
                nc.gpsimd.tensor_copy(q_part(0), both_of(q_rows)).then_inc(s_hl, 1)
                nc.gpsimd.tensor_copy(k_part(0), both_of(k_rows)).then_inc(s_hl, 1)
                after(eng, s_hl, i, 4, 1)
                eng.sem_inc(K.held_pool)
                nc.gpsimd.tensor_tensor(q_part(1), both_of(q_rows), q_part(0).bitcast(F32), ALU.subtract).then_inc(s_hl, 1)
                after(eng, s_hl, i, 4, 2)
                eng.sem_inc(K.held_pool)
                nc.gpsimd.tensor_tensor(k_part(1), both_of(k_rows), k_part(0).bitcast(F32), ALU.subtract).then_inc(s_hl, 1)
            ops.append([("gpsimd", split)])

            def load_v(eng):
                if not isinstance(i, int) or i >= 2:
                    eng.wait_ge(s_pv, NG * (i - 1))
                for a in range(2):
                    src = v_dram[bass.ds(i * P + a * (P // 2), P // 2), :].rearrange("(kb r) (c d) -> (r c) kb d", r=P // C16, d=HD)
                    eng.dma_start(v[p][:, a, :, 0:HD], src).then_inc(s_v[p], 16)
            ops.append([("sync", load_v)])

            def group(g):
                def pe(eng):
                    if g == 0:
                        after(eng, s_hl, i, 4)
                        if n_positive(i):
                            eng.wait_ge(s_nmc, i)
                    if g or n_positive(i):
                        eng.wait_ge(s_qT, i * 4 + g)
                        eng.wait_ge(s_kT, i * 4 + g)
                        eng.sem_inc(K.held_tensor)
                    for cc in range(4):
                        col = q_hl[p][:, 4 * g + cc, :, :, :].rearrange("p x y d -> p (x y d)").bitcast(F32)
                        last = nc.tensor.transpose(pF[0][0:PARTS, cc * P:(cc + 1) * P], col, K.ident[:, :])
                    last.then_inc(s_tq, 1)
                    for cc in range(4):
                        col = k_hl[p][:, 4 * g + cc, :, :, :].rearrange("p x y d -> p (x y d)").bitcast(F32)
                        last = nc.tensor.transpose(pF[1][0:PARTS, cc * P:(cc + 1) * P], col, K.ident[:, :])
                    last.then_inc(s_tk, 1)

                def out(T):
                    return T[0:PARTS, :, :].rearrange("x a (r c) -> x c a r", c=C16)[:, 4 * g:4 * g + 4, :, :]

                def act(eng):
                    if g == 0 and (not isinstance(i, int) or i >= 2):
                        eng.wait_ge(s_pv, NG * (i - 1))
                    after(eng, s_tq, i, 4, g + 1)
                    nc.scalar.copy(out(qT[p]), pF[0][0:PARTS, :].rearrange("x (c a r) -> x c a r", c=4, a=2)).then_inc(s_qT, 1)

                def dve(eng):
                    if g == 0 and (not isinstance(i, int) or i >= 2):
                        eng.wait_ge(s_pv, NG * (i - 1))
                    after(eng, s_tk, i, 4, g + 1)
                    nc.vector.tensor_copy(out(kT[p]), pF[1][0:PARTS, :].rearrange("x (c a r) -> x c a r", c=4, a=2)).then_inc(s_kT, 1)
                ops.append([("tensor", pe), ("scalar", act), ("vector", dve)])
            for g in range(4):
                group(g)

            def item(s):
                heads, qb = S_ITEMS[s]
                w = (qb + 1) * P

                def pe(eng):
                    if s == 0:
                        after(eng, s_qT, i, 4)
                        after(eng, s_kT, i, 4)
                    if s or n_positive(i):
                        eng.wait_ge(s_max, i * NS + s)
                    for a in heads:
                        for w0 in range(0, w, 512):
                            w1 = min(w, w0 + 512)
                            bank = a if len(heads) == 2 else w0 // 512
                            nc.tensor.matmul(pS[:, bank, 0:w1 - w0], qT[p][0:PARTS, a, qb * P:(qb + 1) * P],
                                             kT[p][0:PARTS, a, w0:w1], start=True, stop=(w1 < w))
                        last = nc.tensor.matmul(pS[:, bank, w1 - w0 - P:w1 - w0], ident_bf[:, :], mask_q[:, :],
                                                start=False, stop=True)
                    last.then_inc(s_sc, 1)

                def dve(eng):
                    after(eng, s_sc, i, NS, s + 1)
                    if len(heads) == 2:
                        src, dst = pS[:, :, 0:w], nm[:, :, qb]
                    else:
                        src, dst = pS[:, :, :].rearrange("p b n -> p (b n)")[:, 0:w], nm[:, heads[0], qb:qb + 1]
                    nc.vector.tensor_reduce(dst, src, axis=AX.X, op=ALU.max, negate=True).then_inc(s_max, 1)
                ops.append([("tensor", pe), ("vector", dve)])
            for s in range(NS):
                item(s)

            def parts_of_max(eng):
                after(eng, s_max, i, NS)
                if n_positive(i):
                    eng.wait_ge(s_nmT, i)
                nc.vector.tensor_copy(nm_hl[:, 0, :, :], nm[:, :, :]).then_inc(s_nm, 1)
                after(eng, s_nm, i, 2, 1)
                nc.vector.tensor_tensor(nm_hl[:, 1, :, :], nm[:, :, :], nm_hl[:, 0, :, :].bitcast(F32), ALU.subtract).then_inc(s_nm, 1)

            def pe_max(eng):
                after(eng, s_nm, i, 2)
                nc.tensor.transpose(pF[0][0:4 * QB, 0:P], nm_hl[:, :, :, :].rearrange("p x a b -> p (x a b)").bitcast(F32), K.ident[:, :]).then_inc(s_nmT, 1)

            def act_max(eng):
                if not isinstance(i, int) or i >= 2:
                    eng.wait_ge(s_row[p], (i // 2) * 32)
                after(eng, s_nmT, i, 1)
                nc.scalar.copy(nmT[p][:, :], pF[0][0:4 * QB, 0:P]).then_inc(s_nmc, 1)

            def move_max(eng):
                after(eng, s_nmc, i, 1)
                for part in range(2):
                    eng.dma_start(qT[p][PARTS + part:PARTS + part + 1, :, :].bitcast(F32).rearrange("o a (b q) -> o (a b) q", q=P),
                                  nmT[p][part * 2 * QB:(part + 1) * 2 * QB, :].bitcast(F32)).then_inc(s_row[p], 16)
            ops.append([("vector", parts_of_max), ("tensor", pe_max), ("scalar", act_max), ("sync", move_max)])
            return ops

        def tail(i, p):
            ops = []

            def scores(g):
                def pe(eng):
                    if g == 0:
                        eng.wait_ge(s_row[p], (i // 2) * 32 + 32)
                    if g or n_positive(i):
                        eng.wait_ge(s_ex, i * NG + g)
                    for a in range(2):
                        at = 0
                        for n, (hf, kb) in enumerate(SLOTS[g]):
                            w = width(hf, kb)
                            diag = kb * P >= hf * HALF
                            q0 = HALF * (hf + 1) - w
                            last = nc.tensor.matmul(pE[:, a, at:at + w], kT[p][:, a, kb * P:(kb + 1) * P],
                                                    qT[p][:, a, q0:q0 + w], start=(n == 0), stop=not diag, skip_group_check=True)
                            if diag:
                                last = nc.tensor.matmul(pE[:, a, at:at + P], ident_bf[:, :], mask_k[:, :],
                                                        start=False, stop=True, skip_group_check=True)
                            at += w
                    last.then_inc(s_st, 1)

                def act(eng):
                    after(eng, s_st, i, NG, g + 1)
                    if g >= 3 or n_positive(i):
                        eng.wait_ge(s_pv, i * NG + g - 2)
                    nc.scalar.activation(e[g % 3][:, :, :], pE[:, :, :], ACT.Exp).then_inc(s_ex, 1)
                return [("tensor", pe), ("scalar", act)]

            def product(g):
                def pe(eng):
                    if g == 0:
                        eng.wait_ge(s_v[p], (i // 2) * 32 + 32)
                        if n_positive(i):
                            eng.wait_ge(s_res, i)
                    after(eng, s_ex, i, NG, g + 1)
                    at = 0
                    for hf, kb in SLOTS[g]:
                        w = width(hf, kb)
                        for a in range(2):
                            j = 2 * a + kb % 2
                            first, final = FIRST[hf, kb % 2] == (hf, kb), LAST[hf, kb % 2] == (hf, kb)
                            last = nc.tensor.matmul(pO[hf][32 * j:32 * j + 32, HALF - w:HALF], v[p][:, a, kb, :],
                                                    e[g % 3][:, a, at:at + w], start=first, stop=final, skip_group_check=True)
                            if first and w < HALF:
                                last = nc.tensor.matmul(pO[hf][32 * j:32 * j + 32, 0:HALF - w], zero_bf[:, :],
                                                        ident_bf[:, 0:HALF - w], start=False, stop=True, skip_group_check=True)
                        at += w
                    last.then_inc(s_pv, 1)
                return [("tensor", pe)]
            ops.append(scores(0))
            for g in range(1, NG):
                ops.append(scores(g))
                ops.append(product(g - 1))
            ops.append(product(NG - 1))

            def act_o(eng):
                after(eng, s_pv, i, NG)
                if n_positive(i):
                    eng.wait_ge(s_bk, i)
                nc.scalar.copy(o_sb[:, 0, :], pO[0][:, :]).then_inc(s_ob0, 1)

            def dve_o(eng):
                after(eng, s_pv, i, NG)
                if n_positive(i):
                    eng.wait_ge(s_bk, i)
                nc.vector.tensor_copy(o_sb[:, 1, :], pO[1][:, :]).then_inc(s_ob1, 1)

            def pe_back(eng):
                after(eng, s_ob0, i, 1)
                after(eng, s_ob1, i, 1)
                for cc in range(C16):
                    col = o_sb[:, :, :].rearrange("x f (r c) -> x c (f r)", c=C16)[:, cc, :]
                    for a in range(2):
                        last = nc.tensor.matmul(pO[0][64 * a:64 * a + 64, cc * (HD + 1):(cc + 1) * (HD + 1)], col, pick[:, a, :],
                                                start=True, stop=True)
                last.then_inc(s_bk, 1)

            def dve_wei(eng):
                back = pO[0][:, 0:C16 * (HD + 1)].rearrange("p (c d) -> p c d", d=HD + 1)
                after(eng, s_bk, i, 1)
                nc.vector.reciprocal(inv[:, :], back[:, :, HD]).then_inc(s_inv, 1)
                after(eng, s_inv, i, 1)
                if n_positive(i):
                    eng.wait_ge(s_wT, i)
                nc.vector.tensor_tensor(wei[:, :].rearrange("p (c d) -> p c d", d=HD), back[:, :, 0:HD],
                                        inv[:, :].unsqueeze(2).to_broadcast([P, C16, HD]), ALU.mult).then_inc(s_wei, 1)

            def pe_wT(eng):
                after(eng, s_wei, i, 1)
                for k in range(KD):
                    last = nc.tensor.transpose(pO[1][:, k * P:(k + 1) * P], wei[:, k * P:(k + 1) * P], K.ident[:, :])
                last.then_inc(s_wT, 1)

            def act_wT(eng):
                after(eng, s_wT, i, 1)
                if n_positive(i):
                    eng.wait_ge(s_f, i)
                nc.scalar.copy(weiT[:, :, :], pO[1][:, 0:D].rearrange("p (k q) -> p k q", k=KD)).then_inc(s_wTc, 1)

            def pe_f(eng):
                after(eng, s_wTc, i, 1)
                for k in range(KD):
                    last = nc.tensor.matmul(pO[0][:, 0:D], weiT[:, k, :], wo[:, k, :], start=(k == 0), stop=(k == KD - 1))
                last.then_inc(s_f, 1)

            def dve_res(eng):
                after(eng, s_f, i, 1)
                row = flat(R[:, bass.ds(i, 1), :])
                nc.vector.tensor_tensor(row, row, pO[0][:, 0:D], ALU.add).then_inc(s_res, 1)
            ops.append([("scalar", act_o), ("vector", dve_o), ("tensor", pe_back)])
            ops.append([("vector", dve_wei), ("tensor", pe_wT)])
            ops.append([("scalar", act_wT), ("tensor", pe_f)])
            ops.append([("vector", dve_res)])
            return ops

        def both(tail_ops, front_ops):
            out, done = [], 0
            for n, op in enumerate(tail_ops):
                out.append(op)
                upto = (n + 1) * len(front_ops) // len(tail_ops)
                out += front_ops[done:upto]
                done = upto
            return out + front_ops[done:]

        def emit(name, eng):
            def run(ops):
                for op in ops:
                    for who, fn in op:
                        if who == name:
                            fn(eng)
            run(front(0, 0))
            run(both(tail(0, 0), front(1, 1)))
            with eng.Fori(1, NT // 2) as j:
                run(both(tail(2 * j - 1, 1), front(2 * j, 0)))
                run(both(tail(2 * j, 0), front(2 * j + 1, 1)))
            run(tail(NT - 1, 1))

        block = c.enter_context(nc.Block())

        @block.sync
        def _(eng):
            eng.dma_start(wo[:, :, :], io["sa_woT"].rearrange("(k p) n -> p k n", p=P)).then_inc(s_in, 16)
            eng.wait_ge(s_c2, 1)
            emit("sync", eng)

        @block.gpsimd
        def _(eng):
            eng.wait_ge(s_c, 1)
            for mask, step, mult in ((mask_q, -1, 1), (mask_k, 1, -1)):
                nc.gpsimd.affine_select(out=mask[:, :], in_=mask[:, :], compare_op=ALU.is_ge, fill=NEG,
                                        base=0, pattern=[[step, P]], channel_multiplier=mult)
            nc.gpsimd.tensor_copy(ident_bf[:, :], K.ident[:, :])
            for par in range(2):
                nc.gpsimd.affine_select(out=pick[:, :, :], in_=pick[:, :, :], compare_op=ALU.not_equal, fill=1.0,
                                        base=-32 * par, pattern=[[-64, 2], [-1, HD + 1]], channel_multiplier=1).then_inc(s_c2, 1)
                eng.wait_ge(s_c2, 1 + par)
            emit("gpsimd", eng)

        @block.vector
        def _(eng):
            nc.vector.memset(mask_q[:, :], 0.0)
            nc.vector.memset(mask_k[:, :], 0.0)
            nc.vector.memset(zero_bf[:, :], 0.0)
            nc.vector.memset(pick[:, :, :], 0.0)
            nc.vector.memset(ones[:, :], 1.0)
            for p in range(2):
                nc.vector.memset(v[p][:, :, :, HD:HD + 1], 1.0)
                nc.vector.memset(v[p][:, :, :, HD + 1:32], 0.0)
            eng.drain().then_inc(s_c, 1)
            eng.wait_ge(s_c, 1)
            for p in range(2):
                last = nc.vector.tensor_copy(kT[p][PARTS:PARTS + 2, :, :],
                                             ones[PARTS:PARTS + 2, :].rearrange("x (a l) -> x a l", a=2)).then_inc(s_c, 1)
            emit("vector", eng)

        @block.scalar
        def _(eng):
            emit("scalar", eng)

        @block.tensor
        def _(eng):
            eng.wait_ge(s_in, 16)
            eng.wait_ge(s_c, 3)
            eng.wait_ge(s_c2, 2)
            emit("tensor", eng)


def cross_attention(K):
    nc, io, R = K.nc, K.io, K.resid
    HD = 16
    NH = D // HD
    HM = P // HD
    HG = HM // 2
    SCALE = float(HD) ** -0.5
    with ExitStack() as c:
        ln = LayerNormFront(K, c, "xa")
        sb = lambda n, s, d=F32: K.sb(c, f"xa_{n}", s, d)
        sem = lambda n: K.sem(c, f"xa_{n}")
        ctxT = sb("ctxT", [P, KD, NB, CTX])
        wq, wk, wv, wo = (sb(n, [P, KD, D]) for n in ("wq", "wk", "wv", "wo"))
        bq, bk = sb("bq", [P, KD]), sb("bk", [P, KD])
        bv, bo = sb("bv", [P, D]), sb("bo", [P, D])
        own = sb("own", [P, HM])
        kT = sb("kT", [P, KD, NB, CTX])
        kdiag = [sb(f"kdiag{m}", [P, NB, HM, CTX]) for m in range(KD)]
        v = sb("v", [CTX, NB, D])
        qT = [sb(f"qT{p}", [P, KD, CH]) for p in range(2)]
        top = [sb(f"top{m}", [P, HM]) for m in range(KD)]
        e = [sb(f"e{m}", [P, HM, CTX]) for m in range(KD)]
        total = sb("total", [P, NH])
        inv = sb("inv", [P, NH])
        eT = [sb(f"eT{q}", [CTX, 4, P]) for q in range(2)]
        mixed = sb("mixed", [P, D])
        mixedT = sb("mixedT", [P, KD, P])
        pS = [K.ps(c, f"xa_pS{m}", [P, 2, 512]) for m in range(KD)]
        pX = K.ps(c, "xa_pX", [P, 512])
        pV = K.ps(c, "xa_pV", [P, D])
        (s_in, s_own, s_kT, s_kTc, s_kd, s_vp, s_vc, s_q, s_qc, s_S, s_sub, s_v, s_exp, s_eT, s_eTc, s_pv, s_mix, s_mT,
         s_mTc, s_F, s_res, s_bo) = (sem(n) for n in (
             "in", "own", "kTp", "kTc", "kd", "vp", "vc", "q", "qc", "S", "sub", "v", "exp", "eTp", "eTc", "pv", "mix",
             "mT", "mTc", "F", "res", "bosum"))
        LOADS = 9
        block = c.enter_context(nc.Block())

        def tiles(fn):
            def tail(i, p):
                for t in range(TC):
                    fn(i, p, t, i * TC + t)
            return tail

        @block.sync
        def _(eng):
            for k in range(KD):
                eng.dma_start(ctxT[:, k, :, :], io["ctxT"][:, k * P:(k + 1) * P, :].rearrange("b p s -> p b s")).then_inc(s_in, 16)
            for dst, name in ((wq, "xa_wqT"), (wk, "xa_wkT"), (wv, "xa_wvT"), (wo, "xa_woT")):
                eng.dma_start(dst[:, :, :], io[name].rearrange("(k p) n -> p k n", p=P)).then_inc(s_in, 16)
            with nc.allow_non_contiguous_dma(reason="256 biases, one to a partition"):
                eng.dma_start(bq[:, :], io["xa_bq"].rearrange("(k p) -> p k", p=P)).then_inc(s_in, 16)
                eng.dma_start(bk[:, :], io["xa_bk"].rearrange("(k p) -> p k", p=P)).then_inc(s_in, 16)
            eng.dma_start(bv[:, :], io["xa_bv"].partition_broadcast(P)).then_inc(s_in, 16)
            eng.dma_start(bo[:, :], io["xa_bo"].partition_broadcast(P)).then_inc(s_in, 16)
        ALL_IN = 16 * (KD + 8)

        @block.gpsimd
        def _(eng):
            nc.gpsimd.memset(own[:, :], 1.0).then_inc(s_own, 1)
            eng.wait_ge(s_own, 1)
            nc.gpsimd.affine_select(out=own[:, :], in_=own[:, :], compare_op=ALU.is_ge, fill=0.0, base=0,
                                    pattern=[[-HD, HM]], channel_multiplier=1).then_inc(s_own, 1)
            eng.wait_ge(s_own, 2)
            nc.gpsimd.affine_select(out=own[:, :], in_=own[:, :], compare_op=ALU.is_ge, fill=0.0, base=HD - 1,
                                    pattern=[[HD, HM]], channel_multiplier=-1).then_inc(s_own, 1)

            def tail(i, p, t, n):
                after(eng, s_res, n, 1)
                row = R[:, bass.ds(n, 1), :].rearrange("p a d -> p (a d)")
                nc.gpsimd.tensor_tensor(row, row, bo[:, :], ALU.add).then_inc(s_bo, 1)
            eng.wait_ge(s_in, ALL_IN)
            chunks(eng, NCH, nothing, lambda i, p: ln.gpsimd(eng, i, p), tiles(tail))

        @block.vector
        def _(eng):
            eng.wait_ge(s_in, ALL_IN)
            eng.wait_ge(s_own, 3)
            for m in range(KD):
                eng.wait_ge(s_kTc, m + 1)
                for h in range(HM):
                    ins = nc.vector.tensor_scalar(kdiag[m][:, :, h, :], kT[:, m, :, :], own[:, h:h + 1], None, ALU.mult)
                ins.then_inc(s_kd, 1)
            for b in range(NB):
                eng.wait_ge(s_vp, b + 1)
                nc.vector.tensor_tensor(v[:, b, :], pV[0:CTX, :], bv[0:CTX, :], ALU.add).then_inc(s_vc, 1)

            def tail(i, p, t, n):
                for m in range(KD):
                    after(eng, s_S, n, KD, m + 1)
                    scores = pS[m][:, :, 0:HG * CTX].rearrange("p g (h s) -> p g h s", s=CTX)
                    nc.vector.tensor_reduce(top[m][:, :].rearrange("p (g h) -> p g h", g=2), scores, axis=AX.X, op=ALU.max
                                            ).then_inc(s_v, 1)
                    after(eng, s_v, n, KD + 2, m + 1)
                    if n_positive(n):
                        eng.wait_ge(s_eT, n * 4)
                    nc.vector.tensor_tensor(e[m][:, :, :].rearrange("p (g h) s -> p g h s", g=2), scores,
                                            top[m][:, :].rearrange("p (g h) -> p g h", g=2).unsqueeze(3).to_broadcast([P, 2, HG, CTX]),
                                            ALU.subtract).then_inc(s_sub, 1)
                for m in range(KD):
                    after(eng, s_exp, n, KD, m + 1)
                    ins = nc.vector.tensor_reduce(total[:, m * HM:(m + 1) * HM], e[m][:, :, :], axis=AX.X, op=ALU.add)
                ins.then_inc(s_v, 1)
                after(eng, s_v, n, KD + 2, KD + 1)
                nc.vector.reciprocal(inv[:, :], total[:, :]).then_inc(s_v, 1)
                after(eng, s_v, n, KD + 2)
                after(eng, s_pv, n, 4)
                if n_positive(n):
                    eng.wait_ge(s_mT, n)
                nc.vector.tensor_tensor(mixed[:, :].rearrange("p (h d) -> p h d", d=HD),
                                        pV[:, :].rearrange("p (h d) -> p h d", d=HD),
                                        inv[:, :].unsqueeze(2).to_broadcast([P, NH, HD]), ALU.mult).then_inc(s_mix, 1)
                after(eng, s_F, n, 1)
                row = R[:, bass.ds(n, 1), :].rearrange("p a d -> p (a d)")
                nc.vector.tensor_tensor(row, row, pX[:, 0:D], ALU.add).then_inc(s_res, 1)
            chunks(eng, NCH, nothing, lambda i, p: ln.vector(eng, i, p), tiles(tail))

        @block.scalar
        def _(eng):
            eng.wait_ge(s_in, ALL_IN)
            for m in range(KD):
                eng.wait_ge(s_kT, m + 1)
                nc.scalar.activation(kT[:, m, :, :], pX[:, 0:NB * CTX].rearrange("p (b s) -> p b s", s=CTX),
                                     ACT.Identity, bias=bk[:, m:m + 1]).then_inc(s_kTc, 1)

            def mid(i, p):
                for m in range(KD):
                    after(eng, s_q, i, KD, m + 1)
                    if m == 0:
                        free(eng, s_S, i, KD * TC)
                    nc.scalar.activation(qT[p][:, m, :], pS[m][:, 0, :], ACT.Identity, bias=bq[:, m:m + 1]).then_inc(s_qc, 1)

            def tail(i, p, t, n):
                for m in range(KD):
                    after(eng, s_sub, n, KD, m + 1)
                    nc.scalar.activation(e[m][:, :, :], e[m][:, :, :], ACT.Exp, scale=SCALE).then_inc(s_exp, 1)
                for g in range(4):
                    after(eng, s_eT, n, 4, g + 1)
                    if n_positive(n) or g >= 2:
                        eng.wait_ge(s_pv, n * 4 + g - 1)
                    nc.scalar.copy(eT[g % 2][:, :, :], pX[0:CTX, :].rearrange("s (h q) -> s h q", q=P)).then_inc(s_eTc, 1)
                after(eng, s_mT, n, 1)
                if n_positive(n):
                    eng.wait_ge(s_F, n)
                nc.scalar.copy(mixedT[:, :, :], pX[:, 0:D].rearrange("p (k q) -> p k q", k=KD)).then_inc(s_mTc, 1)
            chunks(eng, NCH, mid, lambda i, p: ln.scalar(eng, i, p, s_q, KD), tiles(tail))

        @block.tensor
        def _(eng):
            eng.wait_ge(s_in, ALL_IN)
            for m in range(KD):
                if m:
                    eng.wait_ge(s_kTc, m)
                for k in range(KD):
                    last = nc.tensor.matmul(pX[:, 0:NB * CTX], wk[:, k, m * P:(m + 1) * P],
                                            ctxT[:, k, :, :].rearrange("p b s -> p (b s)"), start=(k == 0), stop=(k == KD - 1))
                last.then_inc(s_kT, 1)
            for b in range(NB):
                if b:
                    eng.wait_ge(s_vc, b)
                for k in range(KD):
                    last = nc.tensor.matmul(pV[0:CTX, :], ctxT[:, k, b, :], wv[:, k, :], start=(k == 0), stop=(k == KD - 1))
                last.then_inc(s_vp, 1)
            eng.wait_ge(s_kd, KD)
            eng.wait_ge(s_vc, NB)

            def mid(i, p):
                after(eng, ln.s_xnT, i, KD)
                if n_positive(i):
                    eng.wait_ge(s_sub, i * TC * KD)
                for m in range(KD):
                    for k in range(KD):
                        last = nc.tensor.matmul(pS[m][:, 0, :], wq[:, k, m * P:(m + 1) * P], ln.xnT[p][:, k, :],
                                                start=(k == 0), stop=(k == KD - 1))
                    last.then_inc(s_q, 1)

            def scores(i, p, t, n):
                for m in range(KD):
                    if t == 0:
                        after(eng, s_qc, i, KD)
                    else:
                        eng.wait_ge(s_sub, n * KD - KD + m + 1)
                    for g in range(2):
                        last = nc.tensor.matmul(pS[m][:, g, 0:HG * CTX], qT[p][:, m, t * P:(t + 1) * P],
                                                kdiag[m][:, bass.ds(i // CPB, 1), g * HG:(g + 1) * HG, :].rearrange("p a h s -> p (a h s)"),
                                                start=True, stop=True)
                    last.then_inc(s_S, 1)

            def tail(i, p):
                scores(i, p, 0, i * TC)
                for t in range(TC):
                    n = i * TC + t
                    if n_positive(n):
                        eng.wait_ge(s_res, n)
                        eng.wait_ge(s_mix, n)
                    for g in range(4):
                        after(eng, s_exp, n, KD, g // 2 + 1)
                        if g:
                            eng.wait_ge(s_eTc, n * 4 + g)
                        for h in range(4):
                            last = nc.tensor.transpose(pX[0:CTX, h * P:(h + 1) * P], e[g // 2][:, (g % 2) * 4 + h, :], K.ident[:, :])
                        last.then_inc(s_eT, 1)
                        if g == 0 and t + 1 < TC:
                            scores(i, p, t + 1, n + 1)
                        after(eng, s_eTc, n, 4, g + 1)
                        for h in range(4):
                            hh = g * 4 + h
                            last = nc.tensor.matmul(pV[:, hh * HD:(hh + 1) * HD], eT[g % 2][:, h, :],
                                                    v[:, bass.ds(i // CPB, 1), hh * HD:(hh + 1) * HD].rearrange("s a d -> s (a d)"),
                                                    start=True, stop=True)
                        last.then_inc(s_pv, 1)
                    after(eng, s_mix, n, 1)
                    for k in range(KD):
                        last = nc.tensor.transpose(pX[:, k * P:(k + 1) * P], mixed[:, k * P:(k + 1) * P], K.ident[:, :])
                    last.then_inc(s_mT, 1)
                    after(eng, s_mTc, n, 1)
                    for k in range(KD):
                        last = nc.tensor.matmul(pX[:, 0:D], mixedT[:, k, :], wo[:, k, :], start=(k == 0), stop=(k == KD - 1))
                    last.then_inc(s_F, 1)
            chunks(eng, NCH, mid, lambda i, p: ln.tensor(eng, i, p), tail)


def top2_experts(K):
    NE = K.io["t2_router"].shape[1]
    with ExitStack() as c:
        h_rows = K.sb(c, "t2_h_rows", [P, NT, D])
        weight = K.sb(c, "t2_weight", [P, NT, TOP])
        chosen = [K.sb(c, f"t2_chosen{k}", [P, NT, NE]) for k in range(TOP)]
        slot = [K.sb(c, f"t2_slot{k}", [P, NT], U32) for k in range(TOP)]
        expert_of = K.sb(c, "t2_expert_of", [P, NST_TILES], I32)
        h_sorted = K.nc.dram_tensor("t2_h_sorted", [NST_TILES * ST, D], F32).ap()
        y_sorted = K.nc.dram_tensor("t2_y_sorted", [NST_TILES * ST, D], F32).ap()
        _route_top2(K, h_rows, weight, chosen, h_sorted)
        K.clear()
        _assign_slots(K, chosen, slot, expert_of)
        K.clear()
        _scatter_rows(K, h_rows, slot, h_sorted)
        K.clear()
        _expert_tiles(K, expert_of, h_sorted, y_sorted)
        K.clear()
        _combine(K, weight, slot, y_sorted)


def _route_top2(K, h_rows, weight, chosen, h_sorted):
    nc, io = K.nc, K.io
    NE = chosen[0].shape[2]
    ZT = 4
    with ExitStack() as c:
        ln = LayerNormFront(K, c, "r2")
        sb = lambda n, s, d=F32: K.sb(c, f"r2_{n}", s, d)
        sem = lambda n: K.sem(c, f"r2_{n}")
        router = sb("router", [P, KD, NE])
        router_b = sb("router_b", [P, NE])
        zeros = sb("zeros", [P, ZT, D])
        logit = sb("logit", [P, TC, NE])
        best = sb("best", [P, TC, 8])
        index = sb("index", [P, TC, 8], U32)
        index_f = sb("index_f", [P, TC, TOP])
        behind = sb("behind", [P, TC])
        e2 = sb("e2", [P, TC])
        total = sb("total", [P, TC])
        w0 = sb("w0", [P, TC])
        pS = K.ps(c, "r2_pS", [P, TC, NE])
        s_in, s_lg, s_v, s_e, s_copy, s_w, s_z, s_zero = (sem(n) for n in ("in", "lg", "v", "e", "copy", "w", "z", "zero"))
        N = 9
        block = c.enter_context(nc.Block())

        @block.sync
        def _(eng):
            eng.dma_start(router[:, :, :], io["t2_router"].rearrange("(k p) e -> p k e", p=P)).then_inc(s_in, 16)
            eng.dma_start(router_b[:, :], io["t2_router_b"].partition_broadcast(P)).then_inc(s_in, 16)
            eng.wait_ge(s_z, 1)
            n_zero = NST_TILES * ST // (P * ZT)
            with eng.Fori(0, n_zero) as z:
                eng.dma_start(h_sorted[bass.ds(z * (P * ZT), P * ZT), :].rearrange("(p a) d -> p a d", a=ZT), zeros[:, :, :]
                              ).then_inc(s_zero, 16)
            eng.wait_ge(s_zero, 16 * n_zero)

        @block.gpsimd
        def _(eng):
            def mid(i, p):
                after(eng, ln.s_xn, i, TC)
                eng.sem_inc(K.held_pool)
                nc.gpsimd.tensor_copy(h_rows[:, bass.ds(i * TC, TC), :], ln.xn[p][:, :, :]).then_inc(s_copy, 1)
            chunks(eng, NCH, nothing, lambda i, p: ln.gpsimd(eng, i, p), mid)

        @block.vector
        def _(eng):
            nc.vector.memset(zeros[:, :, :], 0.0).then_inc(s_z, 1)

            def front(i, p):
                free(eng, s_copy, i, 1)
                ln.vector(eng, i, p)

            def mid(i, p):
                after(eng, s_lg, i, 1)
                ch = Chain(eng, s_v, i, N)
                ch.do(nc.vector.tensor_tensor(logit[:, :, :], pS[:, :, :],
                                              router_b[:, :].unsqueeze(1).to_broadcast([P, TC, NE]), ALU.add))
                eng.sem_inc(K.held_vector)
                for t in range(TC):
                    last = nc.vector.max(best[:, t, :], logit[:, t, :])
                ch.do(last)
                eng.sem_inc(K.held_vector)
                for t in range(TC):
                    last = nc.vector.max_index(index[:, t, :], best[:, t, :], logit[:, t, :])
                ch.do(last)
                ch.do(nc.vector.tensor_copy(index_f[:, :, :], index[:, :, 0:TOP]))
                ch.do(nc.vector.tensor_tensor(behind[:, :], best[:, :, 1], best[:, :, 0], ALU.subtract))
                after(eng, s_e, i, 1)
                ch.do(nc.vector.tensor_scalar(total[:, :], e2[:, :], 1.0, None, ALU.add))
                ch.do(nc.vector.reciprocal(w0[:, :], total[:, :]))
                nc.vector.tensor_copy(weight[:, bass.ds(i * TC, TC), 0], w0[:, :])
                ch.do(nc.vector.tensor_tensor(weight[:, bass.ds(i * TC, TC), 1], e2[:, :], w0[:, :], ALU.mult))
                for k in range(TOP):
                    last = nc.vector.tensor_tensor(chosen[k][:, bass.ds(i * TC, TC), :],
                                                   K.iota8[:, :].unsqueeze(1).to_broadcast([P, TC, NE]),
                                                   index_f[:, :, k].unsqueeze(2).to_broadcast([P, TC, NE]), ALU.is_equal)
                ch.do(last)
                ch.done()
            chunks(eng, NCH, mid, front, nothing)

        @block.scalar
        def _(eng):
            def mid(i, p):
                after(eng, s_v, i, N, 5)
                nc.scalar.activation(e2[:, :], behind[:, :], ACT.Exp).then_inc(s_e, 1)
            chunks(eng, NCH, mid, lambda i, p: ln.scalar(eng, i, p, s_lg, 1), nothing)

        @block.tensor
        def _(eng):
            def mid(i, p):
                after(eng, ln.s_xnT, i, KD)
                if n_positive(i):
                    after(eng, s_v, i - 1, N, 1)
                for t in range(TC):
                    for k in range(KD):
                        last = nc.tensor.matmul(pS[:, t, :], ln.xnT[p][:, k, t * P:(t + 1) * P], router[:, k, :],
                                                start=(k == 0), stop=(k == KD - 1))
                last.then_inc(s_lg, 1)
            eng.wait_ge(s_in, 32)
            chunks(eng, NCH, mid, lambda i, p: ln.tensor(eng, i, p), nothing)


def _assign_slots(K, chosen, slot, expert_of):
    nc = K.nc
    NE = chosen[0].shape[2]
    LOG = ST.bit_length() - 1
    with ExitStack() as c:
        sb = lambda n, s, d=F32: K.sb(c, f"as_{n}", s, d)
        sem = lambda n: K.sem(c, f"as_{n}")
        ones = sb("ones", [P, P])
        earlier = sb("earlier", [P, P])
        pairs = sb("pairs", [P, NT, NE])
        upto = sb("upto", [P, NE, NT])
        place = sb("place", [P, NT, NE])
        picked = sb("picked", [P, NT, NE])
        slot_f = sb("slot_f", [P, NT])
        padded = sb("padded", [P, NE])
        padded_i = sb("padded_i", [P, NE], I32)
        tiles_i = sb("tiles_i", [P, NE], I32)
        tiles = sb("tiles", [P, NE])
        end = sb("end", [P, NE])
        first = sb("first", [P, NE])
        number = sb("number", [P, NST_TILES])
        passed = sb("passed", [P, NST_TILES, NE])
        expert_f = sb("expert_f", [P, NST_TILES])
        pRows = K.ps(c, "as_pRows", [P, NT, NE])
        pTile = K.ps(c, "as_pTile", [P, NT, NE])
        s_v, s_g, s_p = sem("v"), sem("g"), sem("p")
        block = c.enter_context(nc.Block())

        @block.gpsimd
        def _(eng):
            eng.wait_ge(s_v, 1)
            nc.gpsimd.affine_select(out=earlier[:, :], in_=earlier[:, :], compare_op=ALU.is_ge, fill=0.0, base=-1,
                                    pattern=[[1, P]], channel_multiplier=-1).then_inc(s_g, 1)
            nc.gpsimd.iota(number[:, :], pattern=[[1, NST_TILES]], base=0, channel_multiplier=0,
                           allow_small_or_imprecise_dtypes=True).then_inc(s_g, 1)

        @block.tensor
        def _(eng):
            eng.wait_ge(s_v, 3)
            eng.wait_ge(s_g, 2)
            flat = pairs[:, :, :].rearrange("p t e -> p (t e)")
            nc.tensor.matmul(pRows[:, :, :], earlier[:, :], flat, start=True, stop=True).then_inc(s_p, 1)
            nc.tensor.matmul(pTile[:, :, :], ones[:, :], flat, start=True, stop=True).then_inc(s_p, 1)

        @block.vector
        def _(eng):
            ch = Chain(eng, s_v, 0, None)
            ch.do(nc.vector.memset(earlier[:, :], 1.0))
            ch.do(nc.vector.memset(ones[:, :], 1.0))
            ch.do(nc.vector.tensor_tensor(pairs[:, :, :], chosen[0][:, :, :], chosen[1][:, :, :], ALU.add))
            eng.wait_ge(s_p, 2)
            for e in range(NE):
                last = nc.vector.tensor_tensor_scan(upto[:, e, :], ones[:, 0:NT], pTile[:, :, e], 0.0, ALU.mult, ALU.add)
            ch.do(last)
            ch.do(nc.vector.tensor_scalar(padded[:, :], upto[:, :, NT - 1], float(ST - 1), None, ALU.add))
            ch.do(nc.vector.tensor_copy(padded_i[:, :], padded[:, :]))
            ch.do(nc.vector.tensor_scalar(tiles_i[:, :], padded_i[:, :], LOG, None, ALU.arith_shift_right))
            ch.do(nc.vector.tensor_copy(tiles[:, :], tiles_i[:, :]))
            ch.do(nc.vector.tensor_tensor_scan(end[:, :], ones[:, 0:NE], tiles[:, :], 0.0, ALU.mult, ALU.add))
            ch.do(nc.vector.tensor_tensor(first[:, :], end[:, :], tiles[:, :], ALU.subtract))
            ch.do(nc.vector.tensor_scalar(first[:, :], first[:, :], float(ST), None, ALU.mult))
            ch.do(nc.vector.tensor_tensor(place[:, :, :], upto[:, :, :].rearrange("p e t -> p t e"), pTile[:, :, :], ALU.subtract))
            ch.do(nc.vector.tensor_tensor(place[:, :, :], place[:, :, :], pRows[:, :, :], ALU.add))
            ch.do(nc.vector.tensor_tensor(place[:, :, :], place[:, :, :],
                                          first[:, :].unsqueeze(1).to_broadcast([P, NT, NE]), ALU.add))
            for k in range(TOP):
                ch.do(nc.vector.tensor_tensor(picked[:, :, :], place[:, :, :], chosen[k][:, :, :], ALU.mult))
                ch.do(nc.vector.tensor_reduce(slot_f[:, :], picked[:, :, :], axis=AX.X, op=ALU.add))
                ch.do(nc.vector.tensor_copy(slot[k][:, :], slot_f[:, :]))
            ch.do(nc.vector.tensor_tensor(passed[:, :, :], number[:, :].unsqueeze(2).to_broadcast([P, NST_TILES, NE]),
                                          end[:, :].unsqueeze(1).to_broadcast([P, NST_TILES, NE]), ALU.is_ge))
            ch.do(nc.vector.tensor_reduce(expert_f[:, :], passed[:, :, :], axis=AX.X, op=ALU.add))
            ch.do(nc.vector.tensor_scalar(expert_f[:, :], expert_f[:, :], float(NE - 1), None, ALU.min))
            ch.do(nc.vector.tensor_copy(expert_of[:, :], expert_f[:, :]))


def _scatter_rows(K, h_rows, slot, h_sorted):
    nc = K.nc
    BUFS = 4
    with ExitStack() as c:
        sb = lambda n, s, d=F32: K.sb(c, f"sc_{n}", s, d)
        sem = lambda n: K.sem(c, f"sc_{n}")
        row = [sb(f"row{q}", [P, D]) for q in range(BUFS)]
        to = [[sb(f"to{q}_{k}", [P, 1], U32) for k in range(TOP)] for q in range(BUFS)]
        s_fill = sem("fill")
        s_out = [sem(f"out{q}") for q in range(BUFS)]
        block = c.enter_context(nc.Block())

        @block.vector
        def _(eng):
            def fill(r, q):
                t = r * BUFS + q
                if n_positive(r):
                    eng.wait_ge(s_out[q], r * (16 * TOP))
                nc.vector.tensor_copy(row[q][:, :], h_rows[:, bass.ds(t, 1), :].rearrange("p a d -> p (a d)"))
                for k in range(TOP):
                    last = nc.vector.tensor_copy(to[q][k][:, :], slot[k][:, bass.ds(t, 1)])
                last.then_inc(s_fill, 1)
            for q in range(BUFS):
                fill(0, q)
            with eng.Fori(1, NT // BUFS) as r:
                for q in range(BUFS):
                    fill(r, q)

        @block.gpsimd
        def _(eng):
            with eng.Fori(0, NT // BUFS) as r:
                for q in range(BUFS):
                    eng.wait_ge(s_fill, r * BUFS + q + 1)
                    eng.sem_inc(K.held_pool)
                    for k in range(TOP):
                        nc.gpsimd.indirect_dma_start(h_sorted, bass.IndirectOffsetOnAxis(ap=to[q][k][:, :], axis=0),
                                                     row[q][:, :], None).then_inc(s_out[q], 16)
            for q in range(BUFS):
                eng.wait_ge(s_out[q], NT // BUFS * 16 * TOP)


def _expert_tiles(K, expert_of, h_sorted, y_sorted):
    nc, io = K.nc, K.io
    NE, _, HID = io["t2_wgT"].shape
    HT = HID // P
    SP_ = ST // P
    PAIR = 2
    NP = HT // PAIR
    with ExitStack() as c:
        sb = lambda n, s, d=F32: K.sb(c, f"et_{n}", s, d)
        sem = lambda n: K.sem(c, f"et_{n}")
        wg = [sb(f"wg{q}", [P, KD, HID]) for q in range(2)]
        wu = [sb(f"wu{q}", [P, KD, HID]) for q in range(2)]
        wd = [sb(f"wd{q}", [P, HT, D]) for q in range(2)]
        h = [sb(f"h{q}", [P, SP_, D]) for q in range(2)]
        hT = [sb(f"hT{q}", [P, KD, ST]) for q in range(2)]
        silu = [sb(f"silu{q}", [P, PAIR, ST]) for q in range(2)]
        mT = [sb(f"mT{q}", [P, PAIR, ST]) for q in range(NP)]
        y = [sb(f"y{q}", [P, SP_, D]) for q in range(2)]
        pT = K.ps(c, "et_pT", [P, KD, ST])
        pG = [K.ps(c, f"et_pG{q}", [P, PAIR, ST]) for q in range(2)]
        pU = [K.ps(c, f"et_pU{q}", [P, PAIR, ST]) for q in range(2)]
        pO = [K.ps(c, f"et_pO{q}", [P, SP_, D]) for q in range(2)]
        s_w = [sem(f"w{q}") for q in range(2)]
        s_h = [sem(f"h{q}s") for q in range(2)]
        s_out = [sem(f"out{q}") for q in range(2)]
        s_tp, s_hT, s_gu, s_silu, s_m, s_o, s_y = (sem(n) for n in ("tp", "hTs", "gu", "silus", "m", "o", "ys"))
        block = c.enter_context(nc.Block())

        def pairs_of_steps(eng, fn):
            fn(0, 0)
            fn(1, 1)
            with eng.Fori(1, NST_TILES // 2) as j:
                fn(2 * j, 0)
                fn(2 * j + 1, 1)

        @block.sync
        def _(eng):
            def load(i, q):
                if not isinstance(i, int) or i >= 2:
                    eng.wait_ge(s_o, i - 1)
                e = eng.value_load(expert_of[0:1, bass.ds(i, 1)], min_val=0, max_val=NE - 1)
                eng.dma_start(h[q][:, :, :], h_sorted[bass.ds(i * ST, ST), :].rearrange("(a p) d -> p a d", p=P)).then_inc(s_h[q], 16)
                for dst, name in ((wg[q], "t2_wgT"), (wu[q], "t2_wuT"), (wd[q], "t2_wdT")):
                    src = io[name][bass.ds(e, 1), :, :].rearrange("a (k p) n -> p (a k) n", p=P)
                    eng.dma_start(dst[:, :, :], src).then_inc(s_w[q], 16)
            pairs_of_steps(eng, load)

        @block.gpsimd
        def _(eng):
            def save(i, q):
                after(eng, s_y, i, 1)
                eng.sem_inc(K.held_pool)
                eng.dma_start(y_sorted[bass.ds(i * ST, ST), :].rearrange("(a p) d -> p a d", p=P), y[q][:, :, :]).then_inc(s_out[q], 16)
            pairs_of_steps(eng, save)
            for q in range(2):
                eng.wait_ge(s_out[q], 16 * (NST_TILES // 2))

        @block.scalar
        def _(eng):
            def step(i, q):
                after(eng, s_tp, i, 1)
                nc.scalar.copy(hT[q][:, :, :], pT[:, :, :]).then_inc(s_hT, 1)
                for j in range(NP):
                    after(eng, s_gu, i, NP, j + 1)
                    if j >= 2 or n_positive(i):
                        eng.wait_ge(s_m, i * NP + j - 1)
                    nc.scalar.activation(silu[j % 2][:, :, :], pG[j % 2][:, :, :], ACT.Silu).then_inc(s_silu, 1)
            pairs_of_steps(eng, step)

        @block.vector
        def _(eng):
            def step(i, q):
                for j in range(NP):
                    after(eng, s_silu, i, NP, j + 1)
                    if n_positive(i) and j == 0:
                        eng.wait_ge(s_o, i)
                    nc.vector.tensor_tensor(mT[j][:, :, :], silu[j % 2][:, :, :], pU[j % 2][:, :, :], ALU.mult).then_inc(s_m, 1)
                after(eng, s_o, i, 1)
                if not isinstance(i, int) or i >= 2:
                    eng.wait_ge(s_out[q], (i // 2) * 16)
                nc.vector.tensor_copy(y[q][:, :, :], pO[q][:, :, :]).then_inc(s_y, 1)
            pairs_of_steps(eng, step)

        @block.tensor
        def _(eng):
            def transpose(i, q):
                eng.wait_ge(s_h[q], (i // 2) * 16 + 16)
                if n_positive(i):
                    eng.wait_ge(s_hT, i)
                    eng.sem_inc(K.held_tensor)
                for k in range(KD):
                    for a in range(SP_):
                        last = nc.tensor.transpose(pT[:, k, a * P:(a + 1) * P], h[q][:, a, k * P:(k + 1) * P], K.ident[:, :])
                last.then_inc(s_tp, 1)

            def gate_up(i, q, j):
                if j >= 2 or n_positive(i):
                    eng.wait_ge(s_m, i * NP + j - 1)
                for w, out in ((wg[q], pG[j % 2]), (wu[q], pU[j % 2])):
                    for x in range(PAIR):
                        col = (j * PAIR + x) * P
                        for k in range(KD):
                            last = nc.tensor.matmul(out[:, x, :], w[:, k, col:col + P], hT[q][:, k, :],
                                                    start=(k == 0), stop=(k == KD - 1))
                last.then_inc(s_gu, 1)

            def down(i, q, j):
                after(eng, s_m, i, NP, j + 1)
                if j == 0 and (not isinstance(i, int) or i >= 2):
                    eng.wait_ge(s_y, i - 1)
                for x in range(PAIR):
                    for a in range(SP_):
                        last = nc.tensor.matmul(pO[q][:, a, :], mT[j][:, x, a * P:(a + 1) * P], wd[q][:, j * PAIR + x, :],
                                                start=(j == 0 and x == 0 and a == 0), stop=(j == NP - 1 and x == PAIR - 1),
                                                skip_group_check=True)
                if j == NP - 1:
                    last.then_inc(s_o, 1)

            def step(i, q, ahead):
                after(eng, s_hT, i, 1)
                eng.wait_ge(s_w[q], (i // 2) * 48 + 48)
                gate_up(i, q, 0)
                gate_up(i, q, 1)
                for j in range(2, NP):
                    down(i, q, j - 2)
                    gate_up(i, q, j)
                if ahead:
                    transpose(i + 1, 1 - q)
                down(i, q, NP - 2)
                down(i, q, NP - 1)
            transpose(0, 0)
            step(0, 0, True)
            with eng.Fori(1, NST_TILES // 2) as j:
                step(2 * j - 1, 1, True)
                step(2 * j, 0, True)
            step(NST_TILES - 1, 1, False)


def _combine(K, weight, slot, y_sorted):
    nc, R = K.nc, K.resid
    BUFS = 4
    with ExitStack() as c:
        sb = lambda n, s, d=F32: K.sb(c, f"cb_{n}", s, d)
        sem = lambda n: K.sem(c, f"cb_{n}")
        y = [[sb(f"y{q}_{k}", [P, D]) for k in range(TOP)] for q in range(BUFS)]
        at = [[sb(f"at{q}_{k}", [P, 1], U32) for k in range(TOP)] for q in range(BUFS)]
        s_at, s_add = sem("at"), sem("add")
        s_y = [sem(f"y{q}") for q in range(BUFS)]
        block = c.enter_context(nc.Block())

        def rounds(eng, fn):
            for q in range(BUFS):
                fn(0, q)
            with eng.Fori(1, NT // BUFS) as r:
                for q in range(BUFS):
                    fn(r, q)

        @block.scalar
        def _(eng):
            def slots(r, q):
                if n_positive(r):
                    eng.wait_ge(s_y[q], r * (16 * TOP))
                for k in range(TOP):
                    last = nc.scalar.copy(at[q][k][:, :], slot[k][:, bass.ds(r * BUFS + q, 1)])
                last.then_inc(s_at, 1)
            rounds(eng, slots)

        @block.gpsimd
        def _(eng):
            def gather(r, q):
                eng.wait_ge(s_at, r * BUFS + q + 1)
                if n_positive(r):
                    eng.wait_ge(s_add, (r * BUFS + q - BUFS + 1) * TOP)
                    eng.sem_inc(K.held_pool)
                for k in range(TOP):
                    nc.gpsimd.indirect_dma_start(y[q][k][:, :], None, y_sorted,
                                                 bass.IndirectOffsetOnAxis(ap=at[q][k][:, :], axis=0)).then_inc(s_y[q], 16)
            rounds(eng, gather)

        @block.vector
        def _(eng):
            def add(r, q):
                t = r * BUFS + q
                row = R[:, bass.ds(t, 1), :].rearrange("p a d -> p (a d)")
                eng.wait_ge(s_y[q], r * (16 * TOP) + 16 * TOP)
                for k in range(TOP):
                    w = weight[:, bass.ds(t, 1), k]
                    nc.vector.scalar_tensor_tensor(row, y[q][k][:, :], w, row, ALU.mult, ALU.add).then_inc(s_add, 1)
                    after(eng, s_add, t, TOP, k + 1)
            rounds(eng, add)


STAGES = [load_and_constants, mamba, context_glu, top1_experts, self_attention, cross_attention, top2_experts, store]


def decoder(nc, io, stages=None):
    with ExitStack() as ctx:
        K = Kernel(nc, ctx, io)
        for stage in stages or STAGES:
            stage(K)
            K.clear()


def layout(inputs):
    t = lambda n, *axes: np.ascontiguousarray(np.transpose(np.asarray(inputs[n]), axes))
    same = lambda n: np.ascontiguousarray(np.asarray(inputs[n]))
    return {
        "x": same("x"), "ctx": same("ctx_1024"), "ctxT": t("ctx_1024", 0, 2, 1),
        "t1_router": same("L0_ffn_router_w"), "t1_router_b": same("L0_ffn_router_b"),
        "t2_router": t("L1_ffn_wg", 1, 0), "t2_router_b": same("L1_ffn_bg"),
        "t2_wgT": t("L1_ffn_Wgate", 0, 2, 1), "t2_wuT": t("L1_ffn_Wup", 0, 2, 1), "t2_wdT": t("L1_ffn_Wdown", 0, 2, 1),
        "xa_wqT": t("L1_xattn_Wq", 1, 0), "xa_wkT": t("L1_xattn_Wk", 1, 0), "xa_wvT": t("L1_xattn_Wv", 1, 0),
        "xa_woT": t("L1_xattn_Wo", 1, 0), "xa_bq": same("L1_xattn_bq"), "xa_bk": same("L1_xattn_bk"),
        "xa_bv": same("L1_xattn_bv"), "xa_bo": same("L1_xattn_bo"),
        "sa_wqT": t("L1_attn_wq", 1, 0), "sa_wkT": t("L1_attn_wk", 1, 0), "sa_wvT": t("L1_attn_wv", 1, 0),
        "sa_woT": t("L1_attn_wo", 1, 0),
        "mb_w_in": same("L0_attn_W_in"), "mb_conv_w": same("L0_attn_conv_w"), "mb_conv_b": same("L0_attn_conv_b"),
        "mb_w_x": same("L0_attn_W_xproj"), "mb_wdt": same("L0_attn_W_dt"), "mb_b_dt": same("L0_attn_b_dt"),
        "mb_A_log": same("L0_attn_A_log"), "mb_D": same("L0_attn_D"), "mb_w_out": same("L0_attn_W_out"),
        "t1_w": same("L0_ffn_expert_w"), "t1_b": same("L0_ffn_expert_b"),
    }


def kernel(**inputs):
    import concourse.bacc as bacc
    from concourse.bass_utils import run_bass_kernel_spmd

    nc = bacc.Bacc("TRN2", target_bir_lowering=False, num_devices=1)
    arrays, io = {}, {}
    for name, a in layout(inputs).items():
        arrays[f"in_{name}"] = a
        io[name] = nc.dram_tensor(f"in_{name}", a.shape, mybir.dt.from_np(a.dtype), kind="ExternalInput").ap()
    io["out"] = nc.dram_tensor("out", (NB, SEQ, D), F32, kind="ExternalOutput").ap()
    decoder(nc, io)
    r = run_bass_kernel_spmd(nc, [arrays], core_ids=[0])
    return r.results[0]["out"]
```

```python
from contextlib import ExitStack

import concourse.bass as bass
from concourse import mybir
import numpy as np

F32 = mybir.dt.float32
F32R = mybir.dt.float32r
BF16 = mybir.dt.bfloat16
I32 = mybir.dt.int32
U32 = mybir.dt.uint32
ALU = mybir.AluOpType
ACT = mybir.ActivationFunctionType
AX = mybir.AxisListType

P = 128
NB, SEQ, D = 4, 1024, 256
TOK = NB * SEQ
NT = TOK // P
KD = D // P
CH = 512
TC = CH // P
NCH = TOK // CH
CPB = SEQ // CH
CTX = 77
EPS = 1e-5
TOP = 2
ST = 256
NST_TILES = (TOP * TOK + 8 * (ST - 1)) // ST


def after(eng, sem, i, per, k=None):
    eng.wait_ge(sem, i * per + (per if k is None else k))


def free(eng, sem, i, per, back=2):
    if not isinstance(i, int) or i >= back:
        eng.wait_ge(sem, (i - back + 1) * per)


def n_positive(n):
    return not isinstance(n, int) or n > 0


def chunks(eng, n, mid, front, tail):
    front(0, 0)
    mid(0, 0)
    front(1, 1)
    tail(0, 0)
    with eng.Fori(1, n // 2) as j:
        mid(2 * j - 1, 1)
        front(2 * j, 0)
        tail(2 * j - 1, 1)
        mid(2 * j, 0)
        front(2 * j + 1, 1)
        tail(2 * j, 0)
    mid(n - 1, 1)
    tail(n - 1, 1)


def nothing(i, p):
    pass


class Kernel:

    def __init__(self, nc, ctx, io):
        self.nc, self.io, self.in_use = nc, io, []
        self.resid = self.sb(ctx, "resid", [P, NT, D])
        self.ident = self.sb(ctx, "ident", [P, P])
        self.iota8 = self.sb(ctx, "iota8", [P, 8])
        self.held_vector = ctx.enter_context(nc.semaphore("held_vector"))
        self.held_pool = ctx.enter_context(nc.semaphore("held_pool"))
        self.held_tensor = ctx.enter_context(nc.semaphore("held_tensor"))
        self.minus_half = self.sb(ctx, "minus_half", [P, TC])

    def sb(self, ctx, name, shape, dt=F32):
        return ctx.enter_context(self.nc.sbuf_tensor(name, shape, dt))

    def ps(self, ctx, name, shape, dt=F32):
        return ctx.enter_context(self.nc.psum_tensor(name, shape, dt))

    def sem(self, ctx, name):
        self.in_use.append(self.nc.alloc_semaphore(name=name))
        return self.in_use[-1]

    def clear(self):
        self.nc.clear_and_free_semaphores(self.in_use)
        self.nc.all_engine_barrier()
        self.in_use = []


class LayerNormFront:

    def __init__(self, K, ctx, tag, keep_rows=False):
        nc = K.nc
        self.K, self.nc = K, nc
        sb = lambda n, s, d=F32: K.sb(ctx, f"{tag}_{n}", s, d)
        self.stats = [sb(f"stats{p}", [P, TC, 6]) for p in range(2)]
        self.mv = [sb(f"mv{p}", [P, TC, 2]) for p in range(2)]
        self.veps = [sb(f"veps{p}", [P, TC]) for p in range(2)]
        self.rstd = [sb(f"rstd{p}", [P, TC]) for p in range(2)]
        self.xn = [sb(f"xn{p}", [P, TC, D]) for p in range(2)]
        self.xnT = [sb(f"xnT{p}", [P, KD, CH]) for p in range(2)]
        self.pT = [K.ps(ctx, f"{tag}_pT{k}", [P, CH]) for k in range(KD)]
        sem = lambda n: K.sem(ctx, f"{tag}_{n}")
        self.s_stats, self.s_mv, self.s_veps = sem("stats"), sem("mv"), sem("veps")
        self.s_rstd, self.s_xn, self.s_pT, self.s_xnT = sem("rstd"), sem("xn"), sem("pT"), sem("xnT")

    def vector(self, eng, i, p):
        self.statistics(eng, i, p)
        self.normalise(eng, i, p)

    def statistics(self, eng, i, p):
        nc, R = self.nc, self.K.resid
        for t in range(TC):
            nc.vector.bn_stats(self.stats[p][:, t, :], R[:, bass.ds(i * TC + t, 1), :].rearrange("p a d -> p (a d)")).then_inc(self.s_stats, 1)
        after(eng, self.s_stats, i, TC)
        eng.sem_inc(self.K.held_vector)
        for t in range(TC):
            nc.vector.bn_aggr(self.mv[p][:, t, :], self.stats[p][:, t, :]).then_inc(self.s_mv, 1)
        after(eng, self.s_mv, i, TC)
        nc.vector.tensor_scalar(self.veps[p][:, :], self.mv[p][:, :, 1], EPS, None, ALU.add).then_inc(self.s_veps, 1)

    def normalise(self, eng, i, p):
        nc, R = self.nc, self.K.resid
        after(eng, self.s_rstd, i, 1)
        free(eng, self.s_pT, i, KD)
        for t in range(TC):
            nc.vector.tensor_scalar(self.xn[p][:, t, :], R[:, bass.ds(i * TC + t, 1), :].rearrange("p a d -> p (a d)"),
                                    self.mv[p][:, t, 0:1], self.rstd[p][:, t:t + 1],
                                    ALU.subtract, ALU.mult).then_inc(self.s_xn, 1)

    def gpsimd(self, eng, i, p):
        after(eng, self.s_veps, i, 1)
        self.nc.gpsimd.tensor_tensor(self.rstd[p][:, :], self.veps[p][:, :], self.K.minus_half[:, :],
                                     ALU.pow).then_inc(self.s_rstd, 1)

    def tensor(self, eng, i, p):
        after(eng, self.s_xn, i, TC)
        for k in range(KD):
            free(eng, self.s_xnT, i, KD, back=1)
            for t in range(TC):
                last = self.nc.tensor.transpose(self.pT[k][:, t * P:(t + 1) * P],
                                                self.xn[p][:, t, k * P:(k + 1) * P], self.K.ident[:, :])
            last.then_inc(self.s_pT, 1)

    def scalar(self, eng, i, p, s_used=None, per_used=None):
        if s_used is not None:
            free(eng, s_used, i, per_used)
        for k in range(KD):
            after(eng, self.s_pT, i, KD, k + 1)
            self.nc.scalar.copy(self.xnT[p][:, k, :], self.pT[k][:, :]).then_inc(self.s_xnT, 1)


def rows(R, i):
    return R[:, bass.ds(i * TC, TC), :]


def load_and_constants(K):
    nc, io = K.nc, K.io
    with ExitStack() as c:
        s_x, s_c = K.sem(c, "ld_x"), K.sem(c, "ld_c")
        block = c.enter_context(nc.Block())

        @block.sync
        def _(eng):
            eng.dma_start(K.resid[:, :, :], io["x"].rearrange("b (t p) d -> p (b t) d", p=P)).then_inc(s_x, 16)
            eng.wait_ge(s_x, 16)

        @block.vector
        def _(eng):
            nc.vector.memset(K.minus_half[:, :], -0.5)
            nc.vector.memset(K.ident[:, :], 0.0).then_inc(s_c, 1)

        @block.gpsimd
        def _(eng):
            eng.wait_ge(s_c, 1)
            nc.gpsimd.affine_select(out=K.ident[:, :], in_=K.ident[:, :], compare_op=ALU.not_equal, fill=1.0,
                                    base=0, pattern=[[-1, P]], channel_multiplier=1)
            nc.gpsimd.iota(K.iota8[:, :], pattern=[[1, 8]], base=0, channel_multiplier=0,
                           allow_small_or_imprecise_dtypes=True)


def store(K):
    nc, io = K.nc, K.io
    with ExitStack() as c:
        s_out = K.sem(c, "st_out")
        block = c.enter_context(nc.Block())

        @block.sync
        def _(eng):
            eng.dma_start(io["out"].rearrange("b (t p) d -> p (b t) d", p=P), K.resid[:, :, :]).then_inc(s_out, 16)
            eng.wait_ge(s_out, 16)


def run_for(name, eng, ops):
    for op in ops:
        for who, fn in op:
            if who == name:
                fn(eng)


def interleave(main, other):
    out, done = [], 0
    for n, op in enumerate(main):
        out.append(op)
        upto = (n + 1) * len(other) // len(main)
        out += other[done:upto]
        done = upto
    return out


def mamba(K):
    nc, io, R = K.nc, K.io, K.resid
    DI = io["mb_D"].shape[0]
    ME = DI // P
    NST = io["mb_A_log"].shape[1]
    RANK = io["mb_wdt"].shape[0]
    NPROJ = RANK + 2 * NST
    TAPS = io["mb_conv_w"].shape[1]
    GN = 4
    NGR = NST // GN
    ITEMS = NGR * ME
    LO = 64
    with ExitStack() as c:
        ln = LayerNormFront(K, c, "ml")
        sb = lambda n, s, d=F32: K.sb(c, f"mb_{n}", s, d)
        sem = lambda n: K.sem(c, f"mb_s_{n}")
        w_in = sb("w_in_sb", [P, KD, 2 * DI])
        w_x = sb("w_x_sb", [P, ME, NPROJ])
        w_dt = sb("w_dt_sb", [RANK, DI])
        w_out = sb("w_out_sb", [P, ME, D])
        conv_w, conv_b = sb("conv_w_sb", [P, ME, TAPS]), sb("conv_b_sb", [P, ME])
        b_dt, skip = sb("b_dt_sb", [P, ME]), sb("skip", [P, ME])
        a_neg = sb("a_neg", [P, ME, NST])
        u = sb("u", [P, ME, TAPS - 1 + CH])
        xc = [sb(f"xc{q}", [P, ME, CH]) for q in range(2)]
        proj = sb("proj", [NPROJ, CH])
        proj_hl = sb("proj_hl", [LO + NPROJ, CH], F32R)
        pick = sb("pick", [LO + NPROJ, 2 * NST])
        spread = sb("spread", [LO + NPROJ, 2 * NST], F32R)
        rests = [sb(f"rest{q}", [P, CH]) for q in range(2)]
        dt = sb("dt", [P, ME, CH])
        dtx = sb("dtx", [P, ME, CH])
        b_rep = [sb(f"b_rep{q}", [P, GN, CH]) for q in range(2)]
        c_rep = [sb(f"c_rep{q}", [P, GN, CH]) for q in range(2)]
        decay = [sb(f"decay{q}", [P, GN, 1 + CH]) for q in range(2)]
        drive = [sb(f"drive{q}", [P, GN, 1 + CH]) for q in range(2)]
        hc = [sb(f"hc{q}", [P, GN, CH]) for q in range(2)]
        log1 = [sb(f"log1{q}", [P, CH]) for q in range(2)]
        carried = sb("carried", [P, ME, NST])
        mix = sb("mix", [P, CH])
        yz = sb("yz", [P, ME, CH])
        pA = [K.ps(c, f"mb_pA{q}", [P, CH]) for q in range(2)]
        pY = [K.ps(c, f"mb_pY{m}", [P, CH]) for m in range(ME)]
        (s_in, s_c, s_a, s_sel, s_A, s_Ac, s_car, s_cv, s_xc, s_phl, s_sp, s_dv, s_dt, s_dtx, s_dA, s_dB, s_scan, s_keep, s_hc, s_y,
         s_yd, s_yz, s_o, s_res, s_gate) = (sem(n) for n in (
             "in", "c", "a", "sel", "A", "Ac", "car", "cv", "xc", "phl", "sp", "dv", "dt", "dtx", "dA", "dB", "scan", "keep",
             "hc", "y", "yd", "yz", "o", "res", "gate"))
        BC = 2 * GN
        bc = lambda g, lo, hi: [(f"BC{g}", k) for k in range(lo, hi)]
        ORDER = ([("DT", 2), ("DT", 3)] + bc(1, 0, BC) + bc(2, 0, 4) + [("XC'", 0)] + bc(2, 4, 6) + [("XC'", 1)]
                 + bc(2, 6, BC) + [("XC'", 2)] + bc(3, 0, 2) + [("XC'", 3)] + bc(3, 2, 4) + [("Z", 0)] + bc(3, 4, 6)
                 + [("Z", 1)] + bc(3, 6, BC) + [("Z", 2), ("Z", 3)]
                 + [("PROJ'", 0), ("DT'", 0), ("DT'", 1)] + bc("0'", 0, BC))
        USES = len(ORDER)
        W = {name: w for w, name in enumerate(ORDER)}
        assert NGR == 4
        window_bc = lambda i, g, k: (i, W[f"BC{g}", k]) if g else (i - 1, W["BC0'", k])

        def bc_done(i, g, n):
            return window_bc(i, g, n - 1)

        def used(eng, i, w):
            eng.wait_ge(s_Ac, (i + 1) * USES + w + 1)
        later = lambda i: not isinstance(i, int) or i > 0

        def use(i, p, w, matmuls, read):
            out = pA[((p + 1) * USES + w) % 2]

            def pe(eng):
                if not isinstance(i, int) or i >= 0 or w >= 2:
                    used(eng, i, w - 2)
                matmuls(eng, out).then_inc(s_A, 1)

            def act(eng):
                eng.wait_ge(s_A, (i + 1) * USES + w + 1)
                read(eng, out).then_inc(s_Ac, 1)
            return [("tensor", pe), ("scalar", act)]

        def skip_uses(i, w, n):
            def act(eng):
                if (i, w) != (-1, 0):
                    used(eng, i, w - 1)
                eng.sem_inc(s_Ac, n)

            def pe(eng):
                if (i, w) != (-1, 0):
                    used(eng, i, w - 1)
                eng.sem_inc(s_A, n)
            return [[("tensor", pe), ("scalar", act)]]

        def front(i, p):
            def act(eng):
                if not isinstance(i, int) or i >= 2:
                    used(eng, i - 2, W["Z", ME - 1])
                ln.scalar(eng, i, p)
            def pe(eng):
                if not isinstance(i, int) or i >= 2:
                    eng.wait_ge(s_res, (i - 1) * TC)
                ln.tensor(eng, i, p)
            return ([("vector", lambda eng: ln.statistics(eng, i, p))], [("gpsimd", lambda eng: ln.gpsimd(eng, i, p))],
                    [("vector", lambda eng: ln.normalise(eng, i, p))], [("tensor", pe), ("scalar", act)])

        def in_projection(i, p, window, w, col, read):
            def matmuls(eng, out):
                if w == W["XC'", 0]:
                    after(eng, ln.s_xnT, i, KD)
                for k in range(KD):
                    last = nc.tensor.matmul(out[:, :], w_in[:, k, col:col + P], ln.xnT[p][:, k, :],
                                            start=(k == 0), stop=(k == KD - 1))
                return last
            return use(*window, w, matmuls, read)

        def project_in(i, p):
            ops = []

            def carry(eng):
                if later(i):
                    eng.wait_ge(s_cv, i * ME * TAPS)
                    eng.sem_inc(K.held_pool)
                if p == 0:
                    ins = nc.gpsimd.memset(u[:, :, 0:TAPS - 1], 0.0)
                else:
                    ins = nc.gpsimd.tensor_copy(u[:, :, 0:TAPS - 1], u[:, :, CH:CH + TAPS - 1])
                ins.then_inc(s_car, 1)
            ops.append([("gpsimd", carry)])
            for m in range(ME):
                def read(eng, out, m=m):
                    if m == 0:
                        after(eng, s_car, i, 1)
                    return nc.scalar.copy(u[:, m, TAPS - 1:], out[:, :])
                ops.append(in_projection(i, p, (i - 1, 1 - p), W["XC'", m], m * P, read))
            return ops

        def convolve(i, p):
            ops, silus = [], []
            for m in range(ME):
                def conv(eng, m=m):
                    after(eng, s_car, i, 1)
                    used(eng, i - 1, W["XC'", m])
                    a = xc[p][:, m, :]
                    if m == 0 and (not isinstance(i, int) or i >= 2):
                        eng.wait_ge(s_yd, (i - 1) * ME)
                    nc.vector.tensor_scalar(a, u[:, m, 0:CH], conv_w[:, m, 0:1], None, ALU.mult).then_inc(s_cv, 1)
                    for j in range(1, TAPS):
                        after(eng, s_cv, i, ME * TAPS, m * TAPS + j)
                        nc.vector.scalar_tensor_tensor(a, u[:, m, j:j + CH], conv_w[:, m, j:j + 1], a,
                                                       ALU.mult, ALU.add).then_inc(s_cv, 1)

                def silu(eng, m=m):
                    after(eng, s_cv, i, ME * TAPS, (m + 1) * TAPS)
                    nc.scalar.activation(xc[p][:, m, :], xc[p][:, m, :], ACT.Silu, bias=conv_b[:, m:m + 1]).then_inc(s_xc, 1)
                ops.append([("vector", conv)])
                silus.append([("scalar", silu)])
            return ops, silus

        def project(i, p):
            def matmuls(eng, out):
                for m in range(ME):
                    after(eng, s_xc, i, ME, m + 1)
                    last = nc.tensor.matmul(out[0:NPROJ, :], w_x[:, m, :], xc[p][:, m, :], start=(m == 0), stop=(m == ME - 1))
                return last

            def parts(eng):
                used(eng, i - 1, W["PROJ'", 0])
                nc.vector.tensor_copy(proj_hl[0:NPROJ, :], proj[:, :]).then_inc(s_phl, 1)
                after(eng, s_phl, i, 2, 1)
                nc.vector.tensor_tensor(proj_hl[LO:LO + NPROJ, :], proj[:, :], proj_hl[0:NPROJ, :].bitcast(F32),
                                        ALU.subtract).then_inc(s_phl, 1)
            return [use(i - 1, 1 - p, W["PROJ'", 0], matmuls, lambda eng, out: nc.scalar.copy(proj[:, :], out[0:NPROJ, :])), [("vector", parts)]]

        def step_sizes(i, p):
            sizes, logs, products = [], [], []
            nth = lambda m, k: 3 * (m - m % 2) + 2 * k + m % 2 + 1

            def logarithms(*tiles):
                def act(eng):
                    for m in tiles:
                        after(eng, s_sp, i, 3 * ME, nth(m, 0))
                        nc.scalar.activation(dtx[:, m, :], dtx[:, m, :], ACT.Exp, scale=-1.0).then_inc(s_sp, 1)
                    for m in tiles:
                        after(eng, s_sp, i, 3 * ME, nth(m, 1))
                        if m >= 2 or later(i):
                            eng.wait_ge(s_dt, i * ME + m - 1)
                        nc.scalar.activation(log1[m % 2][:, :], dtx[:, m, :], ACT.Ln, bias=1.0).then_inc(s_sp, 1)
                return act

            for m in range(ME):
                def matmuls(eng, out, m=m):
                    if m == 0:
                        used(eng, i - 1, W["PROJ'", 0])
                    return nc.tensor.matmul(out[:, :], w_dt[:, m * P:(m + 1) * P], proj[0:RANK, :], start=True, stop=True)

                def read(eng, out, m=m):
                    if later(i):
                        last_of_m = i * ITEMS - ME + m + 1
                        eng.wait_ge(s_dB, 2 * last_of_m)
                        eng.wait_ge(s_dA, last_of_m)
                    nc.scalar.activation(dtx[:, m, :], out[:, :], ACT.Abs, bias=b_dt[:, m:m + 1]).then_inc(s_sp, 1)
                    return nc.scalar.activation(dt[:, m, :], out[:, :], ACT.Relu, bias=b_dt[:, m:m + 1])

                def dve(eng, m=m):
                    ch = Chain(eng, s_dv, i, 3 * ME)
                    ch.n = 3 * m
                    rest = rests[m % 2]
                    after(eng, s_sp, i, 3 * ME, nth(m, 1))
                    if m >= 2 or later(i):
                        eng.wait_ge(s_dt, i * ME + m - 1)
                    ch.do(nc.vector.tensor_scalar(rest[:, :], dtx[:, m, :], 1.0, 1.0, ALU.add, ALU.subtract))
                    ch.do(nc.vector.tensor_tensor(rest[:, :], dtx[:, m, :], rest[:, :], ALU.subtract))
                    after(eng, s_sp, i, 3 * ME, nth(m, 2))
                    ch.do(nc.vector.tensor_tensor(rest[:, :], log1[m % 2][:, :], rest[:, :], ALU.add))
                    nc.vector.tensor_tensor(dt[:, m, :], dt[:, m, :], rest[:, :], ALU.add).then_inc(s_dt, 1)

                def pool(eng, m=m):
                    after(eng, s_dt, i, ME, m + 1)
                    nc.gpsimd.tensor_tensor(dtx[:, m, :], dt[:, m, :], xc[p][:, m, :], ALU.mult).then_inc(s_dtx, 1)
                window = (i - 1, 1 - p, W["DT'", m]) if m < 2 else (i, p, W["DT", m])
                sizes.append(use(*window, matmuls, read))
                logs.append([("vector", dve)])
                products.append([("gpsimd", pool)])
            return sizes[:2] + [[("scalar", logarithms(0, 1))]] + logs[:2], sizes[2:] + [[("scalar", logarithms(2, 3))]] + logs[2:], products

        def broadcast(i, p, g):
            ops = []
            for half, rep in ((0, b_rep), (1, c_rep)):
                for n in range(GN):
                    row = half * NST + g * GN + n

                    def matmuls(eng, out, row=row):
                        if g == 0 and row == 0:
                            after(eng, s_phl, i, 2)
                        return nc.tensor.matmul(out[:, :], spread[:, row:row + 1].to_broadcast([LO + NPROJ, P]), proj_hl[:, :], start=True, stop=True)

                    def read(eng, out, rep=rep, n=n, half=half):
                        if n == 0 and half == 0 and (g >= 2 or later(i)):
                            eng.wait_ge(s_hc, i * ITEMS + ME * (g - 1))
                        return nc.scalar.copy(rep[g % 2][:, n, :], out[:, :])
                    w_i, w = window_bc(i, g, half * GN + n)
                    ops.append(use(w_i, p if g else 1 - p, w, matmuls, read))
            return ops

        def item(i, p, g, m):
            s = g * ME + m
            q = s % 2

            def act(eng):
                if s >= 2 or later(i):
                    eng.wait_ge(s_scan, i * ITEMS + s - 1)
                after(eng, s_dt, i, ME, m + 1)
                for n in range(GN):
                    last = nc.scalar.activation(decay[q][:, n, 1:], dt[:, m, :], ACT.Exp,
                                                scale=a_neg[:, m, g * GN + n:g * GN + n + 1])
                last.then_inc(s_dA, 1)

            def pool(eng):
                if s >= 2 or later(i):
                    eng.wait_ge(s_hc, i * ITEMS + s - 1)
                after(eng, s_dtx, i, ME, m + 1)
                used(eng, *bc_done(i, g, GN))
                nc.gpsimd.tensor_tensor(drive[q][:, :, 1:], dtx[:, m, :].unsqueeze(1).to_broadcast([P, GN, CH]),
                                        b_rep[g % 2][:, :, :], ALU.mult).then_inc(s_dB, 1)
                if p == 0:
                    ins = nc.gpsimd.memset(drive[q][:, :, 0], 0.0)
                else:
                    ins = nc.gpsimd.tensor_copy(drive[q][:, :, 0], carried[:, m, g * GN:(g + 1) * GN])
                ins.then_inc(s_dB, 1)

            def dve(eng):
                after(eng, s_dA, i, ITEMS, s + 1)
                after(eng, s_dB, i, 2 * ITEMS, 2 * s + 2)
                long = lambda T: T[q][:, :, :].rearrange("p n t -> p (n t)")
                nc.vector.tensor_tensor_scan(long(drive), long(decay), long(drive), 0.0, ALU.mult, ALU.add).then_inc(s_scan, 1)
                after(eng, s_scan, i, ITEMS, s + 1)
                if p == 0:
                    nc.vector.tensor_copy(carried[:, m, g * GN:(g + 1) * GN], drive[q][:, :, CH]).then_inc(s_keep, 1)
                used(eng, *bc_done(i, g, BC))
                if s >= 2 or later(i):
                    eng.wait_ge(s_y, i * ITEMS + s - 1)
                nc.vector.tensor_tensor(hc[q][:, :, :], drive[q][:, :, 1:], c_rep[g % 2][:, :, :], ALU.mult).then_inc(s_hc, 1)
            return [("scalar", act), ("gpsimd", pool), ("vector", dve)]

        def state_sum(i, p, g, m):
            s = g * ME + m

            def pe(eng):
                if g == 0 and later(i):
                    eng.wait_ge(s_yd, (i - 1) * ME + m + 1)
                after(eng, s_hc, i, ITEMS, s + 1)
                for n in range(GN):
                    last = nc.tensor.matmul(pY[m][:, :], K.ident[:, :], hc[s % 2][:, n, :], start=(g == 0 and n == 0),
                                            stop=(g == NGR - 1 and n == GN - 1))
                last.then_inc(s_y, 1)
            return [[("tensor", pe)]]

        def gates(i, p):
            ops, silus = [], []
            for m in range(ME):
                def read(eng, out, m=m):
                    if m == 0 and later(i):
                        eng.wait_ge(s_o, i * TC)
                    return nc.scalar.copy(yz[:, m, :], out[:, :])

                def silu(eng, m=m):
                    used(eng, i, W["Z", m])
                    nc.scalar.activation(yz[:, m, :], yz[:, m, :], ACT.Silu).then_inc(s_gate, 1)
                ops.append(in_projection(i, p, (i, p), W["Z", m], DI + m * P, read))
                silus.append([("scalar", silu)])
            return ops, silus

        def finish(i, p):
            ops = []
            for m in range(ME):
                def dve(eng, m=m):
                    after(eng, s_y, i, ITEMS, ITEMS - ME + m + 1)
                    if m > 0 or later(i):
                        eng.wait_ge(s_yz, i * ME + m)
                    nc.vector.scalar_tensor_tensor(mix[:, :], xc[p][:, m, :], skip[:, m:m + 1], pY[m][:, :],
                                                   ALU.mult, ALU.add).then_inc(s_yd, 1)
                    after(eng, s_yd, i, ME, m + 1)
                    after(eng, s_gate, i, ME, m + 1)
                    nc.vector.tensor_tensor(yz[:, m, :], yz[:, m, :], mix[:, :], ALU.mult).then_inc(s_yz, 1)
                ops.append([("vector", dve)])
            return ops

        def project_out(i, p, fronts):
            out = lambda t: ln.pT[t // 2][:, t % 2 * D:(t % 2 + 1) * D]
            matmuls, adds = [], []
            for t in range(TC):
                def pe(eng, t=t):
                    if t == 0:
                        after(eng, s_yz, i, ME)
                        eng.wait_ge(ln.s_xnT, fronts * KD)
                    for m in range(ME):
                        last = nc.tensor.matmul(out(t), yz[:, m, t * P:(t + 1) * P], w_out[:, m, :],
                                                start=(m == 0), stop=(m == ME - 1))
                    if t % 2:
                        last.then_inc(s_o, 2)

                def dve(eng, t=t):
                    after(eng, s_o, i, TC, (t // 2 + 1) * 2)
                    row = R[:, bass.ds(i * TC + t, 1), :].rearrange("p a d -> p (a d)")
                    nc.vector.tensor_tensor(row, row, out(t), ALU.add).then_inc(s_res, 1)
                matmuls.append([("tensor", pe)])
                adds.append([("vector", dve)])
            return matmuls, adds

        def window(i, p, before=True, following=True):
            n, pn = i + 1, 1 - p
            group = [None] + [broadcast(i, p, g) for g in range(1, NGR)]
            z, z_silus = gates(i, p)
            done = finish(i, p)
            slots = [[] for _ in range(ITEMS)]
            for g in range(1, NGR):
                for k in range(BC):
                    slots[ME * (g - 1) + k // 2].append(group[g][k])
            if before:
                late = finish(i - 1, pn)[2:]
                matmuls, adds = project_out(i - 1, pn, i + 1)
            for m in range(ME):
                slots[9 + min(m, 2)].append(z[m])
            slots[12] += z_silus
            _, sizes23, products = step_sizes(i, p)
            slots[0] = sizes23 + slots[0] + (late if before else [])
            slots[1] = slots[1] + products[2:]
            if before:
                slots[2] += matmuls[:1]
                slots[3] += matmuls[1:3] + adds[:2]
                slots[4] = matmuls[3:] + slots[4] + adds[2:]
            if following:
                stats, power, normal, transposes = front(n, pn)
                carried_in, *xs = project_in(n, pn)
                convs, silus = convolve(n, pn)
                sizes01, _, products = step_sizes(n, pn)
                slots[0].append(stats)
                slots[1].append(power)
                slots[2].append(normal)
                slots[4].append(carried_in)
                slots[5] = [transposes] + slots[5]
                for m in range(ME):
                    slots[5 + m].append(xs[m])
                    slots[7 + m].append(convs[m])
                slots[12] += silus
                slots[13] += project(n, pn)
                slots[14] += sizes01 + broadcast(n, pn, 0)[:GN]
                slots[15] += products[:2] + broadcast(n, pn, 0)[GN:] + done[:2]
            else:
                for m in range(ME):
                    slots[5 + m] += skip_uses(i, W["XC'", m], 1)
                slots[15] += done[:2]
            ops, waiting = [], []
            for s in range(ITEMS):
                g, m = s // ME, s % ME
                ops += [item(i, p, g, m)] + slots[s] + waiting
                waiting = state_sum(i, p, g, m)
            return ops + waiting

        def emit(name, eng):
            stats, power, normal, transposes = front(0, 0)
            carried_in, *xs = project_in(0, 0)
            convs, silus = convolve(0, 0)
            sizes01, _, products = step_sizes(0, 0)
            skip = lambda w, upto: skip_uses(-1, w, W[upto] - w)
            start, at = [stats, power, normal, transposes, carried_in], 0
            for m in range(ME):
                start += skip(at, ("XC'", m)) + [xs[m]]
                at = W["XC'", m] + 1
            start += (convs + silus + skip(at, ("PROJ'", 0)) + project(0, 0) + sizes01 + broadcast(0, 0, 0) + products[:2])
            run_for(name, eng, start + window(0, 0, before=False) + window(1, 1))
            with eng.Fori(1, NB - 1) as b:
                run_for(name, eng, window(2 * b, 0) + window(2 * b + 1, 1))
            run_for(name, eng, window(NCH - 2, 0) + window(NCH - 1, 1, following=False))
            matmuls, adds = project_out(NCH - 1, 1, NCH)
            run_for(name, eng, finish(NCH - 1, 1)[2:] + matmuls + adds)

        block = c.enter_context(nc.Block())
        assert ME == TC and TAPS <= CH

        @block.sync
        def _(eng):
            loads = [(w_in[:, :, :], io["mb_w_in"].rearrange("(k p) n -> p k n", p=P)),
                     (w_x[:, :, :], io["mb_w_x"].rearrange("(m p) n -> p m n", p=P)),
                     (w_dt[:, :], io["mb_wdt"]),
                     (w_out[:, :, :], io["mb_w_out"].rearrange("(m p) n -> p m n", p=P)),
                     (a_neg[:, :, :], io["mb_A_log"].rearrange("(m p) n -> p m n", p=P)),
                     (conv_w[:, :, :], io["mb_conv_w"].rearrange("(m p) j -> p m j", p=P))]
            for dst, name in ((conv_b, "mb_conv_b"), (b_dt, "mb_b_dt"), (skip, "mb_D")):
                loads.append((dst[:, :], io[name].rearrange("(m p) -> p m", p=P)))
            with nc.allow_non_contiguous_dma(reason="a few numbers to a partition"):
                for dst, src in loads:
                    eng.dma_start(dst, src).then_inc(s_in, 16)
        ALL_IN = 16 * 9

        @block.gpsimd
        def _(eng):
            eng.wait_ge(s_c, 1)
            for n, lo in enumerate((0, LO)):
                nc.gpsimd.affine_select(out=pick[:, :], in_=pick[:, :], compare_op=ALU.not_equal, fill=1.0,
                                        base=-(lo + RANK), pattern=[[-1, 2 * NST]], channel_multiplier=1).then_inc(s_sel, 1)
                eng.wait_ge(s_sel, n + 1)
            emit("gpsimd", eng)

        @block.vector
        def _(eng):
            nc.vector.memset(pick[:, :], 0.0)
            for q in range(2):
                nc.vector.memset(decay[q][:, :, 0], 0.0)
            nc.vector.memset(rests[0][:, :], 0.0)
            eng.drain().then_inc(s_c, 1)
            eng.wait_ge(s_c, 1)
            nc.vector.tensor_copy(proj_hl[:, :], rests[0][0:LO + NPROJ, :]).then_inc(s_a, 1)
            eng.wait_ge(s_in, ALL_IN)
            eng.wait_ge(s_sel, 2)
            nc.vector.tensor_copy(spread[:, :], pick[:, :]).then_inc(s_a, 1)
            eng.wait_ge(s_c, 2)
            nc.vector.tensor_scalar(a_neg[:, :, :], a_neg[:, :, :], -1.0, None, ALU.mult).then_inc(s_a, 1)
            eng.wait_ge(s_a, 3)
            emit("vector", eng)

        @block.scalar
        def _(eng):
            eng.wait_ge(s_in, ALL_IN)
            eng.wait_ge(s_c, 1)
            nc.scalar.activation(a_neg[:, :, :], a_neg[:, :, :], ACT.Exp).then_inc(s_c, 1)
            eng.wait_ge(s_a, 3)
            emit("scalar", eng)

        @block.tensor
        def _(eng):
            eng.wait_ge(s_in, ALL_IN)
            eng.wait_ge(s_a, 3)
            emit("tensor", eng)


def context_glu(K):
    nc, io, R = K.nc, K.io, K.resid
    with ExitStack() as c:
        ln = LayerNormFront(K, c, "cg")
        sb = lambda n, s, d=F32: K.sb(c, f"cg_{n}", s, d)
        sem = lambda n: K.sem(c, f"cg_{n}")
        ctxT = sb("ctxT", [P, NB, KD, CTX])
        ctx_rows = sb("ctx_rows", [CTX, NB, D])
        ctxT_now = [sb(f"ctxT_now{p}", [P, KD, CTX]) for p in range(2)]
        gelu_h = [sb(f"gelu_h{p}", [CTX, CH]) for p in range(2)]
        gT = [sb(f"gT{p}", [CTX, CH]) for p in range(2)]
        pH = [K.ps(c, f"cg_pH{p}", [CTX, CH]) for p in range(2)]
        pO = K.ps(c, "cg_pO", [P, TC, D])
        s_in, s_now, s_h, s_gelu, s_g, s_o, s_res = (
            sem(n) for n in ("in", "now", "h", "gelu", "g", "o", "res"))
        block = c.enter_context(nc.Block())

        @block.sync
        def _(eng):
            eng.dma_start(ctxT[:, :, :, :], io["ctxT"].rearrange("b (k p) s -> p b k s", p=P)).then_inc(s_in, 16)
            eng.dma_start(ctx_rows[:, :, :], io["ctx"].rearrange("b s d -> s b d")).then_inc(s_in, 16)

        @block.gpsimd
        def _(eng):
            def front(i, p):
                ln.gpsimd(eng, i, p)
                free(eng, s_h, i, 1)
                b = i // CPB
                nc.gpsimd.tensor_copy(ctxT_now[p][:, :, :], ctxT[:, bass.ds(b, 1), :, :].rearrange("p a k s -> p (a k) s")
                                      ).then_inc(s_now, 1)
            eng.wait_ge(s_in, 32)
            chunks(eng, NCH, nothing, front, nothing)

        @block.vector
        def _(eng):
            def tail(i, p):
                after(eng, s_gelu, i, 1)
                free(eng, s_o, i, 1)
                nc.vector.tensor_tensor(gT[p][:, :], gelu_h[p][:, :], pH[p][:, :], ALU.mult).then_inc(s_g, 1)
                after(eng, s_o, i, 1)
                nc.vector.tensor_tensor(rows(R, i), rows(R, i), pO[:, :, :], ALU.add).then_inc(s_res, 1)
            chunks(eng, NCH, nothing, lambda i, p: ln.vector(eng, i, p), tail)

        @block.scalar
        def _(eng):
            def mid(i, p):
                after(eng, s_h, i, 1)
                free(eng, s_g, i, 1)
                nc.scalar.activation(gelu_h[p][:, :], pH[p][:, :], ACT.Gelu).then_inc(s_gelu, 1)
            chunks(eng, NCH, mid, lambda i, p: ln.scalar(eng, i, p, s_h, 1), nothing)

        @block.tensor
        def _(eng):
            def mid(i, p):
                after(eng, ln.s_xnT, i, KD)
                after(eng, s_now, i, 1)
                free(eng, s_g, i, 1)
                for k in range(KD):
                    last = nc.tensor.matmul(pH[p][:, :], ctxT_now[p][:, k, :], ln.xnT[p][:, k, :],
                                            start=(k == 0), stop=(k == KD - 1))
                last.then_inc(s_h, 1)

            def tail(i, p):
                after(eng, s_g, i, 1)
                free(eng, s_res, i, 1, back=1)
                for t in range(TC):
                    last = nc.tensor.matmul(pO[:, t, :], gT[p][:, t * P:(t + 1) * P],
                                            ctx_rows[:, bass.ds(i // CPB, 1), :].rearrange("s a d -> s (a d)"),
                                            start=True, stop=True)
                last.then_inc(s_o, 1)
            eng.wait_ge(s_in, 32)
            chunks(eng, NCH, mid, lambda i, p: ln.tensor(eng, i, p), tail)


class Chain:

    def __init__(self, eng, sem, i, size):
        self.eng, self.sem, self.i, self.size, self.n = eng, sem, i, size, 0

    def do(self, ins):
        self.n += 1
        ins.then_inc(self.sem, 1)
        after(self.eng, self.sem, self.i, self.size or 0, self.n)

    def done(self):
        assert self.n == self.size


def top1_experts(K):
    nc, io, R = K.nc, K.io, K.resid
    NE = io["t1_w"].shape[0]
    HALF = NE // 2
    with ExitStack() as c:
        ln = LayerNormFront(K, c, "t1")
        sb = lambda n, s, d=F32: K.sb(c, f"t1_{n}", s, d)
        sem = lambda n: K.sem(c, f"t1_{n}")
        router = sb("router", [P, KD, NE])
        router_b = sb("router_b", [P, NE])
        w = sb("w", [P, KD, NE, D])
        b = sb("b", [NE, D])
        logit = sb("logit", [P, TC, NE])
        top = sb("top", [P, TC])
        shifted = sb("shifted", [P, TC, NE])
        e = sb("e", [P, TC, NE])
        total = sb("total", [P, TC])
        gate = sb("gate", [P, TC])
        best = sb("best", [P, TC, 8])
        index = sb("index", [P, TC, 8], U32)
        index_f = sb("index_f", [P, TC])
        send = [sb(f"send{p}", [P, TC, NE]) for p in range(2)]
        sendT = [sb(f"sendT{p}", [NE, CH]) for p in range(2)]
        pY = [K.ps(c, f"t1_pY{h}", [P, HALF, D]) for h in range(2)]
        pB = K.ps(c, "t1_pB", [P, D])
        pS = K.ps(c, "t1_pS", [P, CH])
        logits_ps = pS[:, 0:TC * NE].rearrange("p (t e) -> p t e", e=NE)
        bias_ps = pB[:, :]
        s_in, s_lg, s_v, s_e, s_send, s_sT, s_sTc, s_b, s_badd, s_y, s_comb, s_acc = (
            sem(n) for n in ("in", "lg", "v", "e", "send", "sT", "sTc", "b", "badd", "y", "comb", "acc"))
        block = c.enter_context(nc.Block())
        G = 2 * TC
        ALL_IN = 16 * (3 + KD)

        @block.sync
        def _(eng):
            eng.dma_start(router[:, :, :], io["t1_router"].rearrange("(k p) e -> p k e", p=P)).then_inc(s_in, 16)
            eng.dma_start(router_b[:, :], io["t1_router_b"].partition_broadcast(P)).then_inc(s_in, 16)
            eng.dma_start(b[:, :], io["t1_b"]).then_inc(s_in, 16)
            for k in range(KD):
                eng.dma_start(w[:, k, :, :], io["t1_w"][:, k * P:(k + 1) * P, :].rearrange("e p d -> p e d")).then_inc(s_in, 16)

        def front(i, p):
            return ([("vector", lambda eng: ln.statistics(eng, i, p)), ("gpsimd", lambda eng: ln.gpsimd(eng, i, p))],
                    [("vector", lambda eng: ln.normalise(eng, i, p))],
                    [("tensor", lambda eng: ln.tensor(eng, i, p)), ("scalar", lambda eng: ln.scalar(eng, i, p, s_y, G))])

        def route(i, p):
            def logits(eng):
                after(eng, ln.s_xnT, i, KD)
                free(eng, s_sTc, i, 1, back=1)
                for t in range(TC):
                    for k in range(KD):
                        last = nc.tensor.matmul(logits_ps[:, t, :], ln.xnT[p][:, k, t * P:(t + 1) * P], router[:, k, :],
                                                start=(k == 0), stop=(k == KD - 1))
                last.then_inc(s_lg, 1)

            def shift(eng):
                after(eng, s_lg, i, 1)
                ch = Chain(eng, s_v, i, 8)
                ch.do(nc.vector.tensor_tensor(logit[:, :, :], logits_ps,
                                              router_b[:, :].unsqueeze(1).to_broadcast([P, TC, NE]), ALU.add))
                ch.do(nc.vector.tensor_reduce(top[:, :], logit[:, :, :], axis=AX.X, op=ALU.max))
                nc.vector.tensor_tensor(shifted[:, :, :], logit[:, :, :],
                                        top[:, :].unsqueeze(2).to_broadcast([P, TC, NE]), ALU.subtract).then_inc(s_v, 1)

            def exp(eng):
                after(eng, s_v, i, 8, 3)
                nc.scalar.activation(e[:, :, :], shifted[:, :, :], ACT.Exp).then_inc(s_e, 1)

            def choose(eng):
                ch = Chain(eng, s_v, i, 8)
                ch.n = 3
                after(eng, s_e, i, 1)
                ch.do(nc.vector.tensor_reduce(total[:, :], e[:, :, :], axis=AX.X, op=ALU.add))
                ch.do(nc.vector.reciprocal(gate[:, :], total[:, :]))
                eng.sem_inc(K.held_vector)
                for t in range(TC):
                    last = nc.vector.max(best[:, t, :], e[:, t, :])
                ch.do(last)
                eng.sem_inc(K.held_vector)
                for t in range(TC):
                    last = nc.vector.max_index(index[:, t, :], best[:, t, :], e[:, t, :])
                ch.do(last)
                ch.do(nc.vector.tensor_copy(index_f[:, :], index[:, :, 0]))
                free(eng, s_sT, i, 1)
                for t in range(TC):
                    nc.vector.tensor_scalar(send[p][:, t, :], K.iota8[:, :], index_f[:, t:t + 1], gate[:, t:t + 1],
                                            ALU.is_equal, ALU.mult).then_inc(s_send, 1)
                ch.done()

            def turn(eng):
                after(eng, s_send, i, TC)
                for t in range(TC):
                    last = nc.tensor.transpose(pS[0:NE, t * P:(t + 1) * P], send[p][:, t, :], K.ident[:, :])
                last.then_inc(s_sT, 1)

            def copy(eng):
                after(eng, s_sT, i, 1)
                free(eng, s_b, i, TC)
                nc.scalar.copy(sendT[p][:, :], pS[0:NE, :]).then_inc(s_sTc, 1)
            return [("tensor", logits)], [("vector", shift), ("scalar", exp)], [("vector", choose)], [("tensor", turn), ("scalar", copy)]

        def bias(i, p, t):
            def pe(eng):
                if t == 0:
                    after(eng, s_sTc, i, 1)
                if t > 0 or n_positive(i):
                    eng.wait_ge(s_badd, i * TC + t)
                nc.tensor.matmul(bias_ps, sendT[p][:, t * P:(t + 1) * P], b[:, :], start=True, stop=True).then_inc(s_b, 1)

            def dve(eng):
                row = R[:, bass.ds(i * TC + t, 1), :].rearrange("p a d -> p (a d)")
                after(eng, s_b, i, TC, t + 1)
                nc.vector.tensor_tensor(row, row, bias_ps, ALU.add).then_inc(s_badd, 1)
                after(eng, s_badd, i, TC, t + 1)
            return [("tensor", pe), ("vector", dve)]

        def group(i, p, t, h):
            n = 2 * t + h

            def pe(eng):
                if n >= 2 or n_positive(i):
                    eng.wait_ge(s_comb, i * G + n - 1)
                for k in range(KD):
                    for q in range(HALF // 2):
                        last = nc.tensor.matmul(pY[h][:, 2 * q:2 * q + 2, :], ln.xnT[p][:, k, t * P:(t + 1) * P],
                                                w[:, k, h * HALF + 2 * q:h * HALF + 2 * q + 2, :],
                                                start=(k == 0), stop=(k == KD - 1))
                last.then_inc(s_y, 1)

            def dve(eng):
                row = R[:, bass.ds(i * TC + t, 1), :].rearrange("p a d -> p (a d)")
                after(eng, s_y, i, G, n + 1)
                for j in range(HALF):
                    ins = nc.vector.scalar_tensor_tensor(row, pY[h][:, j, :], send[p][:, t, h * HALF + j:h * HALF + j + 1],
                                                         row, ALU.mult, ALU.add)
                    if j < HALF - 1:
                        ins.then_inc(s_acc, 1)
                        after(eng, s_acc, i, G * (HALF - 1), n * (HALF - 1) + j + 1)
                ins.then_inc(s_comb, 1)
                after(eng, s_comb, i, G, n + 1)
            return [("tensor", pe), ("vector", dve)]

        def step(i, p, more=True):
            between = [[] for _ in range(G)]
            if more:
                between[0], between[1], between[2] = front(i + 1, 1 - p)
                between[3], between[4], between[5], between[7] = route(i + 1, 1 - p)
            ops = []
            for n in range(G):
                if n % 2 == 0:
                    ops.append(bias(i, p, n // 2))
                ops += [group(i, p, n // 2, n % 2), between[n]]
            return ops

        def emit(name, eng):
            run_for(name, eng, list(front(0, 0)) + list(route(0, 0)) + step(0, 0))
            with eng.Fori(1, NCH // 2) as j:
                run_for(name, eng, step(2 * j - 1, 1) + step(2 * j, 0))
            run_for(name, eng, step(NCH - 1, 1, more=False))

        @block.gpsimd
        def _(eng):
            emit("gpsimd", eng)

        @block.vector
        def _(eng):
            eng.wait_ge(s_in, ALL_IN)
            emit("vector", eng)

        @block.scalar
        def _(eng):
            emit("scalar", eng)

        @block.tensor
        def _(eng):
            eng.wait_ge(s_in, ALL_IN)
            emit("tensor", eng)


def self_attention(K):
    with ExitStack() as c:
        q_rows, k_rows = (K.sb(c, f"sa_{n}_rows", [P, NT, D]) for n in ("q", "k"))
        v_dram = K.nc.dram_tensor("sa_v_dram", [TOK, D], F32).ap()
        _project_qkv(K, q_rows, k_rows, v_dram)
        _attend(K, q_rows, k_rows, v_dram)


def _project_qkv(K, q_rows, k_rows, v_dram):
    nc, io = K.nc, K.io
    with ExitStack() as c:
        ln = LayerNormFront(K, c, "qk")
        sb = lambda n, s, d=F32: K.sb(c, f"qk_{n}", s, d)
        sem = lambda n: K.sem(c, f"qk_{n}")
        w = sb("w", [P, KD, 3, D])
        v_rows = [sb(f"v_rows{p}", [P, TC, D]) for p in range(2)]
        pQK = [K.ps(c, f"qk_pQK{q}", [P, 2, D]) for q in range(2)]
        pV = [K.ps(c, f"qk_pV{q}", [P, D]) for q in range(2)]
        s_in, s_mm, s_q, s_v = (sem(n) for n in ("in", "mm", "q", "v"))
        s_out = [sem(f"out{p}") for p in range(2)]
        block = c.enter_context(nc.Block())

        @block.sync
        def _(eng):
            for n, name in enumerate(("sa_wqT", "sa_wkT", "sa_wvT")):
                eng.dma_start(w[:, :, n, :], io[name].rearrange("(k p) n -> p k n", p=P)).then_inc(s_in, 16)

            def tail(i, p):
                after(eng, s_v, i, TC)
                eng.dma_start(v_dram[bass.ds(i * CH, CH), :].rearrange("(t p) d -> p t d", p=P), v_rows[p][:, :, :]
                              ).then_inc(s_out[p], 16)
            chunks(eng, NCH, nothing, nothing, tail)
            for p in range(2):
                eng.wait_ge(s_out[p], 16 * (NCH // 2))

        def front(i, p):
            return ([("vector", lambda eng: ln.statistics(eng, i, p)), ("gpsimd", lambda eng: ln.gpsimd(eng, i, p))],
                    [("vector", lambda eng: ln.normalise(eng, i, p))],
                    [("tensor", lambda eng: ln.tensor(eng, i, p)), ("scalar", lambda eng: ln.scalar(eng, i, p, s_mm, TC))])

        def project(i, p, t):
            n = i * TC + t

            def pe(eng):
                if t == 0:
                    after(eng, ln.s_xnT, i, KD)
                if t >= 2 or n_positive(i):
                    eng.wait_ge(s_q, 2 * n - 2)
                    eng.wait_ge(s_v, n - 1)
                for k in range(KD):
                    nc.tensor.matmul(pQK[t % 2][:, :, :], ln.xnT[p][:, k, t * P:(t + 1) * P], w[:, k, 0:2, :],
                                     start=(k == 0), stop=(k == KD - 1))
                for k in range(KD):
                    last = nc.tensor.matmul(pV[t % 2][:, :], ln.xnT[p][:, k, t * P:(t + 1) * P], w[:, k, 2, :],
                                            start=(k == 0), stop=(k == KD - 1))
                last.then_inc(s_mm, 1)

            def dve(eng):
                after(eng, s_mm, i, TC, t + 1)
                nc.vector.tensor_scalar(q_rows[:, bass.ds(n, 1), :].rearrange("p a d -> p (a d)"),
                                        pQK[t % 2][:, 0, :], 0.25, None, ALU.mult).then_inc(s_q, 1)
                nc.vector.tensor_copy(k_rows[:, bass.ds(n, 1), :].rearrange("p a d -> p (a d)"),
                                      pQK[t % 2][:, 1, :]).then_inc(s_q, 1)

            def act(eng):
                if t == 0 and (not isinstance(i, int) or i >= 2):
                    eng.wait_ge(s_out[p], (i // 2) * 16)
                after(eng, s_mm, i, TC, t + 1)
                nc.scalar.copy(v_rows[p][:, t, :], pV[t % 2][:, :]).then_inc(s_v, 1)
            return [("tensor", pe), ("vector", dve), ("scalar", act)]

        def step(i, p, more=True):
            ahead = front(i + 1, 1 - p) if more else ([], [], [])
            tile = [project(i, p, t) for t in range(TC)]
            return [ahead[0], tile[0], ahead[1], tile[1], tile[2], ahead[2], tile[3]]

        def emit(name, eng):
            run_for(name, eng, list(front(0, 0)) + step(0, 0))
            with eng.Fori(1, NCH // 2) as j:
                run_for(name, eng, step(2 * j - 1, 1) + step(2 * j, 0))
            run_for(name, eng, step(NCH - 1, 1, more=False))

        @block.gpsimd
        def _(eng):
            emit("gpsimd", eng)

        @block.vector
        def _(eng):
            emit("vector", eng)

        @block.scalar
        def _(eng):
            emit("scalar", eng)

        @block.tensor
        def _(eng):
            eng.wait_ge(s_in, 48)
            emit("tensor", eng)


def _attend(K, q_rows, k_rows, v_dram):
    nc, io, R = K.nc, K.io, K.resid
    HD = 16
    C16 = D // HD
    NPOS = P // 2 * C16
    QB = NPOS // P
    PARTS = 4 * HD
    NEG = -3e38
    HALF = NPOS // 2
    with ExitStack() as c:
        sb = lambda n, s, d=F32: K.sb(c, f"at_{n}", s, d)
        sem = lambda n: K.sem(c, f"at_{n}")
        wo = sb("wo", [P, KD, D])
        ident_bf = sb("ident_bf", [P, P], BF16)
        mask_q = sb("mask_q", [P, P], BF16)
        mask_k = sb("mask_k", [P, P], BF16)
        zero_bf = sb("zero_bf", [P, 32], BF16)
        pick = sb("pick", [P, 2, HD + 1])
        qk_hl = [sb(f"qk_hl{p}", [P, C16, 2, 2, 2, HD], F32R) for p in range(2)]
        qT = [sb(f"qT{p}", [PARTS + 2, 2, NPOS], F32R) for p in range(2)]
        kT = [sb(f"kT{p}", [PARTS + 2, 2, NPOS], F32R) for p in range(2)]
        ones = sb("ones", [P, 2 * NPOS])
        nm_of = sb("nm_of", [P, 2, 2, QB])
        nm = sb("nm", [P, 2, QB])
        nm_hl = sb("nm_hl", [P, 2, 2, QB], F32R)
        nmT = [sb(f"nmT{p}", [4 * QB, P], F32R) for p in range(2)]
        v = [sb(f"v{p}", [P, 2, QB, 32]) for p in range(2)]
        e = [sb(f"e{g}", [P, 2, 512]) for g in range(4)]
        NE = len(e)
        R32 = HALF // C16
        o_sb = sb("o_sb", [P, C16, 2, R32])
        inv = sb("inv", [P, 2, C16 // 2])
        wei = sb("wei", [P, 2, C16 // 2, HD])
        weiT = sb("weiT", [P, 2, 2, P // 2])
        pF = [K.ps(c, f"at_pF{q}", [P, 512]) for q in range(2)]
        pS = [K.ps(c, f"at_pS{q}", [P, 512]) for q in range(2)]
        pE = [K.ps(c, f"at_pE{a}", [P, 512]) for a in range(2)]
        pO = [K.ps(c, f"at_pO{q}", [P, 512]) for q in range(2)]
        (s_in, s_c, s_c2, s_hl, s_t, s_qT, s_kT, s_sc, s_max, s_nm, s_nmT, s_nmc, s_st, s_ex, s_pv, s_ob0, s_ob1,
         s_bk, s_inv, s_wei, s_wT, s_wTc, s_f, s_res) = (sem(n) for n in (
             "in", "c", "c2", "hl", "t", "qTs", "kTs", "sc", "max", "nms", "nmTs", "nmc", "st", "ex", "pv", "ob0", "ob1",
             "bk", "invs", "weis", "wT", "wTc", "f", "res"))
        s_row = [sem(f"row{p}") for p in range(2)]
        s_v = [sem(f"v{p}s") for p in range(2)]
        flat = lambda a: a.rearrange("p a d -> p (a d)")

        S_ITEMS = [(a, qb, w0, min((qb + 1) * P, w0 + 512)) for qb in range(QB) for a in range(2)
                   for w0 in range(0, (qb + 1) * P, 512)]
        NS = len(S_ITEMS)
        width = lambda hf, kb: min(HALF, HALF * (hf + 1) - kb * P)
        SLOTS = [[(1, 0)], [(1, 1)], [(1, 2)], [(1, 3)], [(0, 0)], [(0, 1), (0, 3)], [(1, 4)], [(1, 5), (1, 7)], [(0, 2), (1, 6)]]
        NG = len(SLOTS)
        assert all(sum(width(*x) for x in s) == 512 for s in SLOTS)
        acc_of = lambda hf, kb: {(0, 3): 0, (1, 7): 0, (1, 6): 1}.get((hf, kb), kb % 2)
        LAST = {(hf, acc_of(hf, kb)): (hf, kb) for s in SLOTS for hf, kb in s}
        FIRST = {}
        for s in SLOTS:
            for hf, kb in s:
                FIRST.setdefault((hf, acc_of(hf, kb)), (hf, kb))

        def front(i, p):
            transposes, items = [], []

            def split(eng):
                if not isinstance(i, int) or i >= 2:
                    eng.wait_ge(s_t, 4 * i - 4)
                both_of = lambda rows_: flat(rows_[:, bass.ds(i, 1), :]).rearrange("p (c d) -> p c d", d=HD
                                                                                    ).unsqueeze(2).to_broadcast([P, C16, 2, HD])
                q_part = lambda x: qk_hl[p][:, :, 0, :, x, :]
                k_part = lambda x: qk_hl[p][:, :, 1, x, :, :]
                nc.gpsimd.tensor_copy(q_part(0), both_of(q_rows)).then_inc(s_hl, 1)
                nc.gpsimd.tensor_copy(k_part(0), both_of(k_rows)).then_inc(s_hl, 1)
                after(eng, s_hl, i, 4, 1)
                eng.sem_inc(K.held_pool)
                nc.gpsimd.tensor_tensor(q_part(1), both_of(q_rows), q_part(0).bitcast(F32), ALU.subtract).then_inc(s_hl, 1)
                after(eng, s_hl, i, 4, 2)
                eng.sem_inc(K.held_pool)
                nc.gpsimd.tensor_tensor(k_part(1), both_of(k_rows), k_part(0).bitcast(F32), ALU.subtract).then_inc(s_hl, 1)

            def load_v(eng):
                if not isinstance(i, int) or i >= 2:
                    eng.wait_ge(s_pv, NG * (i - 1))
                for a in range(2):
                    src = v_dram[bass.ds(i * P + a * (P // 2), P // 2), :].rearrange("(kb r) (c d) -> (r c) kb d", r=P // C16, d=HD)
                    eng.dma_start(v[p][:, a, :, 0:HD], src).then_inc(s_v[p], 16)

            def group(g):
                bank = pF[g % 2]

                def pe(eng):
                    if g == 0:
                        after(eng, s_hl, i, 4)
                        if n_positive(i):
                            eng.wait_ge(s_nmc, i)
                    if g == 1:
                        if not isinstance(i, int) or i >= 3:
                            eng.wait_ge(s_res, i - 2)
                    if g or n_positive(i):
                        eng.wait_ge((s_qT, s_kT)[g % 2], i * 4 + (2 if g >= 2 else 0))
                        eng.sem_inc(K.held_tensor)
                    for cc in range(4):
                        col = qk_hl[p][:, 4 * g + cc, :, :, :, :].rearrange("p w x y d -> p (w x y d)").bitcast(F32)
                        last = nc.tensor.transpose(bank[:, cc * P:(cc + 1) * P], col, K.ident[:, :])
                    last.then_inc(s_t, 1)

                def out(T):
                    return T[0:PARTS, :, :].rearrange("x a (r c) -> x c a r", c=C16)[:, 4 * g:4 * g + 4, :, :]

                def leave(eng, copy, signal):
                    if g < 2 and (not isinstance(i, int) or i >= 2):
                        eng.wait_ge(s_st, 2 * NG * (i - 1))
                    after(eng, s_t, i, 4, g + 1)
                    for n, T in enumerate((qT[p], kT[p])):
                        copy(out(T), bank[n * PARTS:(n + 1) * PARTS, :].rearrange("x (c a r) -> x c a r", c=4, a=2)).then_inc(signal, 1)
                by = (("scalar", lambda eng: leave(eng, nc.scalar.copy, s_qT)), ("vector", lambda eng: leave(eng, nc.vector.tensor_copy, s_kT)))[g % 2]
                transposes.append([("tensor", pe), by])
            for g in range(4):
                group(g)

            def item(s):
                a, qb, w0, w1 = S_ITEMS[s]
                diag = w1 == (qb + 1) * P

                def pe(eng):
                    if s == 0:
                        after(eng, s_qT, i, 4)
                        after(eng, s_kT, i, 4)
                    if s >= 2 or n_positive(i):
                        eng.wait_ge(s_max, i * NS + s - 1)
                    last = nc.tensor.matmul(pS[s % 2][:, 0:w1 - w0], qT[p][0:PARTS, a, qb * P:(qb + 1) * P],
                                            kT[p][0:PARTS, a, w0:w1], start=True, stop=not diag)
                    if diag:
                        last = nc.tensor.matmul(pS[s % 2][:, w1 - w0 - P:w1 - w0], ident_bf[:, :], mask_q[:, :],
                                                start=False, stop=True)
                    last.then_inc(s_sc, 1)

                def dve(eng):
                    after(eng, s_sc, i, NS, s + 1)
                    nc.vector.tensor_reduce(nm_of[:, w0 // 512, a, qb:qb + 1], pS[s % 2][:, 0:w1 - w0], axis=AX.X,
                                            op=ALU.max, negate=True).then_inc(s_max, 1)
                items.append([("tensor", pe), ("vector", dve)])
            for s in range(NS):
                item(s)

            def parts_of_max(eng):
                after(eng, s_max, i, NS)
                if n_positive(i):
                    eng.wait_ge(s_nmT, i)
                nc.vector.tensor_tensor(nm[:, :, :], nm_of[:, 0, :, :], nm_of[:, 1, :, :], ALU.min).then_inc(s_nm, 1)
                after(eng, s_nm, i, 3, 1)
                nc.vector.tensor_copy(nm_hl[:, 0, :, :], nm[:, :, :]).then_inc(s_nm, 1)
                after(eng, s_nm, i, 3, 2)
                nc.vector.tensor_tensor(nm_hl[:, 1, :, :], nm[:, :, :], nm_hl[:, 0, :, :].bitcast(F32), ALU.subtract).then_inc(s_nm, 1)

            def pe_max(eng):
                after(eng, s_nm, i, 3)
                if not isinstance(i, int) or i >= 2:
                    eng.wait_ge(s_wei, i - 1)
                nc.tensor.transpose(pF[0][0:4 * QB, 0:P], nm_hl[:, :, :, :].rearrange("p x a b -> p (x a b)").bitcast(F32), K.ident[:, :]).then_inc(s_nmT, 1)

            def act_max(eng):
                if not isinstance(i, int) or i >= 2:
                    eng.wait_ge(s_row[p], (i // 2) * 32)
                after(eng, s_nmT, i, 1)
                nc.scalar.copy(nmT[p][:, :], pF[0][0:4 * QB, 0:P]).then_inc(s_nmc, 1)

            def move_max(eng):
                after(eng, s_nmc, i, 1)
                for part in range(2):
                    eng.dma_start(qT[p][PARTS + part:PARTS + part + 1, :, :].bitcast(F32).rearrange("o a (b q) -> o (a b) q", q=P),
                                  nmT[p][part * 2 * QB:(part + 1) * 2 * QB, :].bitcast(F32)).then_inc(s_row[p], 16)
            maxima = [("vector", parts_of_max), ("tensor", pe_max), ("scalar", act_max), ("sync", move_max)]
            return [("gpsimd", split)], [("sync", load_v)], transposes, items, maxima

        def tail(i, p):
            def scores(g, a):
                def pe(eng):
                    if g == 0 and a == 0:
                        eng.wait_ge(s_row[p], (i // 2) * 32 + 32)
                    if g or n_positive(i):
                        eng.wait_ge(s_ex, (i * NG + g) * 2 + a - 1)
                    at = 0
                    for n, (hf, kb) in enumerate(SLOTS[g]):
                        w = width(hf, kb)
                        diag = kb * P >= hf * HALF
                        q0 = HALF * (hf + 1) - w
                        last = nc.tensor.matmul(pE[a][:, at:at + w], kT[p][:, a, kb * P:(kb + 1) * P],
                                                qT[p][:, a, q0:q0 + w], start=(n == 0), stop=not diag, skip_group_check=True)
                        if diag:
                            last = nc.tensor.matmul(pE[a][:, at:at + P], ident_bf[:, :], mask_k[:, :],
                                                    start=False, stop=True, skip_group_check=True)
                        at += w
                    last.then_inc(s_st, 1)

                def act(eng):
                    after(eng, s_st, i, 2 * NG, 2 * g + a + 1)
                    if g >= NE or n_positive(i):
                        eng.wait_ge(s_pv, i * NG + g - NE + 1)
                    nc.scalar.activation(e[g % NE][:, a, :], pE[a][:, :], ACT.Exp).then_inc(s_ex, 1)
                return [("tensor", pe), ("scalar", act)]

            def product(g):
                def pe(eng):
                    if g == 0:
                        eng.wait_ge(s_v[p], (i // 2) * 32 + 32)
                        if n_positive(i):
                            eng.wait_ge(s_ob0, i)
                            eng.wait_ge(s_ob1, i)
                    after(eng, s_ex, i, 2 * NG, 2 * g + 2)
                    at = 0
                    for hf, kb in SLOTS[g]:
                        w = width(hf, kb)
                        for a in range(2):
                            acc = acc_of(hf, kb)
                            j = 2 * a + acc
                            first, final = FIRST[hf, acc] == (hf, kb), LAST[hf, acc] == (hf, kb)
                            last = nc.tensor.matmul(pO[hf][32 * j:32 * j + 32, HALF - w:HALF], v[p][:, a, kb, :],
                                                    e[g % NE][:, a, at:at + w], start=first, stop=final, skip_group_check=True)
                            if first and w < HALF:
                                last = nc.tensor.matmul(pO[hf][32 * j:32 * j + 32, 0:HALF - w], zero_bf[:, :],
                                                        ident_bf[:, 0:HALF - w], start=False, stop=True, skip_group_check=True)
                        at += w
                    last.then_inc(s_pv, 1)
                return [("tensor", pe)]
            return [scores(g, 0) + scores(g, 1) for g in range(NG)], [product(g) for g in range(NG)]

        def result(i, fronts):
            def act_o(eng):
                after(eng, s_pv, i, NG)
                if n_positive(i):
                    eng.wait_ge(s_bk, i)
                nc.scalar.copy(o_sb[:, :, 0, :].rearrange("x c r -> x r c"), pO[0][:, :].rearrange("x (r c) -> x r c", c=C16)).then_inc(s_ob0, 1)

            def dve_o(eng):
                after(eng, s_pv, i, NG)
                if n_positive(i):
                    eng.wait_ge(s_bk, i)
                nc.vector.tensor_copy(o_sb[:, :, 1, :].rearrange("x c r -> x r c"), pO[1][:, :].rearrange("x (r c) -> x r c", c=C16)).then_inc(s_ob1, 1)

            def pe_back(eng):
                after(eng, s_ob0, i, 1)
                after(eng, s_ob1, i, 1)
                eng.wait_ge(s_qT, 4 * fronts)
                for cp in range(C16 // 2):
                    pair = o_sb[:, 2 * cp:2 * cp + 2, :, :].rearrange("x c f r -> x (c f r)")
                    last = nc.tensor.matmul(pF[0][:, cp * 2 * (HD + 1):(cp + 1) * 2 * (HD + 1)], pair,
                                            pick[:, :, :].rearrange("x a d -> x (a d)"), start=True, stop=True)
                last.then_inc(s_bk, 1)

            def dve_wei(eng):
                back = pF[0][:, 0:C16 * (HD + 1)].rearrange("p (c a d) -> p a c d", a=2, d=HD + 1)
                after(eng, s_bk, i, 1)
                nc.vector.reciprocal(inv[:, :, :], back[:, :, :, HD]).then_inc(s_inv, 1)
                after(eng, s_inv, i, 1)
                if n_positive(i):
                    eng.wait_ge(s_wT, i)
                nc.vector.tensor_tensor(wei[:, :, :, :], back[:, :, :, 0:HD],
                                        inv[:, :, :].unsqueeze(3).to_broadcast([P, 2, C16 // 2, HD]), ALU.mult).then_inc(s_wei, 1)

            def pe_wT(eng):
                after(eng, s_wei, i, 1)
                eng.wait_ge(s_kT, 4 * fronts)
                for a in range(2):
                    last = nc.tensor.transpose(pF[1][:, a * P:(a + 1) * P], wei[:, a, :, :].rearrange("p c d -> p (c d)"), K.ident[:, :])
                last.then_inc(s_wT, 1)

            def act_wT(eng):
                after(eng, s_wT, i, 1)
                if n_positive(i):
                    eng.wait_ge(s_f, i)
                nc.scalar.copy(weiT[:, :, :, :].rearrange("p c a r -> p a c r"), pF[1][:, 0:D].rearrange("p (a c r) -> p a c r", a=2, c=2)).then_inc(s_wTc, 1)

            def pe_f(eng):
                after(eng, s_wTc, i, 1)
                for k in range(KD):
                    last = nc.tensor.matmul(pF[1][:, D:2 * D], weiT[:, k, :, :].rearrange("p a r -> p (a r)"), wo[:, k, :], start=(k == 0), stop=(k == KD - 1))
                last.then_inc(s_f, 1)

            def dve_res(eng):
                after(eng, s_f, i, 1)
                row = flat(R[:, bass.ds(i, 1), :])
                nc.vector.tensor_tensor(row, row, pF[1][:, D:2 * D], ALU.add).then_inc(s_res, 1)
            return ([("scalar", act_o), ("vector", dve_o)], [("tensor", pe_back)], [("vector", dve_wei)], [("tensor", pe_wT), ("scalar", act_wT)],
                    [("tensor", pe_f), ("vector", dve_res)])

        def window(i, p, before=True, following=2):
            E, V = tail(i, p)
            T, S, maxima = [[] for _ in range(4)], [[] for _ in range(NS)], []
            begin = []
            if following:
                _, load_v, _, S, maxima = front(i + 1, 1 - p)
                begin = [load_v]
            if following > 1:
                split, _, T, _, _ = front(i + 2, p)
                begin.append(split)
            leave = back = divide = turn = add = []
            if before:
                leave, back, divide, turn, add = result(i - 1, min(i + 2, NT) if isinstance(i, int) else i + 2)
            order = ([leave, E[0]] + S[0:2] + [E[1]] + S[2:4] + [back, E[2]] + S[4:6] + [V[0], divide] + S[6:8]
                     + [E[3], turn] + S[8:10] + [V[1]] + S[10:12] + [E[4], add] + S[12:14] + [V[2]] + S[14:16]
                     + [E[5], V[3]] + S[16:18] + [E[6]] + S[18:20] + [V[4], E[7]] + S[20:22] + [E[8]] + S[22:24]
                     + [maxima, V[5], T[0], T[1], V[6] + V[7], T[2], T[3], V[8]])
            return begin + order

        def emit(name, eng):
            def run(ops):
                for op in ops:
                    for who, fn in op:
                        if who == name:
                            fn(eng)
            split, load_v, T, S, maxima = front(0, 0)
            next_split, _, next_T, _, _ = front(1, 1)
            run([split, load_v, next_split] + T + S + [maxima] + next_T)
            run(window(0, 0, before=False))
            with eng.Fori(1, NT // 2 - 1) as j:
                run(window(2 * j - 1, 1))
                run(window(2 * j, 0))
            run(window(NT - 3, 1) + window(NT - 2, 0, following=1) + window(NT - 1, 1, following=0))
            run(result(NT - 1, NT))

        block = c.enter_context(nc.Block())

        @block.sync
        def _(eng):
            for k, rows_ in enumerate(io["sa_woT"].rearrange("(cp k d) n -> k cp d n", k=2, d=HD)[k] for k in range(2)):
                for cp in range(C16 // 2):
                    eng.dma_start(wo[cp * HD:(cp + 1) * HD, k, :], rows_[cp]).then_inc(s_in, 16)
            eng.wait_ge(s_c2, 1)
            emit("sync", eng)

        @block.gpsimd
        def _(eng):
            eng.wait_ge(s_c, 1)
            for mask, step, mult in ((mask_q, -1, 1), (mask_k, 1, -1)):
                nc.gpsimd.affine_select(out=mask[:, :], in_=mask[:, :], compare_op=ALU.is_ge, fill=NEG,
                                        base=0, pattern=[[step, P]], channel_multiplier=mult)
            nc.gpsimd.tensor_copy(ident_bf[:, :], K.ident[:, :])
            for par in range(2):
                nc.gpsimd.affine_select(out=pick[:, :, :], in_=pick[:, :, :], compare_op=ALU.not_equal, fill=1.0,
                                        base=-32 * par, pattern=[[-64, 2], [-1, HD + 1]], channel_multiplier=1).then_inc(s_c2, 1)
                eng.wait_ge(s_c2, 1 + par)
            emit("gpsimd", eng)

        @block.vector
        def _(eng):
            nc.vector.memset(mask_q[:, :], 0.0)
            nc.vector.memset(mask_k[:, :], 0.0)
            nc.vector.memset(zero_bf[:, :], 0.0)
            nc.vector.memset(pick[:, :, :], 0.0)
            nc.vector.memset(ones[:, :], 1.0)
            nc.vector.memset(nm_of[:, :, :, :], -NEG)
            for p in range(2):
                nc.vector.memset(v[p][:, :, :, HD:HD + 1], 1.0)
                nc.vector.memset(v[p][:, :, :, HD + 1:32], 0.0)
            eng.drain().then_inc(s_c, 1)
            eng.wait_ge(s_c, 1)
            for p in range(2):
                last = nc.vector.tensor_copy(kT[p][PARTS:PARTS + 2, :, :],
                                             ones[PARTS:PARTS + 2, :].rearrange("x (a l) -> x a l", a=2)).then_inc(s_c, 1)
            emit("vector", eng)

        @block.scalar
        def _(eng):
            emit("scalar", eng)

        @block.tensor
        def _(eng):
            eng.wait_ge(s_in, 16 * C16)
            eng.wait_ge(s_c, 3)
            eng.wait_ge(s_c2, 2)
            emit("tensor", eng)


def cross_attention(K):
    nc, io, R = K.nc, K.io, K.resid
    HD = 16
    NH = D // HD
    HM = P // HD
    HG = HM // 2
    SCALE = float(HD) ** -0.5
    with ExitStack() as c:
        ln = LayerNormFront(K, c, "xa")
        sb = lambda n, s, d=F32: K.sb(c, f"xa_{n}", s, d)
        sem = lambda n: K.sem(c, f"xa_{n}")
        ctxT = sb("ctxT", [P, KD, NB, CTX])
        wq, wk, wv, wo = (sb(n, [P, KD, D]) for n in ("wq", "wk", "wv", "wo"))
        bq, bk = sb("bq", [P, KD]), sb("bk", [P, KD])
        bv, bo = sb("bv", [P, D]), sb("bo", [P, D])
        own = sb("own", [P, HM])
        kT = sb("kT", [P, KD, NB, CTX])
        kdiag = [sb(f"kdiag{m}", [P, NB, HM, CTX]) for m in range(KD)]
        v = sb("v", [CTX, NB, D])
        qT = [sb(f"qT{p}", [P, KD, CH]) for p in range(2)]
        top = [sb(f"top{m}", [P, HM]) for m in range(KD)]
        e = [[sb(f"e{q}{m}", [P, HM, CTX]) for m in range(KD)] for q in range(2)]
        total = sb("total", [P, NH])
        inv = sb("inv", [P, NH])
        eT = [sb(f"eT{q}", [CTX, 4, P]) for q in range(2)]
        mixed = sb("mixed", [P, D])
        mixedT = sb("mixedT", [P, KD, P])
        pS = [K.ps(c, f"xa_pS{m}", [P, 2, 512]) for m in range(KD)]
        pX = K.ps(c, "xa_pX", [P, 512])
        pV = K.ps(c, "xa_pV", [P, D])
        (s_in, s_own, s_kT, s_kTc, s_kd, s_vp, s_vc, s_q, s_qc, s_S, s_top, s_sub, s_exp, s_tot, s_inv, s_eT, s_eTc, s_pv, s_mix,
         s_mT, s_mTc, s_F, s_res, s_bo) = (sem(n) for n in (
             "in", "own", "kTp", "kTc", "kd", "vp", "vc", "q", "qc", "S", "top", "sub", "exp", "tot", "invs", "eTp", "eTc", "pv",
             "mix", "mT", "mTc", "F", "res", "bosum"))
        block = c.enter_context(nc.Block())

        def project_q(i, p):
            ops = []
            for m in range(KD):
                def pe(eng, m=m):
                    if m == 0:
                        after(eng, ln.s_xnT, i, KD)
                        if n_positive(i):
                            eng.wait_ge(s_sub, i * TC * KD)
                    for k in range(KD):
                        last = nc.tensor.matmul(pS[m][:, 0, :], wq[:, k, m * P:(m + 1) * P], ln.xnT[p][:, k, :],
                                                start=(k == 0), stop=(k == KD - 1))
                    last.then_inc(s_q, 1)

                def act(eng, m=m):
                    after(eng, s_q, i, KD, m + 1)
                    if m == 0:
                        free(eng, s_S, i, KD * TC)
                    nc.scalar.activation(qT[p][:, m, :], pS[m][:, 0, :], ACT.Identity, bias=bq[:, m:m + 1]).then_inc(s_qc, 1)
                ops.append([("tensor", pe), ("scalar", act)])
            return ops

        def scores(i, p, t, m):
            n = i * TC + t
            em = e[t % 2][m]

            def pe(eng):
                if t == 0:
                    after(eng, s_qc, i, KD)
                else:
                    eng.wait_ge(s_sub, n * KD - KD + m + 1)
                for g in range(2):
                    last = nc.tensor.matmul(pS[m][:, g, 0:HG * CTX], qT[p][:, m, t * P:(t + 1) * P],
                                            kdiag[m][:, bass.ds(i // CPB, 1), g * HG:(g + 1) * HG, :].rearrange("p a h s -> p (a h s)"),
                                            start=True, stop=True)
                last.then_inc(s_S, 1)

            def dve(eng):
                grouped = lambda T: T.rearrange("p (g h) -> p g h", g=2)
                after(eng, s_S, n, KD, m + 1)
                if n_positive(n):
                    eng.wait_ge(s_sub, n * KD - KD + m + 1)
                of = pS[m][:, :, 0:HG * CTX].rearrange("p g (h s) -> p g h s", s=CTX)
                nc.vector.tensor_reduce(grouped(top[m][:, :]), of, axis=AX.X, op=ALU.max).then_inc(s_top, 1)
                after(eng, s_top, n, KD, m + 1)
                if not isinstance(n, int) or n >= 2:
                    eng.wait_ge(s_eT, (n - 1) * 4)
                    eng.wait_ge(s_tot, n - 1)
                nc.vector.tensor_tensor(em[:, :, :].rearrange("p (g h) s -> p g h s", g=2), of,
                                        grouped(top[m][:, :]).unsqueeze(3).to_broadcast([P, 2, HG, CTX]),
                                        ALU.subtract).then_inc(s_sub, 1)

            def act(eng):
                after(eng, s_sub, n, KD, m + 1)
                nc.scalar.activation(em[:, :, :], em[:, :, :], ACT.Exp, scale=SCALE).then_inc(s_exp, 1)
            return [("tensor", pe), ("vector", dve)], [("scalar", act)]

        def transposes(i, p, t, g, fronts):
            n = i * TC + t
            bank = ln.pT[g % 2]

            def pe(eng):
                after(eng, s_exp, n, KD, g // 2 + 1)
                if g < 2:
                    eng.wait_ge(ln.s_xnT, fronts * KD)
                if g >= 2 or n_positive(n):
                    eng.wait_ge(s_eTc, n * 4 + g - 1)
                for h in range(4):
                    last = nc.tensor.transpose(bank[0:CTX, h * P:(h + 1) * P], e[t % 2][g // 2][:, (g % 2) * 4 + h, :], K.ident[:, :])
                last.then_inc(s_eT, 1)

            def act(eng):
                after(eng, s_eT, n, 4, g + 1)
                if n_positive(n) or g >= 2:
                    eng.wait_ge(s_pv, n * 4 + g - 1)
                nc.scalar.copy(eT[g % 2][:, :, :], bank[0:CTX, :].rearrange("s (h q) -> s h q", q=P)).then_inc(s_eTc, 1)
            return [("tensor", pe), ("scalar", act)]

        def weigh(i, p, t, g):
            n = i * TC + t

            def pe(eng):
                if g == 0 and n_positive(n):
                    eng.wait_ge(s_mix, n)
                after(eng, s_eTc, n, 4, g + 1)
                for h in range(4):
                    hh = g * 4 + h
                    last = nc.tensor.matmul(pV[:, hh * HD:(hh + 1) * HD], eT[g % 2][:, h, :],
                                            v[:, bass.ds(i // CPB, 1), hh * HD:(hh + 1) * HD].rearrange("s a d -> s (a d)"),
                                            start=True, stop=True)
                last.then_inc(s_pv, 1)
            return [("tensor", pe)]

        def sums(i, p, t):
            n = i * TC + t

            def dve(eng):
                after(eng, s_exp, n, KD)
                if n_positive(n):
                    eng.wait_ge(s_inv, n)
                for m in range(KD):
                    ins = nc.vector.tensor_reduce(total[:, m * HM:(m + 1) * HM], e[t % 2][m][:, :, :], axis=AX.X, op=ALU.add)
                ins.then_inc(s_tot, 1)
                after(eng, s_tot, n, 1)
                if n_positive(n):
                    eng.wait_ge(s_mix, n)
                nc.vector.reciprocal(inv[:, :], total[:, :]).then_inc(s_inv, 1)
            return [("vector", dve)]

        def mix(i, p, t):
            n = i * TC + t

            def dve(eng):
                after(eng, s_inv, n, 1)
                after(eng, s_pv, n, 4)
                if n_positive(n):
                    eng.wait_ge(s_mT, n)
                nc.vector.tensor_tensor(mixed[:, :].rearrange("p (h d) -> p h d", d=HD),
                                        pV[:, :].rearrange("p (h d) -> p h d", d=HD),
                                        inv[:, :].unsqueeze(2).to_broadcast([P, NH, HD]), ALU.mult).then_inc(s_mix, 1)
            return [("vector", dve)]

        def project_out(n):
            def pe_turn(eng):
                after(eng, s_mix, n, 1)
                if n_positive(n):
                    eng.wait_ge(s_res, n)
                for k in range(KD):
                    last = nc.tensor.transpose(pX[:, k * P:(k + 1) * P], mixed[:, k * P:(k + 1) * P], K.ident[:, :])
                last.then_inc(s_mT, 1)

            def act(eng):
                after(eng, s_mT, n, 1)
                if n_positive(n):
                    eng.wait_ge(s_F, n)
                nc.scalar.copy(mixedT[:, :, :], pX[:, 0:D].rearrange("p (k q) -> p k q", k=KD)).then_inc(s_mTc, 1)

            def pe(eng):
                after(eng, s_mTc, n, 1)
                for k in range(KD):
                    last = nc.tensor.matmul(pX[:, D:2 * D], mixedT[:, k, :], wo[:, k, :], start=(k == 0), stop=(k == KD - 1))
                last.then_inc(s_F, 1)

            def dve(eng):
                after(eng, s_F, n, 1)
                row = R[:, bass.ds(n, 1), :].rearrange("p a d -> p (a d)")
                nc.vector.tensor_tensor(row, row, pX[:, D:2 * D], ALU.add).then_inc(s_res, 1)

            def pool(eng):
                after(eng, s_res, n, 1)
                row = R[:, bass.ds(n, 1), :].rearrange("p a d -> p (a d)")
                nc.gpsimd.tensor_tensor(row, row, bo[:, :], ALU.add).then_inc(s_bo, 1)
            return [("tensor", pe_turn), ("scalar", act)], [("tensor", pe)], [("vector", dve), ("gpsimd", pool)]

        def front(i, p):
            def pe(eng):
                if n_positive(i):
                    eng.wait_ge(s_eTc, (i - 1) * TC * 4 + 2 * 4)
                ln.tensor(eng, i, p)
            return ([("vector", lambda eng: ln.statistics(eng, i, p)), ("gpsimd", lambda eng: ln.gpsimd(eng, i, p))],
                    [("vector", lambda eng: ln.normalise(eng, i, p))],
                    [("tensor", pe), ("scalar", lambda eng: ln.scalar(eng, i, p, s_q, KD))])

        def window(i, p, t, first=False, last=False):
            n = i * TC + t
            T = [transposes(i, p, t, g, i + 1 if t < 2 or last else i + 2) for g in range(4)]
            V = [weigh(i, p, t, g) for g in range(4)]
            turn, product, add = ([], [], []) if first and t == 0 else project_out(n - 1)
            before, S = [], [[], []]
            exp = [[], []]
            if t + 1 < TC:
                (S[0], exp[0]), (S[1], exp[1]) = (scores(i, p, t + 1, m) for m in range(KD))
            elif not last:
                before = project_q(i + 1, 1 - p)
                (S[0], exp[0]), (S[1], exp[1]) = (scores(i + 1, 1 - p, 0, m) for m in range(KD))
            ahead = []
            if not last and t < 3:
                ahead = [front(i + 1, 1 - p)[t]]
            return (before + (ahead if t == 2 else []) + [T[0], S[0], T[1], turn, V[0], T[2], S[1], exp[0], V[1], sums(i, p, t), T[3], product, V[2], add,
                    exp[1], V[3], mix(i, p, t)] + (ahead if t != 2 else []))

        def emit(name, eng):
            start = front(0, 0)
            (S0, e0), (S1, e1) = (scores(0, 0, 0, m) for m in range(KD))
            run_for(name, eng, list(start) + project_q(0, 0) + [S0, S1, e0, e1])
            for t in range(TC):
                run_for(name, eng, window(0, 0, t, first=True))
            with eng.Fori(1, NCH // 2) as j:
                for i, p in ((2 * j - 1, 1), (2 * j, 0)):
                    for t in range(TC):
                        run_for(name, eng, window(i, p, t))
            for t in range(TC):
                run_for(name, eng, window(NCH - 1, 1, t, last=True))
            run_for(name, eng, project_out(NT - 1))

        @block.sync
        def _(eng):
            for k in range(KD):
                eng.dma_start(ctxT[:, k, :, :], io["ctxT"][:, k * P:(k + 1) * P, :].rearrange("b p s -> p b s")).then_inc(s_in, 16)
            for dst, name in ((wq, "xa_wqT"), (wk, "xa_wkT"), (wv, "xa_wvT"), (wo, "xa_woT")):
                eng.dma_start(dst[:, :, :], io[name].rearrange("(k p) n -> p k n", p=P)).then_inc(s_in, 16)
            with nc.allow_non_contiguous_dma(reason="256 biases, one to a partition"):
                eng.dma_start(bq[:, :], io["xa_bq"].rearrange("(k p) -> p k", p=P)).then_inc(s_in, 16)
                eng.dma_start(bk[:, :], io["xa_bk"].rearrange("(k p) -> p k", p=P)).then_inc(s_in, 16)
            eng.dma_start(bv[:, :], io["xa_bv"].partition_broadcast(P)).then_inc(s_in, 16)
            eng.dma_start(bo[:, :], io["xa_bo"].partition_broadcast(P)).then_inc(s_in, 16)
        ALL_IN = 16 * (KD + 8)

        @block.gpsimd
        def _(eng):
            nc.gpsimd.memset(own[:, :], 1.0).then_inc(s_own, 1)
            eng.wait_ge(s_own, 1)
            nc.gpsimd.affine_select(out=own[:, :], in_=own[:, :], compare_op=ALU.is_ge, fill=0.0, base=0,
                                    pattern=[[-HD, HM]], channel_multiplier=1).then_inc(s_own, 1)
            eng.wait_ge(s_own, 2)
            nc.gpsimd.affine_select(out=own[:, :], in_=own[:, :], compare_op=ALU.is_ge, fill=0.0, base=HD - 1,
                                    pattern=[[HD, HM]], channel_multiplier=-1).then_inc(s_own, 1)

            eng.wait_ge(s_in, ALL_IN)
            emit("gpsimd", eng)

        @block.vector
        def _(eng):
            eng.wait_ge(s_in, ALL_IN)
            eng.wait_ge(s_own, 3)
            for m in range(KD):
                eng.wait_ge(s_kTc, m + 1)
                for h in range(HM):
                    ins = nc.vector.tensor_scalar(kdiag[m][:, :, h, :], kT[:, m, :, :], own[:, h:h + 1], None, ALU.mult)
                ins.then_inc(s_kd, 1)
            for b in range(NB):
                eng.wait_ge(s_vp, b + 1)
                nc.vector.tensor_tensor(v[:, b, :], pV[0:CTX, :], bv[0:CTX, :], ALU.add).then_inc(s_vc, 1)
            emit("vector", eng)

        @block.scalar
        def _(eng):
            eng.wait_ge(s_in, ALL_IN)
            for m in range(KD):
                eng.wait_ge(s_kT, m + 1)
                nc.scalar.activation(kT[:, m, :, :], pX[:, 0:NB * CTX].rearrange("p (b s) -> p b s", s=CTX),
                                     ACT.Identity, bias=bk[:, m:m + 1]).then_inc(s_kTc, 1)
            emit("scalar", eng)

        @block.tensor
        def _(eng):
            eng.wait_ge(s_in, ALL_IN)
            for m in range(KD):
                if m:
                    eng.wait_ge(s_kTc, m)
                for k in range(KD):
                    last = nc.tensor.matmul(pX[:, 0:NB * CTX], wk[:, k, m * P:(m + 1) * P],
                                            ctxT[:, k, :, :].rearrange("p b s -> p (b s)"), start=(k == 0), stop=(k == KD - 1))
                last.then_inc(s_kT, 1)
            for b in range(NB):
                if b:
                    eng.wait_ge(s_vc, b)
                for k in range(KD):
                    last = nc.tensor.matmul(pV[0:CTX, :], ctxT[:, k, b, :], wv[:, k, :], start=(k == 0), stop=(k == KD - 1))
                last.then_inc(s_vp, 1)
            eng.wait_ge(s_kd, KD)
            eng.wait_ge(s_vc, NB)
            emit("tensor", eng)


def top2_experts(K):
    NE = K.io["t2_router"].shape[1]
    with ExitStack() as c:
        h_rows = K.sb(c, "t2_h_rows", [P, NT, D])
        weight = K.sb(c, "t2_weight", [P, NT, TOP])
        chosen = [K.sb(c, f"t2_chosen{k}", [P, NT, NE]) for k in range(TOP)]
        slot = [K.sb(c, f"t2_slot{k}", [P, NT], U32) for k in range(TOP)]
        expert_of = K.sb(c, "t2_expert_of", [P, NST_TILES], I32)
        h_sorted = K.nc.dram_tensor("t2_h_sorted", [(NST_TILES + 1) * ST, D], F32).ap()
        y_sorted = K.nc.dram_tensor("t2_y_sorted", [NST_TILES * ST, D], F32).ap()
        _route_top2(K, h_rows, weight, chosen, h_sorted)
        K.clear()
        _assign_slots(K, chosen, slot, expert_of)
        K.clear()
        _scatter_rows(K, h_rows, slot, h_sorted)
        K.clear()
        _expert_tiles(K, expert_of, h_sorted, y_sorted)
        K.clear()
        _combine(K, weight, slot, y_sorted)


def _route_top2(K, h_rows, weight, chosen, h_sorted):
    nc, io = K.nc, K.io
    NE = chosen[0].shape[2]
    ZT = 4
    with ExitStack() as c:
        ln = LayerNormFront(K, c, "r2")
        sb = lambda n, s, d=F32: K.sb(c, f"r2_{n}", s, d)
        sem = lambda n: K.sem(c, f"r2_{n}")
        router = sb("router", [P, KD, NE])
        router_b = sb("router_b", [P, NE])
        zeros = sb("zeros", [P, ZT, D])
        logit = sb("logit", [P, TC, NE])
        best = sb("best", [P, TC, 8])
        index = sb("index", [P, TC, 8], U32)
        index_f = sb("index_f", [P, TC, TOP])
        behind = sb("behind", [P, TC])
        e2 = sb("e2", [P, TC])
        total = sb("total", [P, TC])
        w0 = sb("w0", [P, TC])
        pS = K.ps(c, "r2_pS", [P, TC, NE])
        s_in, s_lg, s_v, s_e, s_copy, s_w, s_z, s_zero = (sem(n) for n in ("in", "lg", "v", "e", "copy", "w", "z", "zero"))
        N = 9
        block = c.enter_context(nc.Block())

        @block.sync
        def _(eng):
            eng.dma_start(router[:, :, :], io["t2_router"].rearrange("(k p) e -> p k e", p=P)).then_inc(s_in, 16)
            eng.dma_start(router_b[:, :], io["t2_router_b"].partition_broadcast(P)).then_inc(s_in, 16)
            eng.wait_ge(s_z, 1)
            n_zero = -(-NST_TILES * ST // (P * ZT))
            with eng.Fori(0, n_zero) as z:
                eng.dma_start(h_sorted[bass.ds(z * (P * ZT), P * ZT), :].rearrange("(p a) d -> p a d", a=ZT), zeros[:, :, :]
                              ).then_inc(s_zero, 16)
            eng.wait_ge(s_zero, 16 * n_zero)

        @block.gpsimd
        def _(eng):
            def mid(i, p):
                after(eng, ln.s_xn, i, TC)
                eng.sem_inc(K.held_pool)
                nc.gpsimd.tensor_copy(h_rows[:, bass.ds(i * TC, TC), :], ln.xn[p][:, :, :]).then_inc(s_copy, 1)
            chunks(eng, NCH, nothing, lambda i, p: ln.gpsimd(eng, i, p), mid)

        @block.vector
        def _(eng):
            nc.vector.memset(zeros[:, :, :], 0.0).then_inc(s_z, 1)

            def front(i, p):
                free(eng, s_copy, i, 1)
                ln.vector(eng, i, p)

            def mid(i, p):
                after(eng, s_lg, i, 1)
                ch = Chain(eng, s_v, i, N)
                ch.do(nc.vector.tensor_tensor(logit[:, :, :], pS[:, :, :],
                                              router_b[:, :].unsqueeze(1).to_broadcast([P, TC, NE]), ALU.add))
                eng.sem_inc(K.held_vector)
                for t in range(TC):
                    last = nc.vector.max(best[:, t, :], logit[:, t, :])
                ch.do(last)
                eng.sem_inc(K.held_vector)
                for t in range(TC):
                    last = nc.vector.max_index(index[:, t, :], best[:, t, :], logit[:, t, :])
                ch.do(last)
                ch.do(nc.vector.tensor_copy(index_f[:, :, :], index[:, :, 0:TOP]))
                ch.do(nc.vector.tensor_tensor(behind[:, :], best[:, :, 1], best[:, :, 0], ALU.subtract))
                after(eng, s_e, i, 1)
                ch.do(nc.vector.tensor_scalar(total[:, :], e2[:, :], 1.0, None, ALU.add))
                ch.do(nc.vector.reciprocal(w0[:, :], total[:, :]))
                nc.vector.tensor_copy(weight[:, bass.ds(i * TC, TC), 0], w0[:, :])
                ch.do(nc.vector.tensor_tensor(weight[:, bass.ds(i * TC, TC), 1], e2[:, :], w0[:, :], ALU.mult))
                for k in range(TOP):
                    last = nc.vector.tensor_tensor(chosen[k][:, bass.ds(i * TC, TC), :],
                                                   K.iota8[:, :].unsqueeze(1).to_broadcast([P, TC, NE]),
                                                   index_f[:, :, k].unsqueeze(2).to_broadcast([P, TC, NE]), ALU.is_equal)
                ch.do(last)
                ch.done()
            chunks(eng, NCH, mid, front, nothing)

        @block.scalar
        def _(eng):
            def mid(i, p):
                after(eng, s_v, i, N, 5)
                nc.scalar.activation(e2[:, :], behind[:, :], ACT.Exp).then_inc(s_e, 1)
            chunks(eng, NCH, mid, lambda i, p: ln.scalar(eng, i, p, s_lg, 1), nothing)

        @block.tensor
        def _(eng):
            def mid(i, p):
                after(eng, ln.s_xnT, i, KD)
                if n_positive(i):
                    after(eng, s_v, i - 1, N, 1)
                for t in range(TC):
                    for k in range(KD):
                        last = nc.tensor.matmul(pS[:, t, :], ln.xnT[p][:, k, t * P:(t + 1) * P], router[:, k, :],
                                                start=(k == 0), stop=(k == KD - 1))
                last.then_inc(s_lg, 1)
            eng.wait_ge(s_in, 32)
            chunks(eng, NCH, mid, lambda i, p: ln.tensor(eng, i, p), nothing)


def _assign_slots(K, chosen, slot, expert_of):
    nc = K.nc
    NE = chosen[0].shape[2]
    LOG = ST.bit_length() - 1
    with ExitStack() as c:
        sb = lambda n, s, d=F32: K.sb(c, f"as_{n}", s, d)
        sem = lambda n: K.sem(c, f"as_{n}")
        ones = sb("ones", [P, P])
        earlier = sb("earlier", [P, P])
        pairs = sb("pairs", [P, NT, NE])
        upto = sb("upto", [P, NE, NT])
        place = sb("place", [P, NT, NE])
        picked = sb("picked", [P, NT, NE])
        slot_f = sb("slot_f", [P, NT])
        padded = sb("padded", [P, NE])
        padded_i = sb("padded_i", [P, NE], I32)
        tiles_i = sb("tiles_i", [P, NE], I32)
        tiles = sb("tiles", [P, NE])
        end = sb("end", [P, NE])
        first = sb("first", [P, NE])
        number = sb("number", [P, NST_TILES])
        passed = sb("passed", [P, NST_TILES, NE])
        expert_f = sb("expert_f", [P, NST_TILES])
        pRows = K.ps(c, "as_pRows", [P, NT, NE])
        pTile = K.ps(c, "as_pTile", [P, NT, NE])
        s_v, s_g, s_p = sem("v"), sem("g"), sem("p")
        block = c.enter_context(nc.Block())

        @block.gpsimd
        def _(eng):
            eng.wait_ge(s_v, 1)
            nc.gpsimd.affine_select(out=earlier[:, :], in_=earlier[:, :], compare_op=ALU.is_ge, fill=0.0, base=-1,
                                    pattern=[[1, P]], channel_multiplier=-1).then_inc(s_g, 1)
            nc.gpsimd.iota(number[:, :], pattern=[[1, NST_TILES]], base=0, channel_multiplier=0,
                           allow_small_or_imprecise_dtypes=True).then_inc(s_g, 1)

        @block.tensor
        def _(eng):
            eng.wait_ge(s_v, 3)
            eng.wait_ge(s_g, 2)
            flat = pairs[:, :, :].rearrange("p t e -> p (t e)")
            nc.tensor.matmul(pRows[:, :, :], earlier[:, :], flat, start=True, stop=True).then_inc(s_p, 1)
            nc.tensor.matmul(pTile[:, :, :], ones[:, :], flat, start=True, stop=True).then_inc(s_p, 1)

        @block.vector
        def _(eng):
            ch = Chain(eng, s_v, 0, None)
            ch.do(nc.vector.memset(earlier[:, :], 1.0))
            ch.do(nc.vector.memset(ones[:, :], 1.0))
            ch.do(nc.vector.tensor_tensor(pairs[:, :, :], chosen[0][:, :, :], chosen[1][:, :, :], ALU.add))
            eng.wait_ge(s_p, 2)
            for e in range(NE):
                last = nc.vector.tensor_tensor_scan(upto[:, e, :], ones[:, 0:NT], pTile[:, :, e], 0.0, ALU.mult, ALU.add)
            ch.do(last)
            ch.do(nc.vector.tensor_scalar(padded[:, :], upto[:, :, NT - 1], float(ST - 1), None, ALU.add))
            ch.do(nc.vector.tensor_copy(padded_i[:, :], padded[:, :]))
            ch.do(nc.vector.tensor_scalar(tiles_i[:, :], padded_i[:, :], LOG, None, ALU.arith_shift_right))
            ch.do(nc.vector.tensor_copy(tiles[:, :], tiles_i[:, :]))
            ch.do(nc.vector.tensor_tensor_scan(end[:, :], ones[:, 0:NE], tiles[:, :], 0.0, ALU.mult, ALU.add))
            ch.do(nc.vector.tensor_tensor(first[:, :], end[:, :], tiles[:, :], ALU.subtract))
            ch.do(nc.vector.tensor_scalar(first[:, :], first[:, :], float(ST), None, ALU.mult))
            ch.do(nc.vector.tensor_tensor(place[:, :, :], upto[:, :, :].rearrange("p e t -> p t e"), pTile[:, :, :], ALU.subtract))
            ch.do(nc.vector.tensor_tensor(place[:, :, :], place[:, :, :], pRows[:, :, :], ALU.add))
            ch.do(nc.vector.tensor_tensor(place[:, :, :], place[:, :, :],
                                          first[:, :].unsqueeze(1).to_broadcast([P, NT, NE]), ALU.add))
            for k in range(TOP):
                ch.do(nc.vector.tensor_tensor(picked[:, :, :], place[:, :, :], chosen[k][:, :, :], ALU.mult))
                ch.do(nc.vector.tensor_reduce(slot_f[:, :], picked[:, :, :], axis=AX.X, op=ALU.add))
                ch.do(nc.vector.tensor_copy(slot[k][:, :], slot_f[:, :]))
            ch.do(nc.vector.tensor_tensor(passed[:, :, :], number[:, :].unsqueeze(2).to_broadcast([P, NST_TILES, NE]),
                                          end[:, :].unsqueeze(1).to_broadcast([P, NST_TILES, NE]), ALU.is_ge))
            ch.do(nc.vector.tensor_reduce(expert_f[:, :], passed[:, :, :], axis=AX.X, op=ALU.add))
            ch.do(nc.vector.tensor_scalar(expert_f[:, :], expert_f[:, :], float(NE - 1), None, ALU.min))
            ch.do(nc.vector.tensor_copy(expert_of[:, :], expert_f[:, :]))


def _scatter_rows(K, h_rows, slot, h_sorted):
    nc = K.nc
    BUFS = 4
    with ExitStack() as c:
        sb = lambda n, s, d=F32: K.sb(c, f"sc_{n}", s, d)
        sem = lambda n: K.sem(c, f"sc_{n}")
        row = [sb(f"row{q}", [P, D]) for q in range(BUFS)]
        to = [[sb(f"to{q}_{k}", [P, 1], U32) for k in range(TOP)] for q in range(BUFS)]
        s_fill = sem("fill")
        s_out = [sem(f"out{q}") for q in range(BUFS)]
        block = c.enter_context(nc.Block())

        @block.vector
        def _(eng):
            def fill(r, q):
                t = r * BUFS + q
                if n_positive(r):
                    eng.wait_ge(s_out[q], r * (16 * TOP))
                nc.vector.tensor_copy(row[q][:, :], h_rows[:, bass.ds(t, 1), :].rearrange("p a d -> p (a d)"))
                for k in range(TOP):
                    last = nc.vector.tensor_copy(to[q][k][:, :], slot[k][:, bass.ds(t, 1)])
                last.then_inc(s_fill, 1)
            for q in range(BUFS):
                fill(0, q)
            with eng.Fori(1, NT // BUFS) as r:
                for q in range(BUFS):
                    fill(r, q)

        @block.gpsimd
        def _(eng):
            with eng.Fori(0, NT // BUFS) as r:
                for q in range(BUFS):
                    eng.wait_ge(s_fill, r * BUFS + q + 1)
                    eng.sem_inc(K.held_pool)
                    for k in range(TOP):
                        nc.gpsimd.indirect_dma_start(h_sorted, bass.IndirectOffsetOnAxis(ap=to[q][k][:, :], axis=0),
                                                     row[q][:, :], None).then_inc(s_out[q], 16)
            for q in range(BUFS):
                eng.wait_ge(s_out[q], NT // BUFS * 16 * TOP)


def _expert_tiles(K, expert_of, h_sorted, y_sorted):
    nc, io = K.nc, K.io
    NE, _, HID = io["t2_wgT"].shape
    HT = HID // P
    SP_ = ST // P
    PAIR = 2
    NP = HT // PAIR
    with ExitStack() as c:
        sb = lambda n, s, d=F32: K.sb(c, f"et_{n}", s, d)
        sem = lambda n: K.sem(c, f"et_{n}")
        wg = [sb(f"wg{q}", [P, KD, HID]) for q in range(2)]
        wu = [sb(f"wu{q}", [P, KD, HID]) for q in range(2)]
        wd = [sb(f"wd{q}", [P, HT, D]) for q in range(2)]
        h = [sb(f"h{q}", [P, SP_, D]) for q in range(2)]
        hT = [sb(f"hT{q}", [P, KD, ST]) for q in range(2)]
        silu = [sb(f"silu{q}", [P, PAIR, ST]) for q in range(2)]
        mT = [sb(f"mT{q}", [P, PAIR, ST]) for q in range(NP)]
        y = [sb(f"y{q}", [P, SP_, D]) for q in range(2)]
        pT = K.ps(c, "et_pT", [P, KD, ST])
        pG = [K.ps(c, f"et_pG{q}", [P, PAIR, ST]) for q in range(2)]
        pU = [K.ps(c, f"et_pU{q}", [P, PAIR, ST]) for q in range(2)]
        pO = [K.ps(c, f"et_pO{q}", [P, SP_, D]) for q in range(2)]
        s_w = [sem(f"w{q}") for q in range(2)]
        s_h = [sem(f"h{q}s") for q in range(2)]
        s_out = [sem(f"out{q}") for q in range(2)]
        s_tp, s_hT, s_gu, s_silu, s_m, s_o, s_y = (sem(n) for n in ("tp", "hTs", "gu", "silus", "m", "o", "ys"))
        block = c.enter_context(nc.Block())

        def pairs_of_steps(eng, fn):
            assert NST_TILES % 2 == 1
            fn(0, 0)
            fn(1, 1)
            with eng.Fori(1, NST_TILES // 2) as j:
                fn(2 * j, 0)
                fn(2 * j + 1, 1)
            fn(NST_TILES - 1, 0)

        @block.sync
        def _(eng):
            def load(i, q):
                if not isinstance(i, int) or i >= 2:
                    eng.wait_ge(s_o, i - 1)
                e = eng.value_load(expert_of[0:1, bass.ds(i, 1)], min_val=0, max_val=NE - 1)
                eng.dma_start(h[q][:, :, :], h_sorted[bass.ds(i * ST, ST), :].rearrange("(a p) d -> p a d", p=P)).then_inc(s_h[q], 16)
                for dst, name in ((wg[q], "t2_wgT"), (wu[q], "t2_wuT"), (wd[q], "t2_wdT")):
                    src = io[name][bass.ds(e, 1), :, :].rearrange("a (k p) n -> p (a k) n", p=P)
                    eng.dma_start(dst[:, :, :], src).then_inc(s_w[q], 16)
            pairs_of_steps(eng, load)

        @block.gpsimd
        def _(eng):
            def save(i, q):
                after(eng, s_y, i, 1)
                eng.sem_inc(K.held_pool)
                eng.dma_start(y_sorted[bass.ds(i * ST, ST), :].rearrange("(a p) d -> p a d", p=P), y[q][:, :, :]).then_inc(s_out[q], 16)
            pairs_of_steps(eng, save)
            for q in range(2):
                eng.wait_ge(s_out[q], 16 * ((NST_TILES + 1 - q) // 2))

        @block.scalar
        def _(eng):
            def step(i, q):
                after(eng, s_tp, i, 1)
                nc.scalar.copy(hT[q][:, :, :], pT[:, :, :]).then_inc(s_hT, 1)
                for j in range(NP):
                    after(eng, s_gu, i, NP, j + 1)
                    if j >= 2 or n_positive(i):
                        eng.wait_ge(s_m, i * NP + j - 1)
                    nc.scalar.activation(silu[j % 2][:, :, :], pG[j % 2][:, :, :], ACT.Silu).then_inc(s_silu, 1)
            pairs_of_steps(eng, step)

        @block.vector
        def _(eng):
            def step(i, q):
                for j in range(NP):
                    after(eng, s_silu, i, NP, j + 1)
                    if n_positive(i) and j == 0:
                        eng.wait_ge(s_o, i)
                    nc.vector.tensor_tensor(mT[j][:, :, :], silu[j % 2][:, :, :], pU[j % 2][:, :, :], ALU.mult).then_inc(s_m, 1)
                after(eng, s_o, i, 1)
                if not isinstance(i, int) or i >= 2:
                    eng.wait_ge(s_out[q], (i // 2) * 16)
                nc.vector.tensor_copy(y[q][:, :, :], pO[q][:, :, :]).then_inc(s_y, 1)
            pairs_of_steps(eng, step)

        @block.tensor
        def _(eng):
            def transpose(i, q):
                eng.wait_ge(s_h[q], (i // 2) * 16 + 16)
                if n_positive(i):
                    eng.wait_ge(s_hT, i)
                    eng.sem_inc(K.held_tensor)
                for k in range(KD):
                    for a in range(SP_):
                        last = nc.tensor.transpose(pT[:, k, a * P:(a + 1) * P], h[q][:, a, k * P:(k + 1) * P], K.ident[:, :])
                last.then_inc(s_tp, 1)

            def gate_up(i, q, j):
                if j >= 2 or n_positive(i):
                    eng.wait_ge(s_m, i * NP + j - 1)
                for w, out in ((wg[q], pG[j % 2]), (wu[q], pU[j % 2])):
                    for x in range(PAIR):
                        col = (j * PAIR + x) * P
                        for k in range(KD):
                            last = nc.tensor.matmul(out[:, x, :], w[:, k, col:col + P], hT[q][:, k, :],
                                                    start=(k == 0), stop=(k == KD - 1))
                last.then_inc(s_gu, 1)

            def down(i, q, j):
                after(eng, s_m, i, NP, j + 1)
                if j == 0 and (not isinstance(i, int) or i >= 2):
                    eng.wait_ge(s_y, i - 1)
                for x in range(PAIR):
                    for a in range(SP_):
                        last = nc.tensor.matmul(pO[q][:, a, :], mT[j][:, x, a * P:(a + 1) * P], wd[q][:, j * PAIR + x, :],
                                                start=(j == 0 and x == 0 and a == 0), stop=(j == NP - 1 and x == PAIR - 1),
                                                skip_group_check=True)
                if j == NP - 1:
                    last.then_inc(s_o, 1)

            def step(i, q, ahead):
                after(eng, s_hT, i, 1)
                eng.wait_ge(s_w[q], (i // 2) * 48 + 48)
                gate_up(i, q, 0)
                gate_up(i, q, 1)
                for j in range(2, NP):
                    down(i, q, j - 2)
                    gate_up(i, q, j)
                if ahead:
                    transpose(i + 1, 1 - q)
                down(i, q, NP - 2)
                down(i, q, NP - 1)
            transpose(0, 0)
            step(0, 0, True)
            with eng.Fori(1, NST_TILES // 2) as j:
                step(2 * j - 1, 1, True)
                step(2 * j, 0, True)
            step(NST_TILES - 2, 1, True)
            step(NST_TILES - 1, 0, False)


def _combine(K, weight, slot, y_sorted):
    nc, R = K.nc, K.resid
    BUFS = 4
    with ExitStack() as c:
        sb = lambda n, s, d=F32: K.sb(c, f"cb_{n}", s, d)
        sem = lambda n: K.sem(c, f"cb_{n}")
        y = [[sb(f"y{q}_{k}", [P, D]) for k in range(TOP)] for q in range(BUFS)]
        at = [[sb(f"at{q}_{k}", [P, 1], U32) for k in range(TOP)] for q in range(BUFS)]
        s_at, s_add = sem("at"), sem("add")
        s_y = [sem(f"y{q}") for q in range(BUFS)]
        block = c.enter_context(nc.Block())

        def rounds(eng, fn):
            for q in range(BUFS):
                fn(0, q)
            with eng.Fori(1, NT // BUFS) as r:
                for q in range(BUFS):
                    fn(r, q)

        @block.scalar
        def _(eng):
            def slots(r, q):
                if n_positive(r):
                    eng.wait_ge(s_y[q], r * (16 * TOP))
                for k in range(TOP):
                    last = nc.scalar.copy(at[q][k][:, :], slot[k][:, bass.ds(r * BUFS + q, 1)])
                last.then_inc(s_at, 1)
            rounds(eng, slots)

        @block.gpsimd
        def _(eng):
            def gather(r, q):
                eng.wait_ge(s_at, r * BUFS + q + 1)
                if n_positive(r):
                    eng.wait_ge(s_add, (r * BUFS + q - BUFS + 1) * TOP)
                    eng.sem_inc(K.held_pool)
                for k in range(TOP):
                    nc.gpsimd.indirect_dma_start(y[q][k][:, :], None, y_sorted,
                                                 bass.IndirectOffsetOnAxis(ap=at[q][k][:, :], axis=0)).then_inc(s_y[q], 16)
            rounds(eng, gather)

        @block.vector
        def _(eng):
            def add(r, q):
                t = r * BUFS + q
                row = R[:, bass.ds(t, 1), :].rearrange("p a d -> p (a d)")
                eng.wait_ge(s_y[q], r * (16 * TOP) + 16 * TOP)
                for k in range(TOP):
                    w = weight[:, bass.ds(t, 1), k]
                    nc.vector.scalar_tensor_tensor(row, y[q][k][:, :], w, row, ALU.mult, ALU.add).then_inc(s_add, 1)
                    after(eng, s_add, t, TOP, k + 1)
            rounds(eng, add)


STAGES = [load_and_constants, mamba, context_glu, top1_experts, self_attention, cross_attention, top2_experts, store]


def decoder(nc, io, stages=None):
    with ExitStack() as ctx:
        K = Kernel(nc, ctx, io)
        for stage in stages or STAGES:
            stage(K)
            K.clear()


def layout(inputs):
    t = lambda n, *axes: np.ascontiguousarray(np.transpose(np.asarray(inputs[n]), axes))
    same = lambda n: np.ascontiguousarray(np.asarray(inputs[n]))
    return {
        "x": same("x"), "ctx": same("ctx_1024"), "ctxT": t("ctx_1024", 0, 2, 1),
        "t1_router": same("L0_ffn_router_w"), "t1_router_b": same("L0_ffn_router_b"),
        "t2_router": t("L1_ffn_wg", 1, 0), "t2_router_b": same("L1_ffn_bg"),
        "t2_wgT": t("L1_ffn_Wgate", 0, 2, 1), "t2_wuT": t("L1_ffn_Wup", 0, 2, 1), "t2_wdT": t("L1_ffn_Wdown", 0, 2, 1),
        "xa_wqT": t("L1_xattn_Wq", 1, 0), "xa_wkT": t("L1_xattn_Wk", 1, 0), "xa_wvT": t("L1_xattn_Wv", 1, 0),
        "xa_woT": t("L1_xattn_Wo", 1, 0), "xa_bq": same("L1_xattn_bq"), "xa_bk": same("L1_xattn_bk"),
        "xa_bv": same("L1_xattn_bv"), "xa_bo": same("L1_xattn_bo"),
        "sa_wqT": t("L1_attn_wq", 1, 0), "sa_wkT": t("L1_attn_wk", 1, 0), "sa_wvT": t("L1_attn_wv", 1, 0),
        "sa_woT": t("L1_attn_wo", 1, 0),
        "mb_w_in": same("L0_attn_W_in"), "mb_conv_w": same("L0_attn_conv_w"), "mb_conv_b": same("L0_attn_conv_b"),
        "mb_w_x": same("L0_attn_W_xproj"), "mb_wdt": same("L0_attn_W_dt"), "mb_b_dt": same("L0_attn_b_dt"),
        "mb_A_log": same("L0_attn_A_log"), "mb_D": same("L0_attn_D"), "mb_w_out": same("L0_attn_W_out"),
        "t1_w": same("L0_ffn_expert_w"), "t1_b": same("L0_ffn_expert_b"),
    }


def kernel(**inputs):
    import concourse.bacc as bacc
    from concourse.bass_utils import run_bass_kernel_spmd

    nc = bacc.Bacc("TRN2", target_bir_lowering=False, num_devices=1)
    arrays, io = {}, {}
    for name, a in layout(inputs).items():
        arrays[f"in_{name}"] = a
        io[name] = nc.dram_tensor(f"in_{name}", a.shape, mybir.dt.from_np(a.dtype), kind="ExternalInput").ap()
    io["out"] = nc.dram_tensor("out", (NB, SEQ, D), F32, kind="ExternalOutput").ap()
    decoder(nc, io)
    r = run_bass_kernel_spmd(nc, [arrays], core_ids=[0])
    return r.results[0]["out"]
```
